# Optimizing a Trainium2 kernel written in Bass

```python
import numpy as np
import jax
import jax.numpy as jnp

def _softmax(x, axis=-1):
    return jax.nn.softmax(x, axis=axis)

def _gelu(x):
    return jax.nn.gelu(x, approximate=True)

def _silu(x):
    return jax.nn.silu(x)

def _sigmoid(x):
    return jax.nn.sigmoid(x)

def _layernorm(x, axis=-1, eps=1e-05):
    m = jnp.mean(x, axis=axis, keepdims=True)
    v = jnp.var(x, axis=axis, keepdims=True)
    return (x - m) / jnp.sqrt(v + eps)

def _scatter_add(tgt, idx, src, axis=0):
    return tgt.at[idx].add(src)

def _segment_sum(src, seg, n):
    return jax.ops.segment_sum(src, seg, n)
kernel_name = 'mk_adaln_d1_jaxref_r8_829cce'

def setup_inputs(seed: int=0):
    np.random.seed(seed)
    _w = jnp.asarray

    def _L0_attn_setup():
        import jax, jax.numpy as jnp
        import numpy as np
        B, T, D = (2, 256, 256)
        HQ, HKV = (32, 8)
        HD = D // HQ
        G = HQ // HKV
        ROPE_BASE = 10000.0

        def _rope(q, k):
            t, d = (q.shape[2], q.shape[3])
            inv_freq = 1.0 / ROPE_BASE ** (jnp.arange(0, d, 2, dtype=jnp.float32) / d)
            ang = jnp.arange(t, dtype=jnp.float32)[:, None] * inv_freq[None, :]
            cos = jnp.concatenate([jnp.cos(ang), jnp.cos(ang)], axis=-1)[None, None]
            sin = jnp.concatenate([jnp.sin(ang), jnp.sin(ang)], axis=-1)[None, None]

            def rot_half(x):
                x1, x2 = jnp.split(x, 2, axis=-1)
                return jnp.concatenate([-x2, x1], axis=-1)
            return (q * cos + rot_half(q) * sin, k * cos + rot_half(k) * sin)
        key = jax.random.key(seed)
        ks = jax.random.split(key, 5)
        s = 0.02
        x = jax.random.normal(ks[0], (B, T, D), dtype=jnp.float32)
        Wq = jax.random.normal(ks[1], (D, D), dtype=jnp.float32) * s
        Wk = jax.random.normal(ks[2], (HKV * HD, D), dtype=jnp.float32) * s
        Wv = jax.random.normal(ks[3], (HKV * HD, D), dtype=jnp.float32) * s
        Wo = jax.random.normal(ks[4], (D, D), dtype=jnp.float32) * s
        return {'x': x, 'Wq': Wq, 'bq': jnp.zeros((D,), jnp.float32), 'Wk': Wk, 'bk': jnp.zeros((HKV * HD,), jnp.float32), 'Wv': Wv, 'bv': jnp.zeros((HKV * HD,), jnp.float32), 'Wo': Wo, 'bo': jnp.zeros((D,), jnp.float32)}
    _L0_attn_in = _L0_attn_setup()

    def _L0_ffn_setup():
        import jax, jax.numpy as jnp
        import numpy as np
        CAPACITY_FACTOR = 1.0

        def _top1_gate(x, w_gate):
            S, E = (x.shape[0], w_gate.shape[1])
            capacity = int(CAPACITY_FACTOR * S / E)
            logits = x @ w_gate
            gates = jax.nn.softmax(logits, axis=-1)
            idx1 = jnp.argmax(gates, axis=-1)
            mask1 = jax.nn.one_hot(idx1, E, dtype=gates.dtype)
            locations1 = jnp.cumsum(mask1, axis=0) - mask1
            mask1 = mask1 * (locations1 < capacity)
            locations1_s = jnp.sum(locations1 * mask1, axis=1).astype(jnp.int32)
            gates_masked = gates * mask1
            loc_oh = jax.nn.one_hot(locations1_s, capacity, dtype=gates.dtype) * jnp.sum(mask1, axis=1, keepdims=True)
            combine_weights = jnp.einsum('se,sc->sec', gates_masked, loc_oh)
            dispatch_mask = (combine_weights > 0).astype(gates.dtype)
            return (combine_weights, dispatch_mask)
        key = jax.random.key(seed)
        k1, k2, k3, k4 = jax.random.split(key, 4)
        B, T, D, E, F = (4, 256, 256, 8, 1024)
        hidden_states = jax.random.normal(k1, (B, T, D), dtype=jnp.float32)
        w_gate = jax.random.normal(k2, (D, E), dtype=jnp.float32) * 0.02
        w1 = jax.random.normal(k3, (E, D, F), dtype=jnp.float32) * 0.02
        w2 = jax.random.normal(k4, (E, F, D), dtype=jnp.float32) * 0.02
        return {'hidden_states': hidden_states, 'w_gate': w_gate, 'w1': w1, 'w2': w2}
    _L0_ffn_in = _L0_ffn_setup()
    _L0_c = _w((lambda *s: np.random.randn(*s).astype(np.float32) * 0.05)(2, 256))
    _L0_wmod = _w((lambda *s: np.random.randn(*s).astype(np.float32) * 0.05)(256, 6 * 256) * 256 ** (-0.5))
    _d = {'L0_attn_x': _L0_attn_in['x'], 'L0_attn_Wq': _L0_attn_in['Wq'], 'L0_attn_bq': _L0_attn_in['bq'], 'L0_attn_Wk': _L0_attn_in['Wk'], 'L0_attn_bk': _L0_attn_in['bk'], 'L0_attn_Wv': _L0_attn_in['Wv'], 'L0_attn_bv': _L0_attn_in['bv'], 'L0_attn_Wo': _L0_attn_in['Wo'], 'L0_attn_bo': _L0_attn_in['bo'], 'L0_ffn_w_gate': _L0_ffn_in['w_gate'], 'L0_ffn_w1': _L0_ffn_in['w1'], 'L0_ffn_w2': _L0_ffn_in['w2'], 'L0_c': _L0_c, 'L0_wmod': _L0_wmod}
    _x0 = _d['L0_attn_x']
    _d['L0_attn_x'] = jax.random.normal(jax.random.fold_in(jax.random.key(seed), 1), (2, 512, 256), dtype=_x0.dtype)
    del _x0
    return _d

def reference(L0_attn_x, L0_attn_Wq, L0_attn_bq, L0_attn_Wk, L0_attn_bk, L0_attn_Wv, L0_attn_bv, L0_attn_Wo, L0_attn_bo, L0_ffn_w_gate, L0_ffn_w1, L0_ffn_w2, L0_c, L0_wmod):

    def _L0_attn_ref(x, Wq, bq, Wk, bk, Wv, bv, Wo, bo):
        import jax, jax.numpy as jnp
        import numpy as np
        B, T, D = (2, 256, 256)
        HQ, HKV = (32, 8)
        HD = D // HQ
        G = HQ // HKV
        ROPE_BASE = 10000.0

        def _rope(q, k):
            t, d = (q.shape[2], q.shape[3])
            inv_freq = 1.0 / ROPE_BASE ** (jnp.arange(0, d, 2, dtype=jnp.float32) / d)
            ang = jnp.arange(t, dtype=jnp.float32)[:, None] * inv_freq[None, :]
            cos = jnp.concatenate([jnp.cos(ang), jnp.cos(ang)], axis=-1)[None, None]
            sin = jnp.concatenate([jnp.sin(ang), jnp.sin(ang)], axis=-1)[None, None]

            def rot_half(x):
                x1, x2 = jnp.split(x, 2, axis=-1)
                return jnp.concatenate([-x2, x1], axis=-1)
            return (q * cos + rot_half(q) * sin, k * cos + rot_half(k) * sin)
        b, t, _ = x.shape
        Q = (x @ Wq.T + bq).reshape(b, t, HQ, HD).transpose(0, 2, 1, 3)
        K = (x @ Wk.T + bk).reshape(b, t, HKV, HD).transpose(0, 2, 1, 3)
        V = (x @ Wv.T + bv).reshape(b, t, HKV, HD).transpose(0, 2, 1, 3)
        Q, K = _rope(Q, K)
        K = jnp.repeat(K, G, axis=1)
        V = jnp.repeat(V, G, axis=1)
        scores = jnp.einsum('bhqd,bhkd->bhqk', Q, K) / np.sqrt(HD).astype(np.float32)
        w = jax.nn.softmax(scores, axis=-1)
        attn = jnp.einsum('bhqk,bhkd->bhqd', w, V)
        out = attn.transpose(0, 2, 1, 3).reshape(b, t, D)
        return out @ Wo.T + bo

    def _L0_ffn_ref(hidden_states, w_gate, w1, w2):
        import jax, jax.numpy as jnp
        import numpy as np
        CAPACITY_FACTOR = 1.0

        def _top1_gate(x, w_gate):
            S, E = (x.shape[0], w_gate.shape[1])
            capacity = int(CAPACITY_FACTOR * S / E)
            logits = x @ w_gate
            gates = jax.nn.softmax(logits, axis=-1)
            idx1 = jnp.argmax(gates, axis=-1)
            mask1 = jax.nn.one_hot(idx1, E, dtype=gates.dtype)
            locations1 = jnp.cumsum(mask1, axis=0) - mask1
            mask1 = mask1 * (locations1 < capacity)
            locations1_s = jnp.sum(locations1 * mask1, axis=1).astype(jnp.int32)
            gates_masked = gates * mask1
            loc_oh = jax.nn.one_hot(locations1_s, capacity, dtype=gates.dtype) * jnp.sum(mask1, axis=1, keepdims=True)
            combine_weights = jnp.einsum('se,sc->sec', gates_masked, loc_oh)
            dispatch_mask = (combine_weights > 0).astype(gates.dtype)
            return (combine_weights, dispatch_mask)
        B, T, D = hidden_states.shape
        x = hidden_states.reshape(-1, D)
        combine_weights, dispatch_mask = _top1_gate(x, w_gate)
        dispatched = jnp.einsum('sec,sm->ecm', dispatch_mask, x)
        h = jax.nn.gelu(jnp.einsum('ecd,edf->ecf', dispatched, w1))
        expert_out = jnp.einsum('ecf,efd->ecd', h, w2)
        combined = jnp.einsum('sec,ecm->sm', combine_weights, expert_out)
        return combined.reshape(B, T, D)
    x = L0_attn_x
    mod = (_silu(L0_c) @ L0_wmod).reshape(L0_c.shape[0], 6, 1, -1)
    sa, ca, ga, sb, cb, gb = (mod[:, 0], mod[:, 1], mod[:, 2], mod[:, 3], mod[:, 4], mod[:, 5])
    ga = (2 * (ga >= 0) - 1) * jnp.maximum(jnp.abs(ga), 0.25)
    gb = (2 * (gb >= 0) - 1) * jnp.maximum(jnp.abs(gb), 0.25)
    h = _layernorm(x, axis=-1) * (1 + ca) + sa
    x = x + ga * _L0_attn_ref(h, L0_attn_Wq, L0_attn_bq, L0_attn_Wk, L0_attn_bk, L0_attn_Wv, L0_attn_bv, L0_attn_Wo, L0_attn_bo)
    h = _layernorm(x, axis=-1) * (1 + cb) + sb
    x = x + gb * _L0_ffn_ref(h, L0_ffn_w_gate, L0_ffn_w1, L0_ffn_w2)
    return x

_drawn_inputs = setup_inputs


def setup_inputs(seed=0):
    import zlib

    import numpy as np

    out = dict(_drawn_inputs(seed))
    spreads = {'L0_attn_bq': (0.0, 0.8),
     'L0_attn_bk': (0.0, 0.8),
     'L0_attn_bv': (0.0, 0.8),
     'L0_attn_bo': (0.0, 0.33)}
    factors = {'L0_attn_Wq': 8.0,
     'L0_attn_Wk': 8.0,
     'L0_attn_Wv': 8.0,
     'L0_attn_Wo': 6.783,
     'L0_ffn_w_gate': 8.0,
     'L0_ffn_w1': 8.0,
     'L0_ffn_w2': 8.0}
    for name, (base, spread) in spreads.items():
        noise = np.random.default_rng([zlib.crc32(name.encode()), seed]).standard_normal(out[name].shape)
        drawn = base * np.exp(spread * noise) if base else spread * noise
        out[name] = jnp.asarray(drawn.astype(out[name].dtype))
    for name, factor in factors.items():
        out[name] = (out[name] * factor).astype(out[name].dtype)
    return out
```

```python
from contextlib import ExitStack

import concourse.bass as bass
from concourse import mybir

F32 = mybir.dt.float32
BF16 = mybir.dt.bfloat16
I32 = mybir.dt.int32
ALU = mybir.AluOpType
ACT = mybir.ActivationFunctionType
AX_X = mybir.AxisListType.X

P = 128


def adaln_attention_moe_kernel(nc, x, c_t, wmod, wqkv_t, bq, bk, bv, wo_t, bo, w_gate, w1, w2,
                               rope_cos, rope_sin, rope_rot, out):
    B = c_t.shape[1]
    S, D = x.shape
    T = S // B
    HD = 8
    HQ = D // HD
    HKV = bk.shape[0] // HD
    G = HQ // HKV
    NG = B * HKV
    E, _, F = w1.shape
    CAP = S // E
    DC = D // P
    NT = S // P
    TB = T // P
    FT = F // P
    CH = 6
    EPS = 1e-5
    GATE_MIN = 0.25
    FAR = 4 * S
    PARTS = 3
    COMBOS = PARTS * PARTS
    ROWS = COMBOS * HD
    SHIFT_ROW = 96
    BROWS = SHIFT_ROW + 2
    SLOTS = 4
    SCALE = float(HD) ** -0.5
    assert (P, T, TB, G, DC, CAP, NG % SLOTS) == (128, 512, 4, 4, 2, P, 0)

    qx_dram = nc.dram_tensor("qx_scratch", (B * HQ, HD * COMBOS, T), BF16, kind="Internal").ap()
    kx_dram = nc.dram_tensor("kx_scratch", (NG, HD * COMBOS, T), BF16, kind="Internal").ap()
    routed_dram = nc.dram_tensor("routed_scratch", (E * CAP, D), F32, kind="Internal").ap()
    expert_dram = nc.dram_tensor("expert_scratch", (E * CAP, D), F32, kind="Internal").ap()

    with ExitStack() as ctx:
        def sb(name, shape, dt):
            return ctx.enter_context(nc.sbuf_tensor("sb_" + name, shape, dt))

        def sem(name):
            return ctx.enter_context(nc.semaphore(name))

        bank = [ctx.enter_context(nc.psum_tensor(f"bank{i}", [P, 512], F32)) for i in range(8)]
        max_bank, exp_bank, o_bank, tr_bank = bank[0:4], bank[4:6], bank[6], bank[7]

        PROJ_BANK = [4, 5, 0, 5, 2, 3]
        ROT_BANK = [7, 1, 4, 0, 7, 5]
        ROWS_BANK = [1, 4, 2, 3]

        CHUNK = DC * F
        wbuf = sb("experts", [P, 2 * E * CHUNK], F32)
        pbuf = sb("probs", [P, 2 * G * T], F32)
        qx = sb("qx", [P, SLOTS, G, T], BF16)
        kx = sb("kx", [P, SLOTS, T], BF16)
        xres = sb("x", [P, NT, D], F32)
        vx = sb("vx", [P, NG, TB * (HD + 1)], F32)
        vs = sb("vs", [P, SLOTS, TB, HD + 1], F32)
        attn = sb("attn", [P, B * DC, TB, P], F32)
        rows = sb("mod_rows", [P, 4, B, D], F32)
        osb = sb("o_sbuf", [P, T], F32)
        wo_sb = sb("wo", [P, DC, D], F32)
        wg_sb = sb("w_gate", [P, DC, E], F32)
        bo_sb = sb("bo", [P, D], F32)
        bv_sb = sb("bv", [P, HKV * HD], F32)
        bq_sb = sb("bq", [P, DC], F32)
        bk_sb = sb("bk", [HKV * HD, 1], F32)
        ident = sb("ident", [P, P], F32)
        ident_h = sb("ident_h", [P, P], BF16)
        before = sb("before", [P, P], BF16)
        ones_h = sb("ones_h", [P, P], BF16)
        cT = sb("cT", [P, DC, B], F32)
        c_exp = sb("c_exp", [P, DC, B], F32)
        silu = sb("silu", [P, DC, B], F32)
        mod_scale = sb("mod_scale", [P, DC, B], F32)
        mod_shift = sb("mod_shift", [P, DC, B], F32)
        stats = sb("stats", [P, NT, 6], F32)
        meanvar = sb("meanvar", [P, NT, 2], F32)
        rstd = sb("rstd", [P, NT], F32)
        minus_half = sb("minus_half", [P, NT], F32)
        negmax = sb("negmax", [P, 2, G * TB], F32)
        negparts = sb("negparts", [P, 2, G * TB], BF16)
        shift_rows = sb("shift_rows", [2 * G * TB, 2, P], BF16)
        rden = sb("rden", [P, TB, G], F32)
        expert_no = sb("expert_no", [P, NT, E], F32)
        g_work = sb("g_work", [P, 2, NT, E], F32)
        g_one = sb("g_one", [P, 8, NT], F32)
        onehot = sb("onehot", [P, NT, E], BF16)
        gate_e, is_top = g_work[:, 0], g_work[:, 1]
        one = sb("one", [P, 1], F32)
        ga_bo = sb("ga_bo", [P, B, D], F32)
        zeros_row = sb("zeros_row", [P, D], F32)
        slot_i = sb("slot_i", [P, NT], I32)

        at = [6 * CHUNK]

        def early(words):
            at[0] += words
            assert at[0] <= 2 * E * CHUNK
            return wbuf[:, at[0] - words:at[0]]

        wmod_sb = early(DC * CH * D).rearrange("p (c n) -> p c n", c=DC)
        NQKV = (HQ + 2 * HKV) * HD
        wqkv_sb = early(DC * NQKV).rearrange("p (c n) -> p c n", c=DC)
        at[0] = 8 * CHUNK
        b0_words = [[early(T) for _ in range(3)] for _ in range(3)]
        b0_parts = [early(PARTS * T // 2).bitcast(BF16).rearrange("p (a t) -> p a t", a=PARTS)
                    for _ in range(3)]
        assert at[0] >= 9 * CHUNK
        b1_words = [[early(T) for _ in range(3)] for _ in range(3)]
        b1_parts = [early(PARTS * T // 2).bitcast(BF16).rearrange("p (a t) -> p a t", a=PARTS)
                    for _ in range(3)]
        cos_sb, sin_sb = early(T), early(T)
        rot_sb = sb("rot", [P, P], F32)
        tile_words, tile_parts = b0_words + b1_words, b0_parts + b1_parts
        TILE_ROWS = [HKV * HD, P, P] * B
        xn = pbuf[:, 0:S * D // P].rearrange("p (t d) -> p t d", t=NT)
        hT = attn[:].rearrange("p a b c -> p (a b c)").rearrange("p (c s) -> p c s", c=DC)
        HALF = S * D // P
        attnT = pbuf[:, 0:HALF].rearrange("p (a t) -> p a t", a=B * DC)
        h2 = pbuf[:, HALF:2 * HALF].rearrange("p (t d) -> p t d", t=NT)
        qx_words = qx[:].rearrange("p a b c -> p (a b c)").bitcast(F32)
        h2T = qx_words[:, 0:HALF].rearrange("p (c s) -> p c s", c=DC)
        routed = qx_words[:, HALF:2 * HALF].rearrange("p (e d) -> p e d", e=E)
        routedT = hT
        gelu = pbuf[:, 0:HALF].rearrange("p (a f s) -> p a f s", a=2, f=FT)
        picked = qx_words[:, 0:HALF].rearrange("p (t d) -> p t d", t=NT)
        expert_sb = osb[:, :].rearrange("p (a d) -> p a d", a=2)
        probs = pbuf[:].rearrange("p (a i t) -> p a i t", a=2, i=G)
        y_work = osb[:].rearrange("p (t d) -> p t d", t=2)
        w1_sb = [wbuf[:, 2 * e * CHUNK:(2 * e + 1) * CHUNK].rearrange("p (c f) -> p c f", c=DC)
                 for e in range(E)]
        w2_sb = [wbuf[:, (2 * e + 1) * CHUNK:(2 * e + 2) * CHUNK].rearrange("p (t d) -> p t d", t=FT)
                 for e in range(E)]
        w1_v = w1.rearrange("e (c p) f -> e p c f", p=P)
        w2_v = w2.rearrange("e (t p) d -> e p t d", p=P)
        x_v = x.rearrange("(t p) d -> p t d", p=P)
        out_v = out.rearrange("(t p) d -> p t d", p=P)


        def q_rows(half):
            return qx_dram[half * P // HD:(half + 1) * P // HD].rearrange(
                "h (d r a) t -> (h d) r (a t)", r=PARTS, a=PARTS)

        def k_rows(b):
            return kx_dram[b * HKV:(b + 1) * HKV].rearrange("h (d a r) t -> (h d) a r t", r=PARTS, a=PARTS)

        def copies(ap):
            return ap.unsqueeze(1).to_broadcast([ap.shape[0], PARTS, ap.shape[1]])

        def all_parts(n):
            return tile_parts[n].rearrange("p a t -> p (a t)")

        c_in, wmod_in, wqkv_in, bias_in, rope_in, wo_in = map(
            sem, ("c_in", "wmod_in", "wqkv_in", "bias_in", "rope_in", "wo_in"))
        x_in = [sem(f"x_in{b}") for b in range(B)]
        consts = sem("consts")
        ident_done, masks_done, rows_clear = sem("ident_done"), sem("masks_done"), sem("rows_clear")
        routed_zero, zeros_done, o_clear, row_one = map(
            sem, ("routed_zero", "zeros_done", "o_clear", "row_one"))
        c_exp_done, silu_done, mod_done, mod_saved = map(
            sem, ("c_exp_done", "silu_done", "mod_done", "mod_saved"))
        var_done, rstd_done, xn_done = map(sem, ("var_done", "rstd_done", "xn_done"))
        xT_done, hT_by_dve, hT_by_act = map(sem, ("xT_done", "hT_by_dve", "hT_by_act"))
        proj_done, v_proj_done, biased, rotated = map(
            sem, ("proj_done", "v_proj_done", "biased", "rotated"))
        rot_read, rot_copied, vx_done = map(sem, ("rot_read", "rot_copied", "vx_done"))
        split_by_dve, split_by_pool = sem("split_by_dve"), sem("split_by_pool")
        kx_written, qx_written = sem("kx_written"), sem("qx_written")
        kx_b1_written, qx_b1_written = sem("kx_b1_written"), sem("qx_b1_written")
        rows_in_dram = sem("rows_in_dram")
        rows_done, rows_copied = sem("rows_done"), sem("rows_copied")
        xg_done = sem("xg_done")
        dve_step, pool_step = sem("dve_step"), sem("pool_step")
        qk_in = [sem(f"qk_in{u}") for u in range(SLOTS)]
        shift_in = [sem(f"shift_in{u}") for u in range(SLOTS)]
        a_done, max_done, b_done, exp_done, pv_done = map(
            sem, ("a_done", "max_done", "b_done", "exp_done", "pv_done"))
        neg_hi, neg_done, negT_done, shift_saved = map(
            sem, ("neg_hi", "neg_done", "negT_done", "shift_saved"))
        vs_done, o_saved, oT_done, rden_done, norm_done = map(
            sem, ("vs_done", "o_saved", "oT_done", "rden_done", "norm_done"))
        h2_norm, rT_by_dve, rT_by_act = map(
            sem, ("h2_norm", "rT_by_dve", "rT_by_act"))
        w_in = [sem(f"w_in{k}") for k in range(2)]
        aT_done, aT_saved, wo_done, wo_read = map(sem, ("aT_done", "aT_saved", "wo_done", "wo_read"))
        var2_done, rstd2_done, h2_done, h2T_done, h2T_saved = map(
            sem, ("var2_done", "rstd2_done", "h2_done", "h2T_done", "h2T_saved"))
        logits_done, gate_sub, gate_exp, onehot_done, count_done = map(
            sem, ("logits_done", "gate_sub", "gate_exp", "onehot_done", "count_done"))
        slots_done, scattered, rT_done = map(sem, ("slots_done", "scattered", "rT_done"))
        routed_in = [sem(f"routed_in{k}") for k in range(2)]
        h_done, gelu_done, y_done, y_saved = map(sem, ("h_done", "gelu_done", "y_done", "y_saved"))
        y_out = [sem(f"y_out{k}") for k in range(2)]
        picked_zero, final_done, out_done = map(sem, ("picked_zero", "final_done", "out_done"))
        picked_in = [sem(f"picked_in{t}") for t in range(NT)]

        block = ctx.enter_context(nc.Block())

        TURNS = (NG - 4) // SLOTS


        @block.sync
        def _(sp):
            sp.dma_start(cT[:], c_t.rearrange("(c p) b -> p c b", p=P)).then_inc(c_in, 16)
            sp.dma_start(xres[:, 0:TB, :], x_v[:, 0:TB, :]).then_inc(x_in[0], 16)
            sp.dma_start(wmod_sb, wmod.rearrange("(c p) n -> p c n", p=P)).then_inc(wmod_in, 16)
            sp.dma_start(wqkv_sb, wqkv_t.rearrange("(c p) n -> p c n", p=P)).then_inc(wqkv_in, 16)
            sp.dma_start(xres[:, TB:, :], x_v[:, TB:, :]).then_inc(x_in[1], 16)

            sp.wait_ge(split_by_dve, 1)
            for a in range(PARTS):
                sp.dma_start(k_rows(0)[:, a], copies(tile_parts[0][0:HKV * HD, a, :])).then_inc(kx_written, 16)
            sp.wait_ge(split_by_dve, 2)
            sp.dma_start(q_rows(0), copies(all_parts(1))).then_inc(qx_written, 16)

            def load_group(g, u):
                sp.dma_start(kx[0:ROWS, u, :], kx_dram[g]).then_inc(qk_in[u], 16)
                sp.dma_start(qx[0:ROWS, u, :, :],
                             qx_dram[bass.ds(g * G, G)].rearrange("i r t -> r i t")).then_inc(qk_in[u], 16)

            def load_shift(buf, u):
                sp.dma_start(qx[SHIFT_ROW:BROWS, u, :, :].rearrange("a i (q t) -> a (i q) t", q=TB),
                             shift_rows[:, buf, :]).then_inc(shift_in[u], 16)

            sp.wait_ge(consts, 2)
            sp.wait_ge(rows_clear, 1)
            sp.wait_ge(kx_written, 16 * PARTS)
            sp.wait_ge(qx_written, 16)
            for g in range(3):
                load_group(g, g)
            sp.wait_ge(split_by_dve, 3)
            sp.dma_start(q_rows(1), copies(all_parts(2))).then_inc(qx_written, 16)
            sp.wait_ge(shift_saved, 1)
            load_shift(0, 0)

            def period(it, v, load=True, shift=True):
                g = 4 * it + 1 + v
                if load:
                    if not isinstance(it, int):
                        sp.wait_ge(b_done, 16 * g)
                    load_group(g + 3, v)
                if shift:
                    sp.wait_ge(shift_saved, g + 2)
                    load_shift((v + 2) % 2, (v + 2) % SLOTS)
                if v % 2:
                    sp.dma_start(wbuf[:, bass.ds(g * CHUNK, CHUNK)].rearrange("p (c f) -> p c f", c=DC),
                                 w1_v[2 * it + (1 + v) // 2]).then_inc(w_in[0], 16)
                else:
                    sp.dma_start(wbuf[:, bass.ds(g * CHUNK, CHUNK)].rearrange("p (t d) -> p t d", t=FT),
                                 w2_v[2 * it + v // 2]).then_inc(w_in[1], 16)

            period(-1, 3)
            with sp.Fori(0, TURNS) as it:
                for v in range(SLOTS):
                    period(it, v)
            period(TURNS, 0, load=False)
            period(TURNS, 1, load=False)
            period(TURNS, 2, load=False, shift=False)

            sp.wait_ge(scattered, 16 * NT)
            for half in range(2):
                es = slice(half * E // 2, (half + 1) * E // 2)
                sp.dma_start(routed[:, es, :],
                             routed_dram.rearrange("(e p) d -> p e d", p=P)[:, es, :]).then_inc(routed_in[half], 16)
            for e in range(E):
                sp.wait_ge(y_saved, e + 1)
                sp.dma_start(expert_dram[e * CAP:(e + 1) * CAP, :], expert_sb[:, e % 2, :]).then_inc(y_out[e % 2], 16)
            for k in range(NT // 2):
                sp.wait_ge(final_done, k + 1)
                sp.dma_start(out_v[:, 2 * k:2 * k + 2, :], picked[:, 2 * k:2 * k + 2, :]).then_inc(out_done, 16)
            sp.wait_ge(out_done, 16 * (NT // 2))

        @block.gpsimd
        def _(pool):
            step = [0]

            def link(ins):
                step[0] += 1
                ins.then_inc(pool_step, 1)
                pool.wait_ge(pool_step, step[0])

            link(nc.gpsimd.memset(ident[:], 0.0))
            nc.gpsimd.affine_select(out=ident[:], in_=ident[:], compare_op=ALU.not_equal, fill=1.0,
                                    base=0, pattern=[[-1, P]], channel_multiplier=1).then_inc(ident_done, 1)
            link(nc.gpsimd.memset(minus_half[:], -0.5))
            nc.gpsimd.memset(qx[64:SHIFT_ROW].rearrange("p a b c -> p (a b c)").bitcast(F32),
                             0.0).then_inc(rows_clear, 1)
            pool.wait_ge(rows_clear, 1)
            for b in range(B):
                ts = slice(b * TB, (b + 1) * TB)
                pool.wait_ge(var_done, b + 1)
                nc.gpsimd.tensor_tensor(rstd[:, ts], rstd[:, ts], minus_half[:, ts],
                                        ALU.pow).then_inc(rstd_done, 1)
                pool.wait_ge(rstd_done, b + 1)
            pool.wait_ge(ident_done, 1)
            link(nc.gpsimd.tensor_copy(ident_h[:], ident[:]))
            link(nc.gpsimd.memset(ones_h[:], 1.0))
            nc.gpsimd.affine_select(out=before[:], in_=ones_h[:], compare_op=ALU.is_gt, fill=0.0,
                                    base=0, pattern=[[1, P]], channel_multiplier=-1).then_inc(masks_done, 1)
            pool.wait_ge(masks_done, 1)
            nc.gpsimd.iota(expert_no[:], pattern=[[0, NT], [-1, E]], base=E, channel_multiplier=0,
                           allow_small_or_imprecise_dtypes=True).then_inc(masks_done, 1)
            pool.wait_ge(masks_done, 2)

            pool.wait_ge(rope_in, 48)
            for n in range(3, 6):
                r = TILE_ROWS[n]
                biased_w, turned_w, sum_w = (w[0:r, :] for w in tile_words[n])
                part = tile_parts[n]
                pool.wait_ge(rot_copied, n - 2)
                link(nc.gpsimd.tensor_tensor(turned_w, turned_w, sin_sb[0:r, :], ALU.mult))
                link(nc.gpsimd.tensor_tensor(sum_w, biased_w, cos_sb[0:r, :], ALU.mult))
                link(nc.gpsimd.tensor_tensor(sum_w, sum_w, turned_w, ALU.add))
                link(nc.gpsimd.tensor_copy(part[0:r, 0, :], sum_w))
                link(nc.gpsimd.tensor_tensor(sum_w, sum_w, part[0:r, 0, :], ALU.subtract))
                link(nc.gpsimd.tensor_copy(part[0:r, 1, :], sum_w))
                link(nc.gpsimd.tensor_tensor(part[0:r, 2, :], sum_w, part[0:r, 1, :], ALU.subtract))
                if n == 3:
                    for a in range(PARTS):
                        pool.dma_start(k_rows(1)[:, a], copies(part[0:r, a, :])).then_inc(kx_b1_written, 16)
                    pool.wait_ge(qx_written, 32)
                    pool.sem_inc(rows_in_dram, 1)
                else:
                    pool.dma_start(q_rows(n - 2), copies(all_parts(n))).then_inc(qx_b1_written, 16)
                    pool.wait_ge(kx_b1_written, 16 * PARTS)
                    pool.wait_ge(qx_b1_written, 16 * (n - 3))
                    pool.sem_inc(rows_in_dram, 1)
            pool.sem_inc(rows_in_dram, 1)

            pool.wait_ge(rows_copied, 4)
            pool.wait_ge(bias_in, 64)
            sign = ga_bo[:].rearrange("p b d -> p (b d)")
            for m in (0, 3):
                gate = rows[:, m].rearrange("p b d -> p (b d)")
                link(nc.gpsimd.tensor_scalar(sign, gate, 0.0, 2.0, ALU.is_ge, ALU.mult))
                link(nc.gpsimd.tensor_scalar(sign, sign, -1.0, None, ALU.add))
                link(nc.gpsimd.tensor_tensor(gate, gate, sign, ALU.mult))
                link(nc.gpsimd.tensor_scalar(gate, gate, GATE_MIN, None, ALU.max))
                link(nc.gpsimd.tensor_tensor(gate, gate, sign, ALU.mult))
            for b in range(B):
                link(nc.gpsimd.tensor_tensor(ga_bo[:, b], rows[:, 0, b], bo_sb[:], ALU.mult))
                for t in range(b * TB, (b + 1) * TB):
                    nc.gpsimd.tensor_tensor(xres[:, t], xres[:, t], ga_bo[:, b], ALU.add).then_inc(xg_done, 1)
                    pool.wait_ge(xg_done, t + 1)
            nc.gpsimd.memset(zeros_row[:], 0.0).then_inc(zeros_done, 1)
            pool.wait_ge(zeros_done, 1)
            pool.dma_start(routed_dram.rearrange("(p e) d -> p e d", p=P),
                           zeros_row[:].unsqueeze(1).to_broadcast([P, E, D])).then_inc(routed_zero, 16)

            for b in range(B):
                ts = slice(b * TB, (b + 1) * TB)
                pool.wait_ge(var2_done, b + 1)
                nc.gpsimd.tensor_tensor(rstd[:, ts], rstd[:, ts], minus_half[:, ts],
                                        ALU.pow).then_inc(rstd2_done, 1)
                pool.wait_ge(rstd2_done, b + 1)

            pool.wait_ge(routed_zero, 16)
            pool.wait_ge(slots_done, 1)
            pool.wait_ge(h2_done, B)
            for t in range(NT):
                pool.indirect_dma_start(
                    routed_dram[:, :], bass.IndirectOffsetOnAxis(ap=slot_i[:, t:t + 1], axis=0),
                    h2[:, t, :], None, bounds_check=E * CAP - 1, oob_is_err=False).then_inc(scattered, 16)

            pool.wait_ge(logits_done, 1)
            nc.gpsimd.memset(picked, 0.0).then_inc(picked_zero, 1)
            pool.wait_ge(picked_zero, 1)
            for k in range(2):
                pool.wait_ge(y_out[k], 16 * (E // 2))
            for t in range(NT):
                pool.indirect_dma_start(
                    picked[:, t, :], None, expert_dram[:, :],
                    bass.IndirectOffsetOnAxis(ap=slot_i[:, t:t + 1], axis=0),
                    bounds_check=E * CAP - 1, oob_is_err=False).then_inc(picked_in[t], 16)

        @block.scalar
        def _(act):
            act.dma_start(bq_sb[:], bq).then_inc(bias_in, 16)
            act.dma_start(bk_sb[:], bk.rearrange("(p a) -> p a", a=1)).then_inc(bias_in, 16)
            act.dma_start(rot_sb[:], rope_rot).then_inc(rope_in, 16)
            act.dma_start(bv_sb[:], bv.rearrange("(a n) -> a n", a=1).to_broadcast([P, HKV * HD])).then_inc(bias_in, 16)
            act.dma_start(bo_sb[:], bo.rearrange("(a n) -> a n", a=1).to_broadcast([P, D])).then_inc(bias_in, 16)
            act.dma_start(cos_sb, rope_cos).then_inc(rope_in, 16)
            act.dma_start(sin_sb, rope_sin).then_inc(rope_in, 16)
            act.dma_start(wo_sb[:], wo_t.rearrange("(c p) n -> p c n", p=P)).then_inc(wo_in, 16)
            act.dma_start(wg_sb[:], w_gate.rearrange("(c p) n -> p c n", p=P)).then_inc(wo_in, 16)
            act.wait_ge(c_in, 16)
            nc.scalar.activation(c_exp[:], cT[:], ACT.Exp, scale=-1.0).then_inc(c_exp_done, 1)

            def modulate(b):
                act.wait_ge(mod_saved, 2)
                act.wait_ge(xT_done, 2 * b + 2)
                nc.scalar.activation(hT[:, 1, b * T:(b + 1) * T], bank[2 * b + 1][:], ACT.Identity,
                                     bias=mod_shift[:, 1, b:b + 1],
                                     scale=mod_scale[:, 1, b:b + 1]).then_inc(hT_by_act, 1)

            def add_bias(n):
                r = TILE_ROWS[n]
                act.wait_ge(proj_done, n + 1)
                if n == 0:
                    act.wait_ge(bias_in, 64)
                bias = bk_sb[:] if n % 3 == 0 else bq_sb[:, n % 3 - 1:n % 3]
                nc.scalar.activation(tile_words[n][0][0:r, :], bank[PROJ_BANK[n]][0:r, :], ACT.Identity,
                                     bias=bias).then_inc(biased, 1)

            modulate(0)
            for n in range(3):
                add_bias(n)
            modulate(1)
            for n in range(3, 6):
                add_bias(n)
            for n in range(3, 6):
                r = TILE_ROWS[n]
                act.wait_ge(rotated, n + 1)
                nc.scalar.copy(tile_words[n][1][0:r, :], bank[ROT_BANK[n]][0:r, :]).then_inc(rot_copied, 1)
            for k in range(4):
                b, half = k // 2, k % 2
                act.wait_ge(rows_done, k + 1)
                src = bank[ROWS_BANK[k]][:].rearrange("p (m d) -> p m d", m=2)
                dst = rows[:, 2 * half:2 * half + 2, b, :]
                if half == 0:
                    nc.scalar.copy(dst, src).then_inc(rows_copied, 1)
                else:
                    nc.scalar.activation(dst[:, 0], src[:, 0], ACT.Identity, bias=one[:]).then_inc(row_one, 1)
                    nc.scalar.copy(dst[:, 1], src[:, 1]).then_inc(rows_copied, 1)

            def period(it, v):
                g = 4 * it + 1 + v
                for j in range(TB):
                    for i in range(G):
                        act.wait_ge(b_done, 16 * g + 4 * j + i + 1)
                        if i == 0 and not (v == 3 and isinstance(it, int) and j < 2):
                            act.wait_ge(pv_done, 4 * g + j - 1)
                        nc.scalar.activation(probs[:, j % 2, i, :], exp_bank[i % 2][:], ACT.Exp,
                                             scale=SCALE).then_inc(exp_done, 1)
                    if j == 0 and not (v == 3 and isinstance(it, int)):
                        save_o(4 * g)

            def save_o(steps):
                act.wait_ge(pv_done, steps)
                nc.scalar.copy(osb[:], o_bank[:]).then_inc(o_saved, 1)

            period(-1, 3)
            with act.Fori(0, TURNS) as it:
                for v in range(SLOTS):
                    period(it, v)
            for v in range(3):
                period(TURNS, v)
            save_o(4 * NG)

            for k in range(B * DC):
                act.wait_ge(aT_done, k + 1)
                nc.scalar.copy(attnT[:, k, :], bank[k][:]).then_inc(aT_saved, 1)
            for b in range(B):
                for c in range(DC):
                    act.wait_ge(h2T_done, DC * b + c + 1)
                    nc.scalar.copy(h2T[:, c, b * T:(b + 1) * T], bank[DC * b + c][:]).then_inc(h2T_saved, 1)
            act.wait_ge(gate_sub, 1)
            nc.scalar.activation(gate_e, gate_e, ACT.Exp).then_inc(gate_exp, 1)
            for c in range(DC):
                act.wait_ge(rT_done, DC + c + 1)
                nc.scalar.copy(routedT[:, c, S // 2:], bank[2 + c][:]).then_inc(rT_by_act, 1)
            for e in range(E):
                for k in range(2):
                    act.wait_ge(h_done, 2 * e + k + 1)
                    if e >= 2 and k == 0:
                        act.wait_ge(y_done, e - 1)
                    nc.scalar.activation(
                        gelu[:, e % 2, k * FT // 2:(k + 1) * FT // 2, :].rearrange("p f s -> p (f s)"),
                        bank[2 * (e % 2) + k][:], ACT.Gelu_apprx_tanh).then_inc(gelu_done, 1)

        @block.vector
        def _(dve):
            step = [0]

            def link(ins):
                step[0] += 1
                ins.then_inc(dve_step, 1)
                dve.wait_ge(dve_step, step[0])

            nc.vector.memset(one[:], 1.0).then_inc(consts, 1)
            link(nc.vector.memset(kx[64:SHIFT_ROW].rearrange("p a b -> p (a b)").bitcast(F32), 0.0))
            nc.vector.memset(kx[SHIFT_ROW:P].rearrange("p a b -> p (a b)"), 1.0).then_inc(consts, 1)
            nc.vector.memset(vx[:], 1.0).then_inc(consts, 1)
            dve.wait_ge(consts, 3)
            dve.wait_ge(c_exp_done, 1)
            link(nc.vector.tensor_scalar_add(c_exp[:], c_exp[:], 1.0))
            link(nc.vector.reciprocal(c_exp[:], c_exp[:]))
            nc.vector.tensor_tensor(silu[:], cT[:], c_exp[:], ALU.mult).then_inc(silu_done, 1)

            def norm_stats(b, done):
                for t in range(b * TB, (b + 1) * TB):
                    link(nc.vector.bn_stats(stats[:, t, :], xres[:, t, :]))
                    link(nc.vector.bn_aggr(meanvar[:, t, :], stats[:, t, :]))
                ts = slice(b * TB, (b + 1) * TB)
                nc.vector.tensor_scalar(rstd[:, ts], meanvar[:, ts, 1], EPS, None, ALU.add).then_inc(done, 1)

            def normalise(b, dst, ready, done):
                dve.wait_ge(ready, b + 1)
                for t in range(b * TB, (b + 1) * TB):
                    nc.vector.tensor_scalar(dst[:, t, :], xres[:, t, :], meanvar[:, t, 0:1], rstd[:, t:t + 1],
                                            ALU.subtract, ALU.mult).then_inc(done, 1)

            def modulate(b):
                dve.wait_ge(xT_done, 2 * b + 1)
                nc.vector.tensor_scalar(hT[:, 0, b * T:(b + 1) * T], bank[2 * b][:], mod_scale[:, 0, b:b + 1],
                                        mod_shift[:, 0, b:b + 1], ALU.mult, ALU.add).then_inc(hT_by_dve, 1)

            dve.wait_ge(x_in[0], 16)
            norm_stats(0, var_done)
            dve.wait_ge(mod_done, 1)
            mod_ps = bank[7][:, 0:2 * DC * B].rearrange("p (m c b) -> p m c b", m=2, c=DC)
            nc.vector.tensor_copy(mod_shift[:], mod_ps[:, 0]).then_inc(mod_saved, 1)
            nc.vector.tensor_scalar_add(mod_scale[:], mod_ps[:, 1], 1.0).then_inc(mod_saved, 1)
            normalise(0, xn, rstd_done, xn_done)
            dve.wait_ge(x_in[1], 16)
            norm_stats(1, var_done)
            dve.wait_ge(mod_saved, 2)
            modulate(0)
            normalise(1, xn, rstd_done, xn_done)

            def rope_split(n):
                r = TILE_ROWS[n]
                biased_w, turned_w, sum_w = (w[0:r, :] for w in tile_words[n])
                part = tile_parts[n]
                dve.wait_ge(biased, n + 1)
                link(nc.vector.tensor_tensor(sum_w, biased_w, cos_sb[0:r, :], ALU.mult))
                dve.wait_ge(rotated, n + 1)
                rotated_ps = nc.vector.tensor_tensor(turned_w, bank[ROT_BANK[n]][0:r, :], sin_sb[0:r, :], ALU.mult)
                rotated_ps.then_inc(rot_read, 1)
                dve.wait_ge(rot_read, n + 1)
                link(nc.vector.tensor_tensor(sum_w, sum_w, turned_w, ALU.add))
                link(nc.vector.tensor_copy(part[0:r, 0, :], sum_w))
                link(nc.vector.tensor_tensor(sum_w, sum_w, part[0:r, 0, :], ALU.subtract))
                link(nc.vector.tensor_copy(part[0:r, 1, :], sum_w))
                nc.vector.tensor_tensor(part[0:r, 2, :], sum_w, part[0:r, 1, :],
                                        ALU.subtract).then_inc(split_by_dve, 1)

            def save_v(b):
                dve.wait_ge(v_proj_done, b + 1)
                dve.wait_ge(bias_in, 64)
                dst = vx[:, b * HKV:(b + 1) * HKV, :].rearrange("p h (k c) -> p h k c", c=HD + 1)[:, :, :, 0:HD]
                for k in range(TB):
                    nc.vector.tensor_tensor(
                        dst[:, :, k, :],
                        bank[6][:, k * HKV * HD:(k + 1) * HKV * HD].rearrange("p (h d) -> p h d", h=HKV),
                        bv_sb[:].rearrange("p (h d) -> p h d", h=HKV), ALU.add).then_inc(vx_done, 1)

            dve.wait_ge(rope_in, 48)
            rope_split(0)
            save_v(0)
            modulate(1)
            rope_split(1)
            rope_split(2)
            save_v(1)
            dve.wait_ge(vx_done, 2 * TB)
            nc.vector.memset(o_bank[:], 0.0).then_inc(o_clear, 1)

            def take_max(count, buf, col, i):
                dve.wait_ge(a_done, count)
                nc.vector.tensor_reduce(negmax[:, buf, col:col + 1], max_bank[i][:], AX_X, ALU.max,
                                        negate=True).then_inc(max_done, 1)

            def split_max(g, buf):
                dve.wait_ge(max_done, 16 * (g + 1))
                if not (isinstance(g, int) and g == 0):
                    dve.wait_ge(negT_done, g)
                nc.vector.tensor_copy(negparts[:, 0, :], negmax[:, buf, :]).then_inc(neg_hi, 1)
                dve.wait_ge(neg_hi, g + 1)
                nc.vector.tensor_tensor(negparts[:, 1, :], negmax[:, buf, :], negparts[:, 0, :],
                                        ALU.subtract).then_inc(neg_done, 1)

            def save_shift(g, buf, slot, turn):
                dve.wait_ge(negT_done, g + 1)
                if slot is not None:
                    dve.wait_ge(shift_in[slot], 16 * turn)
                nc.vector.tensor_copy(shift_rows[:, buf, :],
                                      tr_bank[0:2 * G * TB, 0:P // 2].bitcast(BF16)).then_inc(shift_saved, 1)

            def copy_v(g, u):
                nc.vector.tensor_copy(vs[:, u].rearrange("p k c -> p (k c)"), vx[:, g, :]).then_inc(vs_done, 1)

            def norm(g, it, u):
                dve.wait_ge(oT_done, g + 1)
                o = tr_bank[:].rearrange("p (q i c) -> p q i c", q=TB, i=G)
                nc.vector.reciprocal(rden[:], o[:, :, :, HD]).then_inc(rden_done, 1)
                dve.wait_ge(rden_done, g + 1)
                nc.vector.tensor_tensor(
                    attn[:, it, :, u * G * HD:(u + 1) * G * HD].rearrange("p q (i d) -> p q i d", i=G),
                    o[:, :, :, 0:HD], rden[:].unsqueeze(3).to_broadcast([P, TB, G, HD]),
                    ALU.mult).then_inc(norm_done, 1)

            def period(it, v, take=True, split=True):
                g = 4 * it + 1 + v
                first = isinstance(it, int) and it == -1
                if split:
                    split_max(g + 1, (v + 2) % 2)
                    copy_v(g + 1, (v + 2) % SLOTS)
                for j in range(TB):
                    if take:
                        if j == 0:
                            dve.wait_ge(neg_done, g + 1)
                        for i in range(G):
                            take_max(16 * (g + 2) + 4 * j + i + 1, (v + 3) % 2, 4 * i + j, i)
                    if j == 1 and split:
                        save_shift(g + 1, (v + 2) % 2, None if first else v, it + 1)
                if not first:
                    norm(g - 1, it, v)

            for j in range(TB):
                for i in range(G):
                    take_max(4 * j + i + 1, 0, 4 * i + j, i)
            split_max(0, 0)
            copy_v(0, 0)
            for j in range(TB):
                for i in range(G):
                    take_max(16 + 4 * j + i + 1, 1, 4 * i + j, i)
                if j == 1:
                    save_shift(0, 0, None, 0)
            period(-1, 3)
            with dve.Fori(0, TURNS) as it:
                for v in range(SLOTS):
                    period(it, v)
            period(TURNS, 0)
            period(TURNS, 1, take=False)
            period(TURNS, 2, take=False, split=False)
            norm(NG - 1, TURNS, 3)

            for k in range(NT // 2):
                b = 2 * k // TB
                dve.wait_ge(wo_done, k + 1)
                if k == 0:
                    dve.wait_ge(xg_done, NT)
                y = bank[4 + k][:].rearrange("p (t d) -> p t d", t=2)
                ts = slice(2 * k, 2 * k + 2)
                nc.vector.tensor_tensor(y_work[:], y, rows[:, 0, b].unsqueeze(1).to_broadcast([P, 2, D]),
                                        ALU.mult).then_inc(wo_read, 1)
                dve.wait_ge(wo_read, k + 1)
                link(nc.vector.tensor_tensor(xres[:, ts, :], xres[:, ts, :], y_work[:], ALU.add))
                if k % 2 == 1:
                    norm_stats(b, var2_done)

            for b in range(B):
                ts = slice(b * TB, (b + 1) * TB)
                normalise(b, h2, rstd2_done, h2_norm)
                dve.wait_ge(h2_norm, TB * (b + 1))
                link(nc.vector.tensor_tensor(h2[:, ts], h2[:, ts],
                                             rows[:, 2, b].unsqueeze(1).to_broadcast([P, TB, D]), ALU.mult))
                nc.vector.tensor_tensor(h2[:, ts], h2[:, ts],
                                        rows[:, 1, b].unsqueeze(1).to_broadcast([P, TB, D]),
                                        ALU.add).then_inc(h2_done, 1)

            def over_e(ap):
                return ap.unsqueeze(2).to_broadcast([P, NT, E])

            top, total, best, place, number, keep, gate = (g_one[:, k] for k in range(7))
            logits = bank[4][:, 0:NT * E].rearrange("p (t e) -> p t e", e=E)
            dve.wait_ge(logits_done, 1)
            link(nc.vector.tensor_reduce(top, logits, AX_X, ALU.max))
            nc.vector.tensor_tensor(gate_e, logits, over_e(top), ALU.subtract).then_inc(gate_sub, 1)
            dve.wait_ge(gate_exp, 1)
            link(nc.vector.tensor_reduce(total, gate_e, AX_X, ALU.add))
            link(nc.vector.reciprocal(total, total))
            link(nc.vector.tensor_tensor(gate_e, gate_e, over_e(total), ALU.mult))
            link(nc.vector.tensor_reduce(gate, gate_e, AX_X, ALU.max))
            link(nc.vector.tensor_tensor(is_top, gate_e, over_e(gate), ALU.is_equal))
            link(nc.vector.tensor_tensor(is_top, is_top, expert_no[:], ALU.mult))
            link(nc.vector.tensor_reduce(best, is_top, AX_X, ALU.max))
            nc.vector.tensor_tensor(onehot[:], is_top, over_e(best), ALU.is_equal).then_inc(onehot_done, 1)
            dve.wait_ge(count_done, 1)
            counts = bank[5][:, 0:NT * E].rearrange("p (t e) -> p t e", e=E)
            dve.wait_ge(onehot_done, 1)
            link(nc.vector.tensor_tensor(is_top, counts, onehot[:], ALU.mult))
            link(nc.vector.tensor_reduce(place, is_top, AX_X, ALU.add))
            link(nc.vector.tensor_scalar(keep, place, float(CAP), None, ALU.is_lt))
            link(nc.vector.tensor_tensor(gate, gate, keep, ALU.mult))
            link(nc.vector.tensor_scalar(number, best, -float(CAP), float(E * CAP), ALU.mult, ALU.add))
            link(nc.vector.tensor_tensor(place, place, number, ALU.add))
            link(nc.vector.tensor_scalar(keep, keep, -float(FAR), float(FAR), ALU.mult, ALU.add))
            nc.vector.tensor_tensor(slot_i[:], place, keep, ALU.add).then_inc(slots_done, 1)

            for c in range(DC):
                dve.wait_ge(rT_done, c + 1)
                nc.vector.tensor_copy(routedT[:, c, 0:S // 2], bank[c][:]).then_inc(rT_by_dve, 1)
            for e in range(E):
                dve.wait_ge(y_done, e + 1)
                if e >= 2:
                    dve.wait_ge(y_out[e % 2], 16 * (e // 2))
                nc.vector.tensor_copy(expert_sb[:, e % 2, :], bank[4 + e % 2][:, 0:D]).then_inc(y_saved, 1)

            for t in range(NT):
                dve.wait_ge(picked_in[t], 16)
                link(nc.vector.scalar_tensor_tensor(out=picked[:, t], in0=picked[:, t], scalar=gate[:, t:t + 1],
                                                    in1=rows[:, 3, t // TB], op0=ALU.mult, op1=ALU.mult))
                last = nc.vector.tensor_tensor(picked[:, t], picked[:, t], xres[:, t], ALU.add)
                if t % 2:
                    last.then_inc(final_done, 1)
                else:
                    link(last)

        @block.tensor
        def _(pe):
            pe.wait_ge(silu_done, 1)
            pe.wait_ge(wmod_in, 16)
            for m in range(2):
                for c in range(DC):
                    col = (m * DC + c) * B
                    for k in range(DC):
                        last = nc.tensor.matmul(bank[7][:, col:col + B],
                                                wmod_sb[:, k, m * D + c * P:m * D + (c + 1) * P],
                                                silu[:, k, :], start=(k == 0), stop=(k == DC - 1))
            last.then_inc(mod_done, 1)

            def transpose_x(b):
                for c in range(DC):
                    for t in range(TB):
                        if c == 0:
                            pe.wait_ge(xn_done, TB * b + t + 1)
                        last = nc.tensor.transpose(bank[DC * b + c][:, t * P:(t + 1) * P],
                                                   xn[:, TB * b + t, c * P:(c + 1) * P], ident[:])
                    last.then_inc(xT_done, 1)

            def project(n, lo):
                b, r = n // 3, TILE_ROWS[n]
                for c in range(DC):
                    last = nc.tensor.matmul(bank[PROJ_BANK[n]][0:r, :], wqkv_sb[:, c, lo:lo + r],
                                            hT[:, c, b * T:(b + 1) * T], start=(c == 0), stop=(c == DC - 1))
                last.then_inc(proj_done, 1)

            def project_v(b):
                for t in range(TB):
                    for c in range(DC):
                        s0 = b * T + t * P
                        last = nc.tensor.matmul(bank[6][:, t * HKV * HD:(t + 1) * HKV * HD],
                                                hT[:, c, s0:s0 + P], wqkv_sb[:, c, (HQ + HKV) * HD:],
                                                start=(c == 0), stop=(c == DC - 1))
                last.then_inc(v_proj_done, 1)

            def rotate(n):
                r = TILE_ROWS[n]
                pe.wait_ge(biased, n + 1)
                nc.tensor.matmul(bank[ROT_BANK[n]][0:r, :], rot_sb[0:r, 0:r], tile_words[n][0][0:r, :],
                                 start=True, stop=True).then_inc(rotated, 1)

            pe.wait_ge(ident_done, 1)
            transpose_x(0)
            transpose_x(1)
            pe.wait_ge(wqkv_in, 16)
            pe.wait_ge(rope_in, 48)
            pe.wait_ge(hT_by_dve, 1)
            pe.wait_ge(hT_by_act, 1)
            project(0, HQ * HD)
            project(1, 0)
            pe.wait_ge(mod_saved, 2)
            rotate(0)
            project_v(0)
            rotate(1)
            project(2, P)
            rotate(2)
            pe.wait_ge(hT_by_dve, 2)
            pe.wait_ge(hT_by_act, 2)
            project(3, HQ * HD)
            project(4, 0)
            project(5, P)
            pe.wait_ge(vx_done, TB)
            project_v(1)
            rotate(3)
            pe.wait_ge(rot_read, 1)
            rotate(4)
            rotate(5)
            for k in range(4):
                b, half = k // 2, k % 2
                if k < 2:
                    pe.wait_ge(rot_read, k + 2)
                for c in range(DC):
                    last = nc.tensor.matmul(bank[ROWS_BANK[k]][:], silu[:, c, b:b + 1].to_broadcast([P, P]),
                                            wmod_sb[:, c, (2 + 2 * half) * D:(4 + 2 * half) * D],
                                            start=(c == 0), stop=(c == DC - 1))
                last.then_inc(rows_done, 1)
            pe.wait_ge(rot_copied, 3)
            pe.wait_ge(rows_copied, 4)

            def max_scores(n, slot, j, i, free):
                if free is not None:
                    pe.wait_ge(max_done, free)
                nc.tensor.matmul(max_bank[i][:], qx[0:SHIFT_ROW, slot, i, j * P:(j + 1) * P],
                                 kx[0:SHIFT_ROW, slot, :], start=True, stop=True).then_inc(a_done, 1)

            def exp_scores(slot, j, i, free):
                if free is not None:
                    pe.wait_ge(exp_done, free)
                nc.tensor.matmul(exp_bank[i % 2][:], kx[0:BROWS, slot, j * P:(j + 1) * P],
                                 qx[0:BROWS, slot, i, :], start=True, stop=True).then_inc(b_done, 1)

            def values(steps, slot, j):
                pe.wait_ge(exp_done, 4 * steps)
                for i in range(G):
                    last = nc.tensor.matmul(o_bank[32 * i:32 * i + HD + 1, :], vs[:, slot, j, :],
                                            probs[:, j % 2, i, :], start=(j == 0), stop=(j == TB - 1))
                last.then_inc(pv_done, 1)

            def transpose_max():
                nc.tensor.transpose(tr_bank[0:2 * G * TB, 0:P // 2].bitcast(BF16),
                                    negparts[:].rearrange("p a n -> p (a n)"), ident_h[:]).then_inc(negT_done, 1)

            def transpose_o():
                for q in range(TB):
                    last = nc.tensor.transpose(tr_bank[:, q * P:(q + 1) * P], osb[:, q * P:(q + 1) * P], ident[:])
                last.then_inc(oT_done, 1)

            def period(it, v, take=True, split=True):
                g = 4 * it + 1 + v
                first = isinstance(it, int) and it == -1
                mslot, slot = (v + 3) % SLOTS, (v + 1) % SLOTS
                if take:
                    pe.wait_ge(qk_in[mslot], 32 * (it + (3 + v) // 4 + 1))
                if v == 3:
                    pe.wait_ge(rows_in_dram, it + 2)
                pe.wait_ge(shift_in[slot], 16 * (it + (1 + v) // 4 + 1))
                for j in range(TB):
                    for i in range(G):
                        if take:
                            max_scores(None, mslot, j, i, 16 * (g + 2) + 4 * j + i - 3)
                        exp_scores(slot, j, i, None if first and j == 0 and i < 2 else 16 * g + 4 * j + i - 1)
                    if j == 0:
                        if not first:
                            values(4 * g, v % SLOTS, TB - 1)
                    else:
                        if j == 1:
                            pe.wait_ge(vs_done, g + 1)
                            if first:
                                pe.wait_ge(o_clear, 1)
                            else:
                                pe.wait_ge(o_saved, g)
                        values(4 * g + j, slot, j - 1)
                    if j == 1 and split:
                        pe.wait_ge(neg_done, g + 2)
                        transpose_max()
                    if j == 2 and not first:
                        if split:
                            pe.wait_ge(shift_saved, g + 2)
                        else:
                            pe.wait_ge(norm_done, g - 1)
                        transpose_o()

            pe.wait_ge(consts, 3)
            pe.wait_ge(masks_done, 2)
            for g in range(2):
                pe.wait_ge(qk_in[g], 32)
                for j in range(TB):
                    for i in range(G):
                        n = 16 * g + 4 * j + i
                        max_scores(n, g, j, i, n - 3 if n > 3 else None)
                    if g == 1 and j == 1:
                        pe.wait_ge(neg_done, 1)
                        transpose_max()
            pe.wait_ge(shift_saved, 1)
            period(-1, 3)
            with pe.Fori(0, TURNS) as it:
                for v in range(SLOTS):
                    period(it, v)
            period(TURNS, 0)
            period(TURNS, 1, take=False)
            period(TURNS, 2, take=False, split=False)
            values(4 * NG, 3, TB - 1)
            pe.wait_ge(o_saved, NG)
            pe.wait_ge(norm_done, NG - 1)
            transpose_o()

            pe.wait_ge(norm_done, NG)
            for k in range(B * DC):
                for q in range(TB):
                    last = nc.tensor.transpose(bank[k][:, q * P:(q + 1) * P], attn[:, k, q, :], ident[:])
                last.then_inc(aT_done, 1)
            pe.wait_ge(wo_in, 32)
            for k in range(NT // 2):
                b = 2 * k // TB
                if k % 2 == 0:
                    pe.wait_ge(aT_saved, DC * (b + 1))
                for t in range(2 * k, 2 * k + 2):
                    q = t % TB
                    for c in range(DC):
                        last = nc.tensor.matmul(bank[4 + k][:, (t % 2) * D:(t % 2 + 1) * D],
                                                attnT[:, DC * b + c, q * P:(q + 1) * P], wo_sb[:, c, :],
                                                start=(c == 0), stop=(c == DC - 1))
                last.then_inc(wo_done, 1)
            for b in range(B):
                pe.wait_ge(h2_done, b + 1)
                pe.wait_ge(aT_saved, DC * B)
                for c in range(DC):
                    for t in range(TB):
                        last = nc.tensor.transpose(bank[DC * b + c][:, t * P:(t + 1) * P],
                                                   h2[:, TB * b + t, c * P:(c + 1) * P], ident[:])
                    last.then_inc(h2T_done, 1)
                pe.wait_ge(h2T_saved, DC * (b + 1))
                pe.wait_ge(wo_read, NT // 2)
                for t in range(b * TB, (b + 1) * TB):
                    for c in range(DC):
                        last = nc.tensor.matmul(bank[4][:, t * E:(t + 1) * E], h2T[:, c, t * P:(t + 1) * P],
                                                wg_sb[:, c, :], start=(c == 0), stop=(c == DC - 1))
            last.then_inc(logits_done, 1)
            pe.wait_ge(onehot_done, 1)
            nc.tensor.matmul(bank[5][:, 0:NT * E], before[:], onehot[:].rearrange("p t e -> p (t e)"),
                             start=True, stop=False)
            for t in range(NT - 1):
                last = nc.tensor.matmul(
                    bank[5][:, (t + 1) * E:NT * E].rearrange("p (t e) -> p t e", e=E), ones_h[:],
                    onehot[:, t:t + 1, :].to_broadcast([P, NT - 1 - t, E]), start=False, stop=(t == NT - 2))
            last.then_inc(count_done, 1)
            for half in range(2):
                pe.wait_ge(routed_in[half], 16)
                for c in range(DC):
                    for k in range(E // 2):
                        last = nc.tensor.transpose(bank[2 * half + c][:, k * P:(k + 1) * P],
                                                   routed[:, half * E // 2 + k, c * P:(c + 1) * P], ident[:])
                    last.then_inc(rT_done, 1)
            pe.wait_ge(slots_done, 1)
            pe.wait_ge(rT_by_dve, DC)
            pe.wait_ge(rT_by_act, DC)
            for k in range(2):
                pe.wait_ge(w_in[k], 16 * E)

            def hidden(e):
                if e >= 2:
                    pe.wait_ge(gelu_done, 2 * e - 2)
                for k in range(2):
                    for f in range(FT // 2):
                        f0 = (k * FT // 2 + f) * P
                        for c in range(DC):
                            last = nc.tensor.matmul(bank[2 * (e % 2) + k][:, f * P:(f + 1) * P],
                                                    w1_sb[e][:, c, f0:f0 + P],
                                                    routedT[:, c, e * CAP:(e + 1) * CAP],
                                                    start=(c == 0), stop=(c == DC - 1))
                    last.then_inc(h_done, 1)

            def expert_out(e):
                pe.wait_ge(gelu_done, 2 * e + 2)
                if e >= 2:
                    pe.wait_ge(y_saved, e - 1)
                for f in range(FT):
                    last = nc.tensor.matmul(bank[4 + e % 2][:, 0:D], gelu[:, e % 2, f, :], w2_sb[e][:, f, :],
                                            start=(f == 0), stop=(f == FT - 1))
                last.then_inc(y_done, 1)

            hidden(0)
            for e in range(E):
                if e + 1 < E:
                    hidden(e + 1)
                expert_out(e)


def kernel(L0_attn_x, L0_attn_Wq, L0_attn_bq, L0_attn_Wk, L0_attn_bk, L0_attn_Wv, L0_attn_bv, L0_attn_Wo,
           L0_attn_bo, L0_ffn_w_gate, L0_ffn_w1, L0_ffn_w2, L0_c, L0_wmod):
    import numpy as np
    import concourse.bacc as bacc
    from concourse.bass_utils import run_bass_kernel_spmd

    a = {k: np.asarray(v) for k, v in dict(
        x=L0_attn_x, wq=L0_attn_Wq, bq=L0_attn_bq, wk=L0_attn_Wk, bk=L0_attn_bk, wv=L0_attn_Wv,
        bv=L0_attn_bv, wo=L0_attn_Wo, bo=L0_attn_bo, w_gate=L0_ffn_w_gate, w1=L0_ffn_w1, w2=L0_ffn_w2,
        c=L0_c, wmod=L0_wmod).items()}
    B, T, D = a["x"].shape
    HD = 8
    inv = (1.0 / np.float32(10000.0) ** (np.arange(0, HD, 2, dtype=np.float32) / np.float32(HD))).astype(np.float32)
    angle = np.tile((inv[:, None] * np.arange(T, dtype=np.float32)[None, :]).astype(np.float32), (2 * P // HD, 1))
    turn = np.zeros((P, P), np.float32)
    for row in range(P):
        if row % HD < HD // 2:
            turn[row + HD // 2, row] = -1.0
        else:
            turn[row - HD // 2, row] = 1.0
    arrays = {
        "x": a["x"].reshape(B * T, D),
        "c_t": np.ascontiguousarray(a["c"].T),
        "wmod": a["wmod"],
        "wqkv_t": np.ascontiguousarray(np.concatenate([a["wq"], a["wk"], a["wv"]], 0).T),
        "bq": np.ascontiguousarray(a["bq"].reshape(D // P, P).T), "bk": a["bk"], "bv": a["bv"],
        "wo_t": np.ascontiguousarray(a["wo"].T),
        "bo": a["bo"], "w_gate": a["w_gate"], "w1": a["w1"], "w2": a["w2"],
        "rope_cos": np.cos(angle), "rope_sin": np.sin(angle), "rope_rot": turn,
    }
    nc = bacc.Bacc("TRN2", target_bir_lowering=False, num_devices=1)
    args = {n: nc.dram_tensor(n + "_in", v.shape, mybir.dt.from_np(v.dtype), kind="ExternalInput").ap()
            for n, v in arrays.items()}
    out = nc.dram_tensor("out_0", (B * T, D), F32, kind="ExternalOutput").ap()
    adaln_attention_moe_kernel(nc, out=out, **args)
    r = run_bass_kernel_spmd(nc, [{n + "_in": v for n, v in arrays.items()}], core_ids=[0])
    return r.results[0]["out_0"].reshape(B, T, D)
```

```python
from contextlib import ExitStack

import concourse.bass as bass
from concourse import mybir

F32 = mybir.dt.float32
BF16 = mybir.dt.bfloat16
I32 = mybir.dt.int32
ALU = mybir.AluOpType
ACT = mybir.ActivationFunctionType
AX_X = mybir.AxisListType.X

P = 128


def adaln_attention_moe_kernel(nc, x, c_t, wmod, wkqv_t, bkq, bv, wo_t, bo, w_gate, w1, w2,
                               rope_cos, rope_sin, rope_rot, out):
    B = c_t.shape[1]
    S, D = x.shape
    T = S // B
    HD = 8
    HQ = D // HD
    HKV = bv.shape[0] // HD
    G = HQ // HKV
    NG = B * HKV
    E, _, F = w1.shape
    CAP = S // E
    DC = D // P
    NT = S // P
    TB = T // P
    FT = F // P
    CH = 6
    EPS = 1e-5
    GATE_MIN = 0.25
    FAR = 4 * S
    TAGS = 4
    PARTS = 3
    COMBOS = PARTS * PARTS
    ROWS = COMBOS * HD
    SHIFT_ROW = 96
    BROWS = SHIFT_ROW + 2
    SLOTS = 4
    SCALE = float(HD) ** -0.5
    assert (P, T, TB, G, DC, CAP, NG % SLOTS) == (128, 512, 4, 4, 2, P, 0)

    qx_dram = nc.dram_tensor("qx_scratch", (B * HQ, HD * COMBOS, T), BF16, kind="Internal").ap()
    kx_dram = nc.dram_tensor("kx_scratch", (NG, HD * COMBOS, T), BF16, kind="Internal").ap()
    routed_dram = nc.dram_tensor("routed_scratch", (E * CAP, D + TAGS), F32, kind="Internal").ap()
    x1_dram = nc.dram_tensor("x1_scratch", (S, D), F32, kind="Internal").ap()

    with ExitStack() as ctx:
        def sb(name, shape, dt):
            return ctx.enter_context(nc.sbuf_tensor("sb_" + name, shape, dt))

        def sem(name):
            return ctx.enter_context(nc.semaphore(name))

        bank = [ctx.enter_context(nc.psum_tensor(f"bank{i}", [P, 512], F32)) for i in range(8)]
        max_bank, exp_bank, o_bank, tr_bank = bank[0:4], bank[4:6], bank[6], bank[7]

        B_TILES = -(-(HKV + HQ) * HD // P)
        TILE_ROWS = [min(P, (HKV + HQ) * HD - n * P) for n in range(B_TILES)] * B
        Q_ROW = HKV * HD
        PROJ_BANK = [4, 5, 3, 6, 4, 5]
        ROT_BANK = [7, 2, 0, 7, 6, 4]
        ROWS_BANK = [4, 5, 1, 7]
        V_BANK = [6, 5]
        X_BANK = [0, 1, 4, 5]

        CHUNK = DC * F
        wbuf = sb("experts", [P, 2 * E * CHUNK], F32)
        pbuf = sb("probs", [P, 2 * G * T], F32)
        qx = sb("qx", [P, SLOTS, G, T], BF16)
        kx = sb("kx", [P, SLOTS, T], BF16)
        xres = sb("x", [P, NT, D], F32)
        vx = sb("vx", [P, NG, TB * (HD + 1)], F32)
        vs = sb("vs", [P, SLOTS, TB, HD + 1], F32)
        attn = sb("attn", [P, B * DC, TB, P], F32)
        rows = sb("mod_rows", [P, 4, B, D], F32)
        osb = sb("o_sbuf", [P, T], F32)
        wo_sb = sb("wo", [P, DC, D], F32)
        wo_ga = sb("wo_ga", [P, B, DC, D], F32)
        h2_cols = sb("h2_cols", [P, 2, B, DC], F32)
        wg_sb = sb("w_gate", [P, DC, E], F32)
        bo_sb = sb("bo", [P, D], F32)
        bv_sb = sb("bv", [P, HKV * HD], F32)
        bkq_sb = sb("bkq", [P, B_TILES], F32)
        ident = sb("ident", [P, P], F32)
        ident_h = sb("ident_h", [P, P], BF16)
        before = sb("before", [P, P], BF16)
        ones_h = sb("ones_h", [P, P], BF16)
        cT = sb("cT", [P, DC, B], F32)
        c_exp = sb("c_exp", [P, DC, B], F32)
        silu = sb("silu", [P, DC, B], F32)
        mod_scale = sb("mod_scale", [P, DC, B], F32)
        mod_shift = sb("mod_shift", [P, DC, B], F32)
        stats = sb("stats", [P, NT, 6], F32)
        meanvar = sb("meanvar", [P, NT, 2], F32)
        rstd = sb("rstd", [P, NT], F32)
        minus_half = sb("minus_half", [P, NT], F32)
        negmax = sb("negmax", [P, 2, G * TB], F32)
        negparts = sb("negparts", [P, 2, G * TB], BF16)
        shift_rows = sb("shift_rows", [2 * G * TB, 2, P], BF16)
        rden = sb("rden", [P, TB, G], F32)
        expert_no = sb("expert_no", [P, NT, E], F32)
        g_work = sb("g_work", [P, 2, NT, E], F32)
        g_one = sb("g_one", [P, 8, NT], F32)
        onehot = sb("onehot", [P, NT, E], BF16)
        gate_e, is_top = g_work[:, 0], g_work[:, 1]
        one = sb("one", [P, 1], F32)
        ga_bo = sb("ga_bo", [P, B, D], F32)
        zeros_row = sb("zeros_row", [P, D + TAGS], F32)
        token_of = sb("token_of", [P, E], I32)
        slot_i = sb("slot_i", [P, NT], I32)

        at = [6 * CHUNK]

        def early(words):
            at[0] += words
            assert at[0] <= 2 * E * CHUNK
            return wbuf[:, at[0] - words:at[0]]

        wmod_sb = early(DC * CH * D).rearrange("p (c n) -> p c n", c=DC)
        NKQV = (HQ + 2 * HKV) * HD
        wkqv_sb = early(DC * NKQV).rearrange("p (c n) -> p c n", c=DC)
        at[0] = 8 * CHUNK
        b0_words = [[early(T) for _ in range(3)] for _ in range(3)]
        b0_parts = [early(PARTS * T // 2).bitcast(BF16).rearrange("p (a t) -> p a t", a=PARTS)
                    for _ in range(3)]
        assert at[0] >= 9 * CHUNK
        b1_words = [[early(T) for _ in range(3)] for _ in range(3)]
        b1_parts = [early(PARTS * T // 2).bitcast(BF16).rearrange("p (a t) -> p a t", a=PARTS)
                    for _ in range(3)]
        cos_sb, sin_sb = early(T), early(T)
        rot_sb = sb("rot", [P, P], F32)
        tile_words, tile_parts = b0_words + b1_words, b0_parts + b1_parts
        xn = pbuf[:, 0:S * D // P].rearrange("p (t d) -> p t d", t=NT)
        hT = attn[:].rearrange("p a b c -> p (a b c)").rearrange("p (c s) -> p c s", c=DC)
        HALF = S * D // P
        h2_at = 2 * (E - 1) * CHUNK + HALF // B
        h2x = wbuf[:, h2_at:h2_at + NT * (D + TAGS)].rearrange("p (t d) -> p t d", t=NT)
        h2 = h2x[:, :, 0:D]
        attnT = [wbuf[:, h2_at - 2 * T:h2_at - T], wbuf[:, h2_at - T:h2_at],
                 wbuf[:, h2_at + NT * (D + TAGS):h2_at + NT * (D + TAGS) + T], pbuf[:, 2 * G * T - T:]]
        qx_words = qx[:].rearrange("p a b c -> p (a b c)").bitcast(F32)
        h2T = qx_words[:, 0:HALF].rearrange("p (b c s) -> p b c s", b=B, c=DC)
        gelu = qx_words[:, HALF:2 * HALF].rearrange("p (a f s) -> p a f s", a=2, f=FT)
        gain, share = (kx[:].rearrange("p a b -> p (a b)").bitcast(F32)[:, k * D:(k + 1) * D] for k in range(2))
        x1_slots = vx[:].rearrange("p g c -> p (g c)")[:, 0:2 * D].rearrange("p (a d) -> p a d", a=2)
        y_slots = osb[:, :].rearrange("p (a d) -> p a d", a=2)
        routed = pbuf[:, 0:E * (D + TAGS)].rearrange("p (e d) -> p e d", e=E)
        routedT = hT
        probs = pbuf[:].rearrange("p (a i t) -> p a i t", a=2, i=G)
        w1_sb = [wbuf[:, 2 * e * CHUNK:(2 * e + 1) * CHUNK].rearrange("p (c f) -> p c f", c=DC)
                 for e in range(E)]
        w2_sb = [wbuf[:, (2 * e + 1) * CHUNK:(2 * e + 2) * CHUNK].rearrange("p (t d) -> p t d", t=FT)
                 for e in range(E)]
        w1_v = w1.rearrange("e (c p) f -> e p c f", p=P)
        w2_v = w2.rearrange("e (t p) d -> e p t d", p=P)
        x_v = x.rearrange("(t p) d -> p t d", p=P)
        out_v = out.rearrange("(t p) d -> p t d", p=P)


        def q_rows(b, lo, hi):
            return qx_dram[b * HQ + lo:b * HQ + hi].rearrange("h (d r a) t -> (h d) r (a t)", r=PARTS, a=PARTS)

        def k_rows(b):
            return kx_dram[b * HKV:(b + 1) * HKV].rearrange("h (d a r) t -> (h d) a r t", r=PARTS, a=PARTS)

        def copies(ap):
            return ap.unsqueeze(1).to_broadcast([ap.shape[0], PARTS, ap.shape[1]])

        def q_parts(b, lo, hi):
            row = Q_ROW + lo * HD
            tile, row = B_TILES * b + row // P, row % P
            return copies(tile_parts[tile].rearrange("p a t -> p (a t)")[row:row + (hi - lo) * HD])

        Q_ENDS = [((n + 1) * P - Q_ROW) // HD for n in range(B_TILES - 1)] + [HQ]

        c_in, wmod_in, wmod_rest_in, wkqv_in, bias_in, rope_in, wo_in = map(
            sem, ("c_in", "wmod_in", "wmod_rest_in", "wkqv_in", "bias_in", "rope_in", "wo_in"))
        x_in = [sem(f"x_in{b}") for b in range(B)]
        consts = sem("consts")
        ident_done, masks_done, rows_clear = sem("ident_done"), sem("masks_done"), sem("rows_clear")
        routed_zero, zeros_done, o_clear, row_one = map(
            sem, ("routed_zero", "zeros_done", "o_clear", "row_one"))
        c_exp_done, silu_done, mod_done, mod_saved = map(
            sem, ("c_exp_done", "silu_done", "mod_done", "mod_saved"))
        stats_done = sem("stats_done")
        var_done, rstd_done, xn_done = map(sem, ("var_done", "rstd_done", "xn_done"))
        xT_done, hT_by_dve, hT_by_act = map(sem, ("xT_done", "hT_by_dve", "hT_by_act"))
        proj_done, v_proj_done, biased, rotated = map(
            sem, ("proj_done", "v_proj_done", "biased", "rotated"))
        rot_read, rot_copied, vx_done = map(sem, ("rot_read", "rot_copied", "vx_done"))
        split_by_dve, split_by_pool = sem("split_by_dve"), sem("split_by_pool")
        kx_written, qx_written = sem("kx_written"), sem("qx_written")
        kx_by_pool, qx_by_pool = sem("kx_by_pool"), sem("qx_by_pool")
        rows_in_dram, q0_written = sem("rows_in_dram"), sem("q0_written")
        q1_written = sem("q1_written")
        vo_bias_in = sem("vo_bias_in")
        rows_done, rows_copied = sem("rows_done"), sem("rows_copied")
        xg_done = sem("xg_done")
        dve_step, pool_step = sem("dve_step"), sem("pool_step")
        qk_in = [sem(f"qk_in{u}") for u in range(SLOTS)]
        shift_in = [sem(f"shift_in{u}") for u in range(SLOTS)]
        a_done, max_done, b_done, exp_done, pv_done = map(
            sem, ("a_done", "max_done", "b_done", "exp_done", "pv_done"))
        neg_hi, neg_done, negT_done, shift_saved = map(
            sem, ("neg_hi", "neg_done", "negT_done", "shift_saved"))
        vs_done, o_saved, oT_done, rden_done, norm_done = map(
            sem, ("vs_done", "o_saved", "oT_done", "rden_done", "norm_done"))
        h2_norm, rT_saved, gate_tagged = map(
            sem, ("h2_norm", "rT_saved", "gate_tagged"))
        w_in = [sem(f"w_in{k}") for k in range(2)]
        aT_done, aT_by_dve, aT_by_act, wo_done = map(
            sem, ("aT_done", "aT_by_dve", "aT_by_act", "wo_done"))
        var2_done, rstd2_done, h2_done, h2T_done, h2T_by_dve, h2T_by_act = map(
            sem, ("var2_done", "rstd2_done", "h2_done", "h2T_done", "h2T_by_dve", "h2T_by_act"))
        logits_done, gate_sub, gate_exp, onehot_done, count_done = map(
            sem, ("logits_done", "gate_sub", "gate_exp", "onehot_done", "count_done"))
        slots_done, scattered, rT_done = map(sem, ("slots_done", "scattered", "rT_done"))
        routed_in = [sem(f"routed_in{k}") for k in range(E // 2)]
        w7_in, tags_done = sem("w7_in"), sem("tags_done")
        h_done, gelu_done, y_done, y_saved = map(sem, ("h_done", "gelu_done", "y_done", "y_saved"))
        x1_done, x1_written, x1_out = map(sem, ("x1_done", "x1_written", "x1_out"))
        wo_scaled, cols_done, cols_saved = map(sem, ("wo_scaled", "cols_done", "cols_saved"))
        exps_taken, place_taken = sem("exps_taken"), sem("place_taken")
        token_done, slots_clear, gain_done, y_scaled = map(
            sem, ("token_done", "slots_clear", "gain_done", "y_scaled"))
        x1_in = [sem(f"x1_in{k}") for k in range(2)]
        y_out = [sem(f"y_out{k}") for k in range(2)]

        block = ctx.enter_context(nc.Block())

        TURNS = (NG - 4) // SLOTS


        @block.sync
        def _(sp):
            sp.dma_start(cT[:], c_t.rearrange("(c p) b -> p c b", p=P)).then_inc(c_in, 16)
            sp.dma_start(xres[:, 0:TB, :], x_v[:, 0:TB, :]).then_inc(x_in[0], 16)
            wmod_v = wmod.rearrange("(c p) n -> p c n", p=P)
            sp.dma_start(wmod_sb[:, :, 0:2 * D], wmod_v[:, :, 0:2 * D]).then_inc(wmod_in, 16)
            sp.dma_start(wkqv_sb, wkqv_t.rearrange("(c p) n -> p c n", p=P)).then_inc(wkqv_in, 16)
            for n in range(B_TILES):
                sp.dma_start(bkq_sb[0:TILE_ROWS[n], n:n + 1],
                             bkq[n * P:n * P + TILE_ROWS[n]].rearrange("(p a) -> p a", a=1)).then_inc(bias_in, 16)
            sp.dma_start(rot_sb[:], rope_rot).then_inc(rope_in, 16)
            sp.dma_start(cos_sb, rope_cos).then_inc(rope_in, 16)
            sp.dma_start(sin_sb, rope_sin).then_inc(rope_in, 16)
            sp.dma_start(xres[:, TB:, :], x_v[:, TB:, :]).then_inc(x_in[1], 16)
            sp.dma_start(wmod_sb[:, :, 2 * D:], wmod_v[:, :, 2 * D:]).then_inc(wmod_rest_in, 16)
            sp.dma_start(bv_sb[:], bv.rearrange("(a n) -> a n", a=1).to_broadcast([P, HKV * HD])).then_inc(vo_bias_in, 16)
            sp.dma_start(bo_sb[:], bo.rearrange("(a n) -> a n", a=1).to_broadcast([P, D])).then_inc(vo_bias_in, 16)
            sp.dma_start(wo_sb[:], wo_t.rearrange("(c p) n -> p c n", p=P)).then_inc(wo_in, 16)
            sp.dma_start(wg_sb[:], w_gate.rearrange("(c p) n -> p c n", p=P)).then_inc(wo_in, 16)

            sp.wait_ge(consts, 2)
            sp.wait_ge(rows_clear, 1)
            for a in range(PARTS):
                sp.wait_ge(split_by_dve, a + 1)
                sp.dma_start(k_rows(0)[:, a], copies(tile_parts[0][0:Q_ROW, a, :])).then_inc(kx_written, 16)
            sp.dma_start(q_rows(0, 0, G), q_parts(0, 0, G)).then_inc(q0_written, 16)
            sp.wait_ge(kx_written, 16 * PARTS)
            sp.dma_start(kx[0:ROWS, 0, :], kx_dram[0]).then_inc(qk_in[0], 16)
            sp.wait_ge(q0_written, 16)
            sp.dma_start(qx[0:ROWS, 0, :, :], qx_dram[0:G].rearrange("i r t -> r i t")).then_inc(qk_in[0], 16)
            sp.dma_start(q_rows(0, G, Q_ENDS[0]), q_parts(0, G, Q_ENDS[0])).then_inc(q1_written, 16)
            sp.wait_ge(split_by_dve, 2 * PARTS)
            sp.dma_start(q_rows(0, Q_ENDS[0], Q_ENDS[1]), q_parts(0, Q_ENDS[0], Q_ENDS[1])).then_inc(qx_written, 16)

            def load_group(g, u):
                sp.dma_start(kx[0:ROWS, u, :], kx_dram[g]).then_inc(qk_in[u], 16)
                sp.dma_start(qx[0:ROWS, u, :, :],
                             qx_dram[bass.ds(g * G, G)].rearrange("i r t -> r i t")).then_inc(qk_in[u], 16)

            def load_shift(buf, u):
                sp.dma_start(qx[SHIFT_ROW:BROWS, u, :, :].rearrange("a i (q t) -> a (i q) t", q=TB),
                             shift_rows[:, buf, :]).then_inc(shift_in[u], 16)

            sp.wait_ge(q1_written, 16)
            load_group(1, 1)
            sp.wait_ge(qx_written, 16)
            load_group(2, 2)
            sp.wait_ge(shift_saved, 1)
            load_shift(0, 0)

            def period(it, v, load=True, shift=True, expert=True):
                g = 4 * it + 1 + v
                if load:
                    if not isinstance(it, int):
                        sp.wait_ge(b_done, 16 * g)
                    load_group(g + 3, v)
                if shift:
                    sp.wait_ge(shift_saved, g + 2)
                    load_shift((v + 2) % 2, (v + 2) % SLOTS)
                if not expert:
                    return
                if v % 2:
                    sp.dma_start(wbuf[:, bass.ds(g * CHUNK, CHUNK)].rearrange("p (c f) -> p c f", c=DC),
                                 w1_v[2 * it + (1 + v) // 2]).then_inc(w_in[0], 16)
                else:
                    sp.dma_start(wbuf[:, bass.ds(g * CHUNK, CHUNK)].rearrange("p (t d) -> p t d", t=FT),
                                 w2_v[2 * it + v // 2]).then_inc(w_in[1], 16)

            period(-1, 3)
            with sp.Fori(0, TURNS) as it:
                for v in range(SLOTS):
                    period(it, v)
            period(TURNS, 0, load=False)
            period(TURNS, 1, load=False, expert=False)

            x1_v = x1_dram.rearrange("(t p) d -> p t d", p=P)
            for b in range(B):
                ts = slice(b * TB, (b + 1) * TB)
                sp.wait_ge(x1_done, TB // 2 * (b + 1))
                sp.dma_start(x1_v[:, ts, :], xres[:, ts, :]).then_inc(x1_written, 16)
                sp.dma_start(out_v[:, ts, :], xres[:, ts, :]).then_inc(x1_out, 16)

            sp.wait_ge(scattered, 16 * NT)
            for pair in range(E // 2):
                es = slice(2 * pair, 2 * pair + 2)
                sp.dma_start(routed[:, es, :],
                             routed_dram.rearrange("(e p) d -> p e d", p=P)[:, es, :]).then_inc(routed_in[pair], 16)
            sp.dma_start(w1_sb[E - 1], w1_v[E - 1]).then_inc(w7_in, 16)
            sp.dma_start(w2_sb[E - 1], w2_v[E - 1]).then_inc(w7_in, 16)
            sp.wait_ge(x1_out, 16 * B)

        @block.gpsimd
        def _(pool):
            step = [0]

            def link(ins):
                step[0] += 1
                ins.then_inc(pool_step, 1)
                pool.wait_ge(pool_step, step[0])

            link(nc.gpsimd.memset(ident[:], 0.0))
            nc.gpsimd.affine_select(out=ident[:], in_=ident[:], compare_op=ALU.not_equal, fill=1.0,
                                    base=0, pattern=[[-1, P]], channel_multiplier=1).then_inc(ident_done, 1)
            link(nc.gpsimd.memset(minus_half[:], -0.5))
            nc.gpsimd.memset(qx[64:SHIFT_ROW].rearrange("p a b c -> p (a b c)").bitcast(F32),
                             0.0).then_inc(rows_clear, 1)
            pool.wait_ge(rows_clear, 1)
            for b in range(B):
                ts = slice(b * TB, (b + 1) * TB)
                pool.wait_ge(var_done, b + 1)
                nc.gpsimd.tensor_tensor(rstd[:, ts], rstd[:, ts], minus_half[:, ts],
                                        ALU.pow).then_inc(rstd_done, 1)
                pool.wait_ge(rstd_done, b + 1)
            pool.wait_ge(ident_done, 1)
            link(nc.gpsimd.tensor_copy(ident_h[:], ident[:]))
            link(nc.gpsimd.memset(ones_h[:], 1.0))
            nc.gpsimd.affine_select(out=before[:], in_=ones_h[:], compare_op=ALU.is_gt, fill=0.0,
                                    base=0, pattern=[[1, P]], channel_multiplier=-1).then_inc(masks_done, 1)
            pool.wait_ge(masks_done, 1)
            nc.gpsimd.iota(expert_no[:], pattern=[[0, NT], [-1, E]], base=E, channel_multiplier=0,
                           allow_small_or_imprecise_dtypes=True).then_inc(masks_done, 1)
            pool.wait_ge(masks_done, 2)

            pool.wait_ge(rope_in, 48)
            for n in range(2, 6):
                r = TILE_ROWS[n]
                biased_w, turned_w, sum_w = (w[0:r, :] for w in tile_words[n])
                part = tile_parts[n]
                pool.wait_ge(rot_copied, n - 1)
                link(nc.gpsimd.tensor_tensor(turned_w, turned_w, sin_sb[0:r, :], ALU.mult))
                link(nc.gpsimd.tensor_tensor(sum_w, biased_w, cos_sb[0:r, :], ALU.mult))
                link(nc.gpsimd.tensor_tensor(sum_w, sum_w, turned_w, ALU.add))
                link(nc.gpsimd.tensor_copy(part[0:r, 0, :], sum_w))
                link(nc.gpsimd.tensor_tensor(sum_w, sum_w, part[0:r, 0, :], ALU.subtract))
                link(nc.gpsimd.tensor_copy(part[0:r, 1, :], sum_w))
                link(nc.gpsimd.tensor_tensor(part[0:r, 2, :], sum_w, part[0:r, 1, :], ALU.subtract))
                if n == 3:
                    for a in range(PARTS):
                        pool.dma_start(k_rows(1)[:, a], copies(part[0:Q_ROW, a, :])).then_inc(kx_by_pool, 16)
                b, lo, hi = n // B_TILES, (0 if n == 3 else Q_ENDS[n % B_TILES - 1]), Q_ENDS[n % B_TILES]
                pool.dma_start(q_rows(b, lo, hi), q_parts(b, lo, hi)).then_inc(qx_by_pool, 16)
                if n != 3:
                    if n > 3:
                        pool.wait_ge(kx_by_pool, 16 * PARTS)
                    pool.wait_ge(qx_by_pool, 16 * (n - 1))
                    pool.sem_inc(rows_in_dram, 1)
            pool.sem_inc(rows_in_dram, 1)

            pool.wait_ge(rows_copied, 4)
            pool.wait_ge(vo_bias_in, 32)
            sign = ga_bo[:].rearrange("p b d -> p (b d)")
            for m in (0, 3):
                gate = rows[:, m].rearrange("p b d -> p (b d)")
                link(nc.gpsimd.tensor_scalar(sign, gate, 0.0, 2.0, ALU.is_ge, ALU.mult))
                link(nc.gpsimd.tensor_scalar(sign, sign, -1.0, None, ALU.add))
                link(nc.gpsimd.tensor_tensor(gate, gate, sign, ALU.mult))
                link(nc.gpsimd.tensor_scalar(gate, gate, GATE_MIN, None, ALU.max))
                link(nc.gpsimd.tensor_tensor(gate, gate, sign, ALU.mult))
            pool.wait_ge(wo_in, 32)
            for b in range(B):
                nc.gpsimd.tensor_tensor(wo_ga[:, b], wo_sb[:], rows[:, 0, b].unsqueeze(1).to_broadcast([P, DC, D]),
                                        ALU.mult).then_inc(wo_scaled, 1)
                pool.wait_ge(wo_scaled, b + 1)
            for b in range(B):
                link(nc.gpsimd.tensor_tensor(ga_bo[:, b], rows[:, 0, b], bo_sb[:], ALU.mult))
                for t in range(b * TB, (b + 1) * TB):
                    nc.gpsimd.tensor_tensor(xres[:, t], xres[:, t], ga_bo[:, b], ALU.add).then_inc(xg_done, 1)
                    pool.wait_ge(xg_done, t + 1)
            nc.gpsimd.memset(zeros_row[:], 0.0).then_inc(zeros_done, 1)
            pool.wait_ge(zeros_done, 1)
            link(nc.gpsimd.memset(h2x[:, :, D:], 0.0))
            nc.gpsimd.iota(h2x[:, :, D:D + 1], pattern=[[-P, NT], [0, 1]], base=FAR, channel_multiplier=-1,
                           allow_small_or_imprecise_dtypes=True).then_inc(tags_done, 1)
            pool.wait_ge(tags_done, 1)
            pool.dma_start(routed_dram.rearrange("(p e) d -> p e d", p=P),
                           zeros_row[:].unsqueeze(1).to_broadcast([P, E, D + TAGS])).then_inc(routed_zero, 16)

            for b in range(B):
                ts = slice(b * TB, (b + 1) * TB)
                pool.wait_ge(var2_done, b + 1)
                nc.gpsimd.tensor_tensor(rstd[:, ts], rstd[:, ts], minus_half[:, ts],
                                        ALU.pow).then_inc(rstd2_done, 1)
                pool.wait_ge(rstd2_done, b + 1)
            pool.wait_ge(routed_zero, 16)
            for b in range(B):
                pool.wait_ge(h2_done, b + 1)
                pool.wait_ge(slots_done, b + 1)
                for t in range(b * TB, (b + 1) * TB):
                    pool.indirect_dma_start(
                        routed_dram[:, :], bass.IndirectOffsetOnAxis(ap=slot_i[:, t:t + 1], axis=0),
                        h2x[:, t, :], None, bounds_check=E * CAP - 1, oob_is_err=False).then_inc(scattered, 16)

            pool.wait_ge(vs_done, NG)
            nc.gpsimd.memset(x1_slots, 0.0).then_inc(slots_clear, 1)
            pool.wait_ge(slots_clear, 1)
            pool.wait_ge(x1_written, 16 * B)

            def gather(e):
                pool.wait_ge(token_done, e // 2 + 1)
                if e >= 2:
                    pool.wait_ge(y_scaled, e - 1)
                pool.indirect_dma_start(
                    x1_slots[:, e % 2, :], None, x1_dram[:, :],
                    bass.IndirectOffsetOnAxis(ap=token_of[:, e:e + 1], axis=0),
                    bounds_check=S - 1, oob_is_err=False).then_inc(x1_in[e % 2], 16)

            gather(0)
            gather(1)
            pool.wait_ge(x1_out, 16 * B)
            for e in range(E):
                pool.wait_ge(y_scaled, e + 1)
                pool.indirect_dma_start(
                    out[:, :], bass.IndirectOffsetOnAxis(ap=token_of[:, e:e + 1], axis=0),
                    y_slots[:, e % 2, :], None, bounds_check=S - 1, oob_is_err=False).then_inc(y_out[e % 2], 16)
                if e + 2 < E:
                    gather(e + 2)
            for k in range(2):
                pool.wait_ge(y_out[k], 16 * (E // 2))

        @block.scalar
        def _(act):
            act.wait_ge(c_in, 16)
            nc.scalar.activation(c_exp[:], cT[:], ACT.Exp, scale=-1.0).then_inc(c_exp_done, 1)

            def modulate(b):
                act.wait_ge(mod_saved, 2)
                act.wait_ge(xT_done, 2 * b + 2)
                nc.scalar.activation(hT[:, 1, b * T:(b + 1) * T], bank[X_BANK[2 * b + 1]][:], ACT.Identity,
                                     bias=mod_shift[:, 1, b:b + 1],
                                     scale=mod_scale[:, 1, b:b + 1]).then_inc(hT_by_act, 1)

            def add_bias(n):
                r = TILE_ROWS[n]
                act.wait_ge(proj_done, n + 1)
                if n == 0:
                    act.wait_ge(bias_in, 16 * B_TILES)
                nc.scalar.activation(tile_words[n][0][0:r, :], bank[PROJ_BANK[n]][0:r, :], ACT.Identity,
                                     bias=bkq_sb[0:r, n % B_TILES:n % B_TILES + 1]).then_inc(biased, 1)

            def copy_rotated(n):
                r = TILE_ROWS[n]
                act.wait_ge(rotated, n + 1)
                nc.scalar.copy(tile_words[n][1][0:r, :], bank[ROT_BANK[n]][0:r, :]).then_inc(rot_copied, 1)

            def copy_rows(k):
                b, half = k // 2, k % 2
                act.wait_ge(rows_done, k + 1)
                src = bank[ROWS_BANK[k]][:].rearrange("p (m d) -> p m d", m=2)
                dst = rows[:, 2 * half:2 * half + 2, b, :]
                if half == 0:
                    nc.scalar.copy(dst, src).then_inc(rows_copied, 1)
                else:
                    nc.scalar.activation(dst[:, 0], src[:, 0], ACT.Identity, bias=one[:]).then_inc(row_one, 1)
                    nc.scalar.copy(dst[:, 1], src[:, 1]).then_inc(rows_copied, 1)

            modulate(0)
            for n in range(3):
                add_bias(n)
            copy_rows(0)
            copy_rows(1)
            copy_rotated(2)
            copy_rows(2)
            copy_rows(3)
            modulate(1)
            add_bias(3)
            add_bias(4)
            copy_rotated(3)
            add_bias(5)
            copy_rotated(4)
            copy_rotated(5)

            def period(it, v):
                g = 4 * it + 1 + v
                for j in range(TB):
                    for i in range(G):
                        act.wait_ge(b_done, 16 * g + 4 * j + i + 1)
                        if i == 0 and not (v == 3 and isinstance(it, int) and j < 2):
                            act.wait_ge(pv_done, 4 * g + j - 1)
                        nc.scalar.activation(probs[:, j % 2, i, :], exp_bank[i % 2][:], ACT.Exp,
                                             scale=SCALE).then_inc(exp_done, 1)
                        if (j, i) == (0, 1) and not (v == 3 and isinstance(it, int)):
                            save_o(4 * g)

            def save_o(steps):
                act.wait_ge(pv_done, steps)
                nc.scalar.copy(osb[:], o_bank[:]).then_inc(o_saved, 1)

            period(-1, 3)
            with act.Fori(0, TURNS) as it:
                for v in range(SLOTS):
                    period(it, v)
            for v in range(3):
                period(TURNS, v)
            save_o(4 * NG)

            def gate_exps(b):
                act.wait_ge(gate_sub, b + 1)
                e_b = gate_e[:, b * TB:(b + 1) * TB]
                nc.scalar.activation(e_b, e_b, ACT.Exp).then_inc(gate_exp, 1)

            gate_exps(0)
            act.wait_ge(aT_done, 4)
            nc.scalar.copy(attnT[3], bank[0][:]).then_inc(aT_by_act, 1)
            for c in range(DC):
                act.wait_ge(h2T_done, DC + c + 1)
                nc.scalar.activation(h2T[:, 1, c, :], bank[c][:], ACT.Identity, bias=h2_cols[:, 0, 1, c:c + 1],
                                     scale=h2_cols[:, 1, 1, c:c + 1]).then_inc(h2T_by_act, 1)
            gate_exps(1)
            for e in range(E):
                for k in range(2):
                    act.wait_ge(h_done, 2 * e + k + 1)
                    if e >= 2 and k == 0:
                        act.wait_ge(y_done, e - 1)
                    nc.scalar.activation(
                        gelu[:, e % 2, k * FT // 2:(k + 1) * FT // 2, :].rearrange("p f s -> p (f s)"),
                        bank[2 * (e % 2) + k][:], ACT.Gelu_apprx_tanh).then_inc(gelu_done, 1)

        @block.vector
        def _(dve):
            step = [0]

            def link(ins):
                step[0] += 1
                ins.then_inc(dve_step, 1)
                dve.wait_ge(dve_step, step[0])

            nc.vector.memset(one[:], 1.0).then_inc(consts, 1)
            link(nc.vector.memset(kx[64:SHIFT_ROW].rearrange("p a b -> p (a b)").bitcast(F32), 0.0))
            nc.vector.memset(kx[SHIFT_ROW:P].rearrange("p a b -> p (a b)"), 1.0).then_inc(consts, 1)
            nc.vector.memset(vx[:], 1.0).then_inc(consts, 1)
            dve.wait_ge(consts, 3)
            dve.wait_ge(c_exp_done, 1)
            link(nc.vector.tensor_scalar_add(c_exp[:], c_exp[:], 1.0))
            link(nc.vector.reciprocal(c_exp[:], c_exp[:]))
            nc.vector.tensor_tensor(silu[:], cT[:], c_exp[:], ALU.mult).then_inc(silu_done, 1)

            def row_stats(tiles):
                for t in tiles:
                    nc.vector.bn_stats(stats[:, t, :], xres[:, t, :]).then_inc(stats_done, 1)

            def norm_stats(b, done, round, taken=0):
                row_stats(range(b * TB + taken, (b + 1) * TB))
                dve.wait_ge(stats_done, TB * (B * round + b + 1))
                for t in range(b * TB, (b + 1) * TB):
                    ins = nc.vector.bn_aggr(meanvar[:, t, :], stats[:, t, :])
                link(ins)
                ts = slice(b * TB, (b + 1) * TB)
                nc.vector.tensor_scalar(rstd[:, ts], meanvar[:, ts, 1], EPS, None, ALU.add).then_inc(done, 1)

            def normalise(b, dst, ready, done):
                dve.wait_ge(ready, b + 1)
                for t in range(b * TB, (b + 1) * TB):
                    nc.vector.tensor_scalar(dst[:, t, :], xres[:, t, :], meanvar[:, t, 0:1], rstd[:, t:t + 1],
                                            ALU.subtract, ALU.mult).then_inc(done, 1)

            def modulate(b):
                dve.wait_ge(xT_done, 2 * b + 1)
                nc.vector.tensor_scalar(hT[:, 0, b * T:(b + 1) * T], bank[X_BANK[2 * b]][:],
                                        mod_scale[:, 0, b:b + 1], mod_shift[:, 0, b:b + 1], ALU.mult, ALU.add).then_inc(hT_by_dve, 1)

            dve.wait_ge(x_in[0], 16)
            norm_stats(0, var_done, 0)
            normalise(0, xn, rstd_done, xn_done)
            dve.wait_ge(mod_done, 1)
            mod_ps = bank[7][:, 0:2 * DC * B].rearrange("p (m c b) -> p m c b", m=2, c=DC)
            nc.vector.tensor_copy(mod_shift[:], mod_ps[:, 0]).then_inc(mod_saved, 1)
            nc.vector.tensor_scalar_add(mod_scale[:], mod_ps[:, 1], 1.0).then_inc(mod_saved, 1)
            dve.wait_ge(mod_saved, 2)
            modulate(0)
            dve.wait_ge(x_in[1], 16)
            norm_stats(1, var_done, 0)

            def rope_split(n):
                r = TILE_ROWS[n]
                biased_w, turned_w, sum_w = (w[0:r, :] for w in tile_words[n])
                part = tile_parts[n]
                dve.wait_ge(biased, n + 1)
                link(nc.vector.tensor_tensor(sum_w, biased_w, cos_sb[0:r, :], ALU.mult))
                dve.wait_ge(rotated, n + 1)
                rotated_ps = nc.vector.tensor_tensor(turned_w, bank[ROT_BANK[n]][0:r, :], sin_sb[0:r, :], ALU.mult)
                rotated_ps.then_inc(rot_read, 1)
                dve.wait_ge(rot_read, n + 1)
                link(nc.vector.tensor_tensor(sum_w, sum_w, turned_w, ALU.add))
                nc.vector.tensor_copy(part[0:r, 0, :], sum_w).then_inc(split_by_dve, 1)
                dve.wait_ge(split_by_dve, PARTS * n + 1)
                link(nc.vector.tensor_tensor(sum_w, sum_w, part[0:r, 0, :], ALU.subtract))
                nc.vector.tensor_copy(part[0:r, 1, :], sum_w).then_inc(split_by_dve, 1)
                dve.wait_ge(split_by_dve, PARTS * n + 2)
                nc.vector.tensor_tensor(part[0:r, 2, :], sum_w, part[0:r, 1, :],
                                        ALU.subtract).then_inc(split_by_dve, 1)

            def save_v(b):
                dve.wait_ge(v_proj_done, b + 1)
                dve.wait_ge(vo_bias_in, 32)
                dst = vx[:, b * HKV:(b + 1) * HKV, :].rearrange("p h (k c) -> p h k c", c=HD + 1)[:, :, :, 0:HD]
                for k in range(TB):
                    nc.vector.tensor_tensor(
                        dst[:, :, k, :],
                        bank[V_BANK[b]][:, k * HKV * HD:(k + 1) * HKV * HD].rearrange("p (h d) -> p h d", h=HKV),
                        bv_sb[:].rearrange("p (h d) -> p h d", h=HKV), ALU.add).then_inc(vx_done, 1)

            dve.wait_ge(rope_in, 48)
            rope_split(0)
            rope_split(1)
            normalise(1, xn, rstd_done, xn_done)
            save_v(0)
            modulate(1)

            def take_max(count, buf, col, i):
                dve.wait_ge(a_done, count)
                nc.vector.tensor_reduce(negmax[:, buf, col:col + 1], max_bank[i][:], AX_X, ALU.max,
                                        negate=True).then_inc(max_done, 1)

            def split_max(g, buf):
                dve.wait_ge(max_done, 16 * (g + 1))
                if not (isinstance(g, int) and g == 0):
                    dve.wait_ge(negT_done, g)
                nc.vector.tensor_copy(negparts[:, 0, :], negmax[:, buf, :]).then_inc(neg_hi, 1)
                dve.wait_ge(neg_hi, g + 1)
                nc.vector.tensor_tensor(negparts[:, 1, :], negmax[:, buf, :], negparts[:, 0, :],
                                        ALU.subtract).then_inc(neg_done, 1)

            def save_shift(g, buf, slot, turn):
                dve.wait_ge(negT_done, g + 1)
                if slot is not None:
                    dve.wait_ge(shift_in[slot], 16 * turn)
                nc.vector.tensor_copy(shift_rows[:, buf, :],
                                      tr_bank[0:2 * G * TB, 0:P // 2].bitcast(BF16)).then_inc(shift_saved, 1)

            def copy_v(g, u):
                nc.vector.tensor_copy(vs[:, u].rearrange("p k c -> p (k c)"), vx[:, g, :]).then_inc(vs_done, 1)

            def norm(g, it, u):
                dve.wait_ge(oT_done, g + 1)
                o = tr_bank[:].rearrange("p (q i c) -> p q i c", q=TB, i=G)
                nc.vector.reciprocal(rden[:], o[:, :, :, HD]).then_inc(rden_done, 1)
                dve.wait_ge(rden_done, g + 1)
                nc.vector.tensor_tensor(
                    attn[:, it, :, u * G * HD:(u + 1) * G * HD].rearrange("p q (i d) -> p q i d", i=G),
                    o[:, :, :, 0:HD], rden[:].unsqueeze(3).to_broadcast([P, TB, G, HD]),
                    ALU.mult).then_inc(norm_done, 1)

            def period(it, v, second=True, third=True):
                g = 4 * it + 1 + v
                first = isinstance(it, int) and it == -1
                for j in range(TB):
                    ahead, jj, take = 1 + j // 2, (j + 2) % TB, (second, third)[j // 2]
                    if j == 2 and take:
                        dve.wait_ge(neg_done, g + 1)
                    for i in range(G):
                        if take:
                            take_max(16 * (g + ahead) + 4 * jj + i + 1, (v + 1 + ahead) % 2, 4 * i + jj, i)
                        if (j, i) == (1, 2) and not first:
                            norm(g - 1, it, v)
                        if (j, i) == (1, 3) and second:
                            split_max(g + 1, (v + 2) % 2)
                        if (j, i) == (2, 0) and second:
                            save_shift(g + 1, (v + 2) % 2, None if first else v, it + 1)
                        if (j, i) == (3, 2) and second:
                            copy_v(g + 1, (v + 2) % SLOTS)

            for j in range(TB):
                for i in range(G):
                    take_max(4 * j + i + 1, 0, 4 * i + j, i)
            split_max(0, 0)
            copy_v(0, 0)
            save_shift(0, 0, None, 0)
            for j in range(TB // 2):
                for i in range(G):
                    take_max(16 + 4 * j + i + 1, 1, 4 * i + j, i)
                    if (j, i) == (1, 1):
                        save_v(1)
            dve.wait_ge(rot_copied, 3)
            nc.vector.memset(o_bank[:], 0.0).then_inc(o_clear, 1)
            period(-1, 3)
            with dve.Fori(0, TURNS) as it:
                for v in range(SLOTS):
                    period(it, v)
            period(TURNS, 0)
            period(TURNS, 1, third=False)

            def residual(k, from_bank):
                b = 2 * k // TB
                dve.wait_ge(wo_done, k + 1)
                if k == 0:
                    dve.wait_ge(xg_done, NT)
                y = bank[from_bank][:].rearrange("p (t d) -> p t d", t=2)
                ts = slice(2 * k, 2 * k + 2)
                nc.vector.tensor_tensor(xres[:, ts, :], xres[:, ts, :], y, ALU.add).then_inc(x1_done, 1)
                dve.wait_ge(x1_done, k + 1)

            def modulate_rows(b):
                ts = slice(b * TB, (b + 1) * TB)
                dve.wait_ge(h2T_done, DC * (b + 1))
                link(nc.vector.tensor_tensor(h2[:, ts], h2[:, ts],
                                             rows[:, 2, b].unsqueeze(1).to_broadcast([P, TB, D]), ALU.mult))
                nc.vector.tensor_tensor(h2[:, ts], h2[:, ts],
                                        rows[:, 1, b].unsqueeze(1).to_broadcast([P, TB, D]),
                                        ALU.add).then_inc(h2_done, 1)

            def over_e(ap):
                return ap.unsqueeze(2).to_broadcast([P, TB, E])

            def of_batch(b):
                ts = slice(b * TB, (b + 1) * TB)
                return [gate_e[:, ts], is_top[:, ts]] + [g_one[:, k, ts] for k in range(7)]

            def start_gates(b):
                gates, tops, top = of_batch(b)[0:3]
                logits = bank[2][:, 0:TB * E].rearrange("p (t e) -> p t e", e=E)
                dve.wait_ge(logits_done, b + 1)
                link(nc.vector.tensor_reduce(top, logits, AX_X, ALU.max))
                nc.vector.tensor_tensor(gates, logits, over_e(top), ALU.subtract).then_inc(gate_sub, 1)

            def choose(b):
                gates, tops, top, total, best, place, number, over, gate = of_batch(b)
                dve.wait_ge(gate_exp, b + 1)
                nc.vector.tensor_reduce(total, gates, AX_X, ALU.add).then_inc(exps_taken, 1)
                nc.vector.tensor_reduce(top, gates, AX_X, ALU.max).then_inc(exps_taken, 1)
                dve.wait_ge(exps_taken, 2 * b + 2)
                link(nc.vector.reciprocal(total, total))
                link(nc.vector.tensor_tensor(gate, top, total, ALU.mult))
                link(nc.vector.tensor_tensor(gates, gates, over_e(total), ALU.mult))
                link(nc.vector.tensor_tensor(tops, gates, over_e(gate), ALU.is_equal))
                link(nc.vector.tensor_tensor(tops, tops, expert_no[:, b * TB:(b + 1) * TB], ALU.mult))
                link(nc.vector.tensor_reduce(best, tops, AX_X, ALU.max))
                nc.vector.tensor_tensor(onehot[:, b * TB:(b + 1) * TB], tops, over_e(best),
                                        ALU.is_equal).then_inc(onehot_done, 1)
                link(nc.vector.tensor_scalar(number, best, -float(CAP), float(E * CAP), ALU.mult, ALU.add))
                dve.wait_ge(tags_done, 1)
                nc.vector.tensor_copy(h2x[:, b * TB:(b + 1) * TB, D + 1 + b], gate).then_inc(gate_tagged, 1)

            def place_tokens(b):
                gates, tops, top, total, best, place, number, over, gate = of_batch(b)
                ts = slice(b * TB, (b + 1) * TB)
                dve.wait_ge(count_done, b + 1)
                counts = bank[3][:, 0:TB * E].rearrange("p (t e) -> p t e", e=E)
                dve.wait_ge(onehot_done, b + 1)
                link(nc.vector.tensor_tensor(tops, counts, onehot[:, ts], ALU.mult))
                link(nc.vector.tensor_reduce(place, tops, AX_X, ALU.add))
                nc.vector.tensor_scalar(over, place, float(CAP), float(FAR), ALU.is_ge,
                                        ALU.mult).then_inc(place_taken, 1)
                nc.vector.tensor_tensor(number, place, number, ALU.add).then_inc(place_taken, 1)
                dve.wait_ge(place_taken, 2 * b + 2)
                dve.wait_ge(gate_tagged, b + 1)
                nc.vector.tensor_tensor(slot_i[:, ts], number, over, ALU.add).then_inc(slots_done, 1)

            for c in range(DC):
                dve.wait_ge(aT_done, c + 1)
                nc.vector.tensor_copy(attnT[c], bank[c][:]).then_inc(aT_by_dve, 1)
            dve.wait_ge(cols_done, 1)
            nc.vector.tensor_copy(h2_cols[:].rearrange("p a b c -> p (a b c)"),
                                  bank[2][:, 0:2 * B * DC]).then_inc(cols_saved, 1)
            residual(0, 3)
            row_stats(range(2))
            residual(1, 2)
            norm_stats(0, var2_done, 1, taken=2)
            dve.wait_ge(aT_done, 3)
            nc.vector.tensor_copy(attnT[2], bank[1][:]).then_inc(aT_by_dve, 1)
            period(TURNS, 2, second=False, third=False)
            normalise(0, h2, rstd2_done, h2_norm)
            dve.wait_ge(cols_saved, 1)
            for c in range(DC):
                dve.wait_ge(h2T_done, c + 1)
                nc.vector.tensor_scalar(h2T[:, 0, c, :], bank[c][:], h2_cols[:, 1, 0, c:c + 1],
                                        h2_cols[:, 0, 0, c:c + 1], ALU.mult, ALU.add).then_inc(h2T_by_dve, 1)
            modulate_rows(0)
            start_gates(0)
            norm(NG - 1, TURNS, 3)
            choose(0)
            residual(2, 4)
            row_stats(range(TB, TB + 2))
            residual(3, 5)
            norm_stats(1, var2_done, 1, taken=2)
            place_tokens(0)
            normalise(1, h2, rstd2_done, h2_norm)
            modulate_rows(1)
            start_gates(1)
            choose(1)
            place_tokens(1)

            def take_routed(pair):
                es = slice(2 * pair, 2 * pair + 2)
                dve.wait_ge(routed_in[pair], 16)
                nc.vector.tensor_scalar(token_of[:, es], routed[:, es, D], -1.0, float(FAR),
                                        ALU.mult, ALU.add).then_inc(token_done, 1)
                dve.wait_ge(rT_done, pair + 1)
                nc.vector.tensor_copy(routedT[:, :, 2 * pair * CAP:2 * (pair + 1) * CAP],
                                      bank[6 + pair % 2][:].rearrange("p (c s) -> p c s", c=DC)
                                      ).then_inc(rT_saved, 1)

            take_routed(0)
            take_routed(1)
            for e in range(E):
                g0, g1 = routed[:, e, D + 1:D + 2], routed[:, e, D + 2:D + 3]
                if e > 0:
                    dve.wait_ge(y_scaled, e)
                nc.vector.tensor_scalar(share, rows[:, 3, 0], g0, None, ALU.mult).then_inc(gain_done, 1)
                dve.wait_ge(gain_done, 2 * e + 1)
                nc.vector.scalar_tensor_tensor(out=gain, in0=rows[:, 3, 1], scalar=g1, in1=share,
                                               op0=ALU.mult, op1=ALU.add).then_inc(gain_done, 1)
                dve.wait_ge(gain_done, 2 * e + 2)
                dve.wait_ge(y_done, e + 1)
                if e >= 2:
                    dve.wait_ge(y_out[e % 2], 16 * (e // 2))
                nc.vector.tensor_tensor(y_slots[:, e % 2, :], bank[4 + e % 2][:, 0:D], gain,
                                        ALU.mult).then_inc(y_saved, 1)
                dve.wait_ge(y_saved, e + 1)
                dve.wait_ge(x1_in[e % 2], 16 * (e // 2 + 1))
                nc.vector.tensor_tensor(y_slots[:, e % 2, :], y_slots[:, e % 2, :], x1_slots[:, e % 2, :],
                                        ALU.add).then_inc(y_scaled, 1)
                if e < 2:
                    take_routed(e + 2)

        @block.tensor
        def _(pe):
            def keep_clock(times, to=3, blocks=4):
                for _ in range(times):
                    nc.tensor.matmul(bank[to][:, 0:blocks * P].rearrange("p (t q) -> p t q", t=blocks), ident[:],
                                     ident[:].unsqueeze(1).to_broadcast([P, blocks, P]), start=True, stop=True)

            pe.wait_ge(ident_done, 1)
            keep_clock(3)
            pe.wait_ge(silu_done, 1)
            pe.wait_ge(wmod_in, 16)
            for m in range(2):
                for c in range(DC):
                    col = (m * DC + c) * B
                    for k in range(DC):
                        last = nc.tensor.matmul(bank[7][:, col:col + B],
                                                wmod_sb[:, k, m * D + c * P:m * D + (c + 1) * P],
                                                silu[:, k, :], start=(k == 0), stop=(k == DC - 1))
            last.then_inc(mod_done, 1)

            def transpose_x(b):
                for c in range(DC):
                    for t in range(TB):
                        if c == 0:
                            pe.wait_ge(xn_done, TB * b + t + 1)
                        last = nc.tensor.transpose(bank[X_BANK[DC * b + c]][:, t * P:(t + 1) * P],
                                                   xn[:, TB * b + t, c * P:(c + 1) * P], ident[:])
                    last.then_inc(xT_done, 1)

            def project(n):
                b, r, lo = n // B_TILES, TILE_ROWS[n], n % B_TILES * P
                for c in range(DC):
                    last = nc.tensor.matmul(bank[PROJ_BANK[n]][0:r, :], wkqv_sb[:, c, lo:lo + r],
                                            hT[:, c, b * T:(b + 1) * T], start=(c == 0), stop=(c == DC - 1))
                last.then_inc(proj_done, 1)

            def project_v(b):
                for t in range(TB):
                    for c in range(DC):
                        s0 = b * T + t * P
                        last = nc.tensor.matmul(bank[V_BANK[b]][:, t * HKV * HD:(t + 1) * HKV * HD],
                                                hT[:, c, s0:s0 + P], wkqv_sb[:, c, (HQ + HKV) * HD:],
                                                start=(c == 0), stop=(c == DC - 1))
                last.then_inc(v_proj_done, 1)

            def rotate(n):
                r = TILE_ROWS[n]
                pe.wait_ge(biased, n + 1)
                nc.tensor.matmul(bank[ROT_BANK[n]][0:r, :], rot_sb[0:r, 0:r], tile_words[n][0][0:r, :],
                                 start=True, stop=True).then_inc(rotated, 1)

            def mod_rows(k):
                b, half = k // 2, k % 2
                for c in range(DC):
                    last = nc.tensor.matmul(bank[ROWS_BANK[k]][:], silu[:, c, b:b + 1].to_broadcast([P, P]),
                                            wmod_sb[:, c, (2 + 2 * half) * D:(4 + 2 * half) * D],
                                            start=(c == 0), stop=(c == DC - 1))
                last.then_inc(rows_done, 1)

            keep_clock(1)
            transpose_x(0)
            keep_clock(2)
            pe.wait_ge(wkqv_in, 16)
            pe.wait_ge(rope_in, 48)
            pe.wait_ge(hT_by_dve, 1)
            pe.wait_ge(hT_by_act, 1)
            project(0)
            project_v(0)
            pe.wait_ge(mod_saved, 2)
            rotate(0)
            project(1)
            project(2)
            rotate(1)
            pe.wait_ge(wmod_rest_in, 16)
            mod_rows(0)
            mod_rows(1)
            rotate(2)
            mod_rows(2)
            pe.wait_ge(rot_read, 1)
            mod_rows(3)
            pe.wait_ge(rows_copied, 2)
            transpose_x(1)

            def second_batch(piece):
                if piece == 0:
                    pe.wait_ge(hT_by_dve, 2)
                    pe.wait_ge(hT_by_act, 2)
                    pe.wait_ge(vx_done, TB)
                    project(3)
                elif piece == 1:
                    project(4)
                elif piece == 2:
                    pe.wait_ge(rows_copied, 4)
                    rotate(3)
                elif piece == 3:
                    project(5)
                elif piece == 4:
                    pe.wait_ge(biased, 5)
                    rotate(4)
                elif piece == 5:
                    pe.wait_ge(biased, 6)
                    project_v(1)
                elif piece == 6:
                    rotate(5)

            def max_scores(slot, j, i, free):
                if free is not None:
                    pe.wait_ge(max_done, free)
                nc.tensor.matmul(max_bank[i][:], qx[0:SHIFT_ROW, slot, i, j * P:(j + 1) * P],
                                 kx[0:SHIFT_ROW, slot, :], start=True, stop=True).then_inc(a_done, 1)

            def exp_scores(slot, j, i, free):
                if free is not None:
                    pe.wait_ge(exp_done, free)
                nc.tensor.matmul(exp_bank[i % 2][:], kx[0:BROWS, slot, j * P:(j + 1) * P],
                                 qx[0:BROWS, slot, i, :], start=True, stop=True).then_inc(b_done, 1)

            def values(steps, slot, j):
                pe.wait_ge(exp_done, 4 * steps)
                for i in range(G):
                    last = nc.tensor.matmul(o_bank[32 * i:32 * i + HD + 1, :], vs[:, slot, j, :],
                                            probs[:, j % 2, i, :], start=(j == 0), stop=(j == TB - 1))
                last.then_inc(pv_done, 1)

            def transpose_max():
                nc.tensor.transpose(tr_bank[0:2 * G * TB, 0:P // 2].bitcast(BF16),
                                    negparts[:].rearrange("p a n -> p (a n)"), ident_h[:]).then_inc(negT_done, 1)

            def transpose_o():
                for q in range(TB):
                    last = nc.tensor.transpose(tr_bank[:, q * P:(q + 1) * P], osb[:, q * P:(q + 1) * P], ident[:])
                last.then_inc(oT_done, 1)

            def transpose_attn(k, to):
                for q in range(TB):
                    last = nc.tensor.transpose(bank[to][:, q * P:(q + 1) * P], attn[:, k, q, :], ident[:])
                last.then_inc(aT_done, 1)

            def wo_product(k, to):
                b = 2 * k // TB
                for t in range(2 * k, 2 * k + 2):
                    q = t % TB
                    for c in range(DC):
                        last = nc.tensor.matmul(bank[to][:, (t % 2) * D:(t % 2 + 1) * D],
                                                attnT[DC * b + c][:, q * P:(q + 1) * P], wo_ga[:, b, c, :],
                                                start=(c == 0), stop=(c == DC - 1))
                last.then_inc(wo_done, 1)

            def transpose_h2(b):
                for t in range(TB):
                    pe.wait_ge(h2_norm, TB * b + t + 1)
                    for c in range(DC):
                        last = nc.tensor.transpose(bank[c][:, t * P:(t + 1) * P],
                                                   h2[:, TB * b + t, c * P:(c + 1) * P], ident[:])
                        if t == TB - 1:
                            last.then_inc(h2T_done, 1)

            def column_of(row, col):
                for c in range(DC):
                    last = nc.tensor.matmul(bank[2][:, col + c:col + c + 1], row[:, c * P:(c + 1) * P],
                                            ident[:, 0:1], start=True, stop=True)
                return last

            def logits(b):
                for t in range(TB):
                    for c in range(DC):
                        last = nc.tensor.matmul(bank[2][:, t * E:(t + 1) * E], h2T[:, b, c, t * P:(t + 1) * P],
                                                wg_sb[:, c, :], start=(c == 0), stop=(c == DC - 1))
                last.then_inc(logits_done, 1)

            def count(b):
                pe.wait_ge(onehot_done, b + 1)
                nc.tensor.matmul(bank[3][:, 0:TB * E], before[:],
                                 onehot[:, b * TB:(b + 1) * TB, :].rearrange("p t e -> p (t e)"),
                                 start=True, stop=False)
                for t in range(b * TB + TB - 1):
                    first = max(t + 1 - b * TB, 0)
                    last = nc.tensor.matmul(
                        bank[3][:, first * E:TB * E].rearrange("p (t e) -> p t e", e=E), ones_h[:],
                        onehot[:, t:t + 1, :].to_broadcast([P, TB - first, E]), start=False,
                        stop=(t == b * TB + TB - 2))
                last.then_inc(count_done, 1)

            def first_batch(piece):
                if piece == 0:
                    pe.wait_ge(max_done, 4 * TB * NG)
                    pe.wait_ge(norm_done, NG // B)
                    for c in range(DC):
                        transpose_attn(c, c)
                    for m in range(2):
                        for b in range(B):
                            last = column_of(rows[:, 1 + m, b, :], (m * B + b) * DC)
                    last.then_inc(cols_done, 1)
                elif piece == 1:
                    pe.wait_ge(wo_scaled, B)
                    pe.wait_ge(aT_by_dve, DC)
                    wo_product(0, 3)
                elif piece == 2:
                    pe.wait_ge(cols_saved, 1)
                    wo_product(1, 2)
                    pe.wait_ge(norm_done, NG // B + TB)
                    transpose_attn(2, 1)
                elif piece == 4:
                    pe.wait_ge(aT_by_dve, DC + 1)
                    transpose_h2(0)
                elif piece == 5:
                    pe.wait_ge(x1_done, 2)
                    pe.wait_ge(h2T_by_dve, DC)
                    logits(0)
                    keep_clock(1, to=0)

            def period(it, v, second=True, third=True, piece=None):
                g = 4 * it + 1 + v
                first = isinstance(it, int) and it == -1
                slot = (v + 1) % SLOTS
                if v == 3:
                    pe.wait_ge(rows_in_dram, it + 2)
                for j in range(TB):
                    ahead, jj = 1 + j // 2, (j + 2) % TB
                    mslot = (slot + ahead) % SLOTS
                    take = (second, third)[j // 2]
                    if j == 2 and take:
                        pe.wait_ge(qk_in[mslot], 32 * (it + (3 + v) // 4 + 1))

                    def for_max(i):
                        if take:
                            max_scores(mslot, jj, i, 16 * (g + ahead) + 4 * jj + i - 3)

                    def for_exp(i):
                        exp_scores(slot, j, i, None if first and j == 0 and i < 2 else 16 * g + 4 * j + i - 1)

                    for_max(0)
                    for_max(1)
                    if j == 0:
                        pe.wait_ge(shift_in[slot], 16 * (it + (1 + v) // 4 + 1))
                    for_exp(0)
                    for_max(2)
                    for_exp(1)
                    if j == 1:
                        pe.wait_ge(vs_done, g + 1)
                        if first:
                            pe.wait_ge(o_clear, 1)
                        else:
                            pe.wait_ge(o_saved, g)
                            if isinstance(it, int) and not second:
                                pe.wait_ge(norm_done, g - 1)
                            else:
                                pe.wait_ge(shift_saved, g + 1)
                            transpose_o()
                    if j == 2 and second:
                        pe.wait_ge(neg_done, g + 2)
                        if not first:
                            pe.wait_ge(norm_done, g)
                        transpose_max()
                    if j > 0:
                        values(4 * g + j, slot, j - 1)
                    elif not first:
                        values(4 * g, v % SLOTS, TB - 1)
                    for_exp(2)
                    for_max(3)
                    for_exp(3)
                    if piece is not None and piece + j >= 0:
                        first_batch(piece + j)

            pe.wait_ge(consts, 3)
            pe.wait_ge(masks_done, 2)
            pe.wait_ge(qk_in[0], 32)
            pe.wait_ge(biased, 3)
            pe.wait_ge(rot_read, 2)
            pe.wait_ge(rot_copied, 1)
            pe.wait_ge(rows_copied, 3)
            for n in range(4 * TB):
                max_scores(0, n // G, n % G, n - 3 if n > 3 else None)
                if n % 4 == 3:
                    second_batch(n // 4)
            pe.wait_ge(rot_copied, 2)
            pe.wait_ge(qk_in[1], 32)
            for n in range(4 * TB, 6 * TB):
                max_scores(1, n // G - TB, n % G, n - 3)
                if n == 4 * TB + 1:
                    pe.wait_ge(neg_done, 1)
                    transpose_max()
                if n % 2:
                    second_batch(n // 2 - 4)
            pe.wait_ge(shift_saved, 1)
            pe.wait_ge(rot_copied, 4)
            pe.wait_ge(vx_done, 2 * TB)
            period(-1, 3)
            with pe.Fori(0, TURNS) as it:
                for v in range(SLOTS):
                    period(it, v)
            period(TURNS, 0)
            period(TURNS, 1, third=False, piece=-2)
            period(TURNS, 2, second=False, third=False, piece=2)
            values(4 * NG, 3, TB - 1)
            keep_clock(1, to=0)
            pe.wait_ge(o_saved, NG)
            pe.wait_ge(norm_done, NG - 1)
            transpose_o()
            keep_clock(1, to=6)

            pe.wait_ge(norm_done, NG)
            transpose_attn(3, 0)
            keep_clock(1, to=6)
            pe.wait_ge(aT_by_act, 1)
            pe.wait_ge(exp_done, 4 * TB * NG)
            wo_product(2, 4)
            wo_product(3, 5)
            count(0)
            keep_clock(2, to=6)
            pe.wait_ge(var2_done, 2)
            keep_clock(2, to=6)
            transpose_h2(1)
            keep_clock(1, to=6)
            pe.wait_ge(h2T_by_act, DC)
            pe.wait_ge(gate_sub, 1)
            logits(1)
            pe.wait_ge(gate_sub, 2)
            keep_clock(1, to=6)
            pe.wait_ge(slots_done, 1)
            count(1)
            keep_clock(9, to=6)

            def transpose_routed(pair):
                pe.wait_ge(routed_in[pair], 16)
                if pair >= 2:
                    pe.wait_ge(rT_saved, pair - 1)
                for c in range(DC):
                    for k in range(2):
                        last = nc.tensor.transpose(bank[6 + pair % 2][:, (2 * c + k) * P:(2 * c + k + 1) * P],
                                                   routed[:, 2 * pair + k, c * P:(c + 1) * P], ident[:])
                last.then_inc(rT_done, 1)

            transpose_routed(0)
            pe.wait_ge(slots_done, 2)
            pe.wait_ge(x1_done, NT // 2)
            for k in range(2):
                pe.wait_ge(w_in[k], 16 * (E - 1))

            def hidden(e):
                if e % 2 == 0:
                    pe.wait_ge(rT_saved, e // 2 + 1)
                if e >= 2:
                    pe.wait_ge(gelu_done, 2 * e - 2)
                if e == E - 1:
                    pe.wait_ge(w7_in, 32)
                for k in range(2):
                    for f in range(FT // 2):
                        f0 = (k * FT // 2 + f) * P
                        for c in range(DC):
                            last = nc.tensor.matmul(bank[2 * (e % 2) + k][:, f * P:(f + 1) * P],
                                                    w1_sb[e][:, c, f0:f0 + P],
                                                    routedT[:, c, e * CAP:(e + 1) * CAP],
                                                    start=(c == 0), stop=(c == DC - 1))
                    last.then_inc(h_done, 1)

            def expert_out(e):
                pe.wait_ge(gelu_done, 2 * e + 2)
                if e >= 2:
                    pe.wait_ge(y_saved, e - 1)
                for f in range(FT):
                    last = nc.tensor.matmul(bank[4 + e % 2][:, 0:D], gelu[:, e % 2, f, :], w2_sb[e][:, f, :],
                                            start=(f == 0), stop=(f == FT - 1))
                last.then_inc(y_done, 1)

            hidden(0)
            transpose_routed(1)
            for e in range(E):
                if e + 1 < E:
                    hidden(e + 1)
                expert_out(e)
                if e < 2:
                    transpose_routed(e + 2)


def kernel(L0_attn_x, L0_attn_Wq, L0_attn_bq, L0_attn_Wk, L0_attn_bk, L0_attn_Wv, L0_attn_bv, L0_attn_Wo,
           L0_attn_bo, L0_ffn_w_gate, L0_ffn_w1, L0_ffn_w2, L0_c, L0_wmod):
    import numpy as np
    import concourse.bacc as bacc
    from concourse.bass_utils import run_bass_kernel_spmd

    a = {k: np.asarray(v) for k, v in dict(
        x=L0_attn_x, wq=L0_attn_Wq, bq=L0_attn_bq, wk=L0_attn_Wk, bk=L0_attn_bk, wv=L0_attn_Wv,
        bv=L0_attn_bv, wo=L0_attn_Wo, bo=L0_attn_bo, w_gate=L0_ffn_w_gate, w1=L0_ffn_w1, w2=L0_ffn_w2,
        c=L0_c, wmod=L0_wmod).items()}
    B, T, D = a["x"].shape
    HD = 8
    inv = (1.0 / np.float32(10000.0) ** (np.arange(0, HD, 2, dtype=np.float32) / np.float32(HD))).astype(np.float32)
    angle = np.tile((inv[:, None] * np.arange(T, dtype=np.float32)[None, :]).astype(np.float32), (2 * P // HD, 1))
    turn = np.zeros((P, P), np.float32)
    for row in range(P):
        if row % HD < HD // 2:
            turn[row + HD // 2, row] = -1.0
        else:
            turn[row - HD // 2, row] = 1.0
    arrays = {
        "x": a["x"].reshape(B * T, D),
        "c_t": np.ascontiguousarray(a["c"].T),
        "wmod": a["wmod"],
        "wkqv_t": np.ascontiguousarray(np.concatenate([a["wk"], a["wq"], a["wv"]], 0).T),
        "bkq": np.concatenate([a["bk"], a["bq"]], 0), "bv": a["bv"],
        "wo_t": np.ascontiguousarray(a["wo"].T),
        "bo": a["bo"], "w_gate": a["w_gate"], "w1": a["w1"], "w2": a["w2"],
        "rope_cos": np.cos(angle), "rope_sin": np.sin(angle), "rope_rot": turn,
    }
    nc = bacc.Bacc("TRN2", target_bir_lowering=False, num_devices=1)
    args = {n: nc.dram_tensor(n + "_in", v.shape, mybir.dt.from_np(v.dtype), kind="ExternalInput").ap()
            for n, v in arrays.items()}
    out = nc.dram_tensor("out_0", (B * T, D), F32, kind="ExternalOutput").ap()
    adaln_attention_moe_kernel(nc, out=out, **args)
    r = run_bass_kernel_spmd(nc, [{n + "_in": v for n, v in arrays.items()}], core_ids=[0])
    return r.results[0]["out_0"].reshape(B, T, D)
```

```python
from contextlib import ExitStack

import concourse.bass as bass
from concourse import mybir

F32 = mybir.dt.float32
BF16 = mybir.dt.bfloat16
I32 = mybir.dt.int32
ALU = mybir.AluOpType
ACT = mybir.ActivationFunctionType
AX_X = mybir.AxisListType.X

P = 128


def adaln_attention_moe_kernel(nc, x, c_t, wmod, wkqv_t, bkq, bv, wo_t, bo, w_gate, w1, w2,
                               rope_cos, rope_sin, rope_rot, out):
    B = c_t.shape[1]
    S, D = x.shape
    T = S // B
    HD = 8
    HQ = D // HD
    HKV = bv.shape[0] // HD
    G = HQ // HKV
    NG = B * HKV
    E, _, F = w1.shape
    CAP = S // E
    DC = D // P
    NT = S // P
    TB = T // P
    FT = F // P
    CH = 6
    EPS = 1e-5
    GATE_MIN = 0.25
    FAR = 4 * S
    TAGS = 4
    PARTS = 3
    COMBOS = PARTS * PARTS
    ROWS = COMBOS * HD
    SHIFT_ROW = 96
    BROWS = SHIFT_ROW + 2
    SLOTS = 4
    SCALE = float(HD) ** -0.5
    assert (P, T, TB, G, DC, CAP, NG % SLOTS) == (128, 512, 4, 4, 2, P, 0)

    mod_dram = nc.dram_tensor("mod_scratch", (4, B, D), F32, kind="Internal").ap()
    qx_dram = nc.dram_tensor("qx_scratch", (B * HQ, HD * COMBOS, T), BF16, kind="Internal").ap()
    kx_dram = nc.dram_tensor("kx_scratch", (NG, HD * COMBOS, T), BF16, kind="Internal").ap()
    routed_dram = nc.dram_tensor("routed_scratch", (E * CAP, D + TAGS), F32, kind="Internal").ap()
    x1_dram = nc.dram_tensor("x1_scratch", (S, D), F32, kind="Internal").ap()

    with ExitStack() as ctx:
        def sb(name, shape, dt):
            return ctx.enter_context(nc.sbuf_tensor("sb_" + name, shape, dt))

        def sem(name):
            return ctx.enter_context(nc.semaphore(name))

        bank = [ctx.enter_context(nc.psum_tensor(f"bank{i}", [P, 512], F32)) for i in range(8)]
        max_bank, exp_bank, o_bank, tr_bank = bank[0:4], bank[4:6], bank[6], bank[7]

        B_TILES = -(-(HKV + HQ) * HD // P)
        TILE_ROWS = [min(P, (HKV + HQ) * HD - n * P) for n in range(B_TILES)] * B
        Q_ROW = HKV * HD
        PROJ_BANK = [4, 5, 3, 6, 4, 5]
        ROT_BANK = [7, 2, 0, 7, 6, 4]
        ROWS_BANK = [1, 7]
        V_BANK = [6, 5]
        X1_BANKS = ((4, 5), (1, 6))
        X_BANK = [0, 1, 4, 5]

        CHUNK = DC * F
        wbuf = sb("experts", [P, 2 * E * CHUNK], F32)
        pbuf = sb("probs", [P, 2 * G * T], F32)
        qx = sb("qx", [P, SLOTS, G, T], BF16)
        kx = sb("kx", [P, SLOTS, T], BF16)
        xres = sb("x", [P, NT, D], F32)
        vx = sb("vx", [P, NG, TB * (HD + 1)], F32)
        vs = sb("vs", [P, SLOTS, TB, HD + 1], F32)
        attn = sb("attn", [P, B * DC, TB, P], F32)
        rows = sb("mod_rows", [P, 4, B, D], F32)
        osb = sb("o_sbuf", [P, T], F32)
        wo_sb = sb("wo", [P, DC, D], F32)
        wo_ga = sb("wo_ga", [P, B, DC, D], F32)
        h2_cols = sb("h2_cols", [P, 2, B, DC], F32)
        wg_sb = sb("w_gate", [P, DC, E], F32)
        bo_sb = sb("bo", [P, D], F32)
        bv_sb = sb("bv", [P, HKV * HD], F32)
        bkq_sb = sb("bkq", [P, B_TILES], F32)
        ident = sb("ident", [P, P], F32)
        ident_h = sb("ident_h", [P, P], BF16)
        before = sb("before", [P, P], BF16)
        ones_h = sb("ones_h", [P, P], BF16)
        cT = sb("cT", [P, DC, B], F32)
        c_exp = sb("c_exp", [P, DC, B], F32)
        silu = sb("silu", [P, DC, B], F32)
        mod_scale = sb("mod_scale", [P, DC, B], F32)
        mod_shift = sb("mod_shift", [P, DC, B], F32)
        stats = sb("stats", [P, NT, 6], F32)
        meanvar = sb("meanvar", [P, NT, 2], F32)
        rstd = sb("rstd", [P, NT], F32)
        minus_half = sb("minus_half", [P, NT], F32)
        negmax = sb("negmax", [P, 2, G * TB], F32)
        negparts = sb("negparts", [P, 2, G * TB], BF16)
        shift_rows = sb("shift_rows", [2 * G * TB, 2, P], BF16)
        rden = sb("rden", [P, TB, G], F32)
        expert_no = sb("expert_no", [P, NT, E], F32)
        g_work = sb("g_work", [P, 2, NT, E], F32)
        g_one = sb("g_one", [P, 8, NT], F32)
        onehot = sb("onehot", [P, NT, E], BF16)
        gate_e, is_top = g_work[:, 0], g_work[:, 1]
        one = sb("one", [P, 1], F32)
        ga_bo = sb("ga_bo", [P, B, D], F32)
        zeros_row = sb("zeros_row", [P, D + TAGS], F32)
        token_of = sb("token_of", [P, E], I32)
        slot_no = sb("slot_no", [P, CAP], F32)
        slot_i = sb("slot_i", [P, NT], I32)

        at = [6 * CHUNK]

        def early(words):
            at[0] += words
            assert at[0] <= 2 * E * CHUNK
            return wbuf[:, at[0] - words:at[0]]

        wmod_sb = early(DC * CH * D).rearrange("p (c n) -> p c n", c=DC)
        NKQV = (HQ + 2 * HKV) * HD
        wkqv_sb = early(DC * NKQV).rearrange("p (c n) -> p c n", c=DC)
        at[0] = 8 * CHUNK
        b0_words = [[early(T) for _ in range(3)] for _ in range(3)]
        b0_parts = [early(PARTS * T // 2).bitcast(BF16).rearrange("p (a t) -> p a t", a=PARTS)
                    for _ in range(3)]
        assert at[0] >= 9 * CHUNK
        b1_words = [[early(T) for _ in range(3)] for _ in range(3)]
        b1_parts = [early(PARTS * T // 2).bitcast(BF16).rearrange("p (a t) -> p a t", a=PARTS)
                    for _ in range(3)]
        cos_sb, sin_sb, rot_sb = early(T), early(T), early(P)
        mod_pair = early(4 * D)[0:B]
        tile_words, tile_parts = b0_words + b1_words, b0_parts + b1_parts
        xn = pbuf[:, 0:S * D // P].rearrange("p (t d) -> p t d", t=NT)
        hT = attn[:].rearrange("p a b c -> p (a b c)").rearrange("p (c s) -> p c s", c=DC)
        HALF = S * D // P
        h2_at = 2 * (E - 1) * CHUNK + HALF // B
        h2x = wbuf[:, h2_at:h2_at + NT * (D + TAGS)].rearrange("p (t d) -> p t d", t=NT)
        h2 = h2x[:, :, 0:D]
        attnT = [wbuf[:, h2_at - 2 * T:h2_at - T], wbuf[:, h2_at - T:h2_at],
                 wbuf[:, h2_at + NT * (D + TAGS):h2_at + NT * (D + TAGS) + T], pbuf[:, 2 * G * T - T:]]
        rows_at = h2_at + NT * (D + TAGS) + T
        cols_rows = wbuf[0:2 * B * DC, rows_at:rows_at + P]
        qx_words = qx[:].rearrange("p a b c -> p (a b c)").bitcast(F32)
        h2T = qx_words[:, 0:HALF].rearrange("p (b c s) -> p b c s", b=B, c=DC)
        gelu = qx_words[:, HALF:2 * HALF].rearrange("p (a f s) -> p a f s", a=2, f=FT)
        gain, share = (kx[:].rearrange("p a b -> p (a b)").bitcast(F32)[:, k * D:(k + 1) * D] for k in range(2))
        x1_slots = vx[:].rearrange("p g c -> p (g c)")[:, 0:2 * D].rearrange("p (a d) -> p a d", a=2)
        y_slots = osb[:, :].rearrange("p (a d) -> p a d", a=2)
        routed = pbuf[:, 0:E * (D + TAGS)].rearrange("p (e d) -> p e d", e=E)
        routedT = hT
        picks = pbuf[:, E * (D + TAGS):E * (D + TAGS) + NT * CAP].rearrange("p (t s) -> p t s", t=NT)
        probs = pbuf[:].rearrange("p (a i t) -> p a i t", a=2, i=G)
        w1_sb = [wbuf[:, 2 * e * CHUNK:(2 * e + 1) * CHUNK].rearrange("p (c f) -> p c f", c=DC)
                 for e in range(E)]
        w2_sb = [wbuf[:, (2 * e + 1) * CHUNK:(2 * e + 2) * CHUNK].rearrange("p (t d) -> p t d", t=FT)
                 for e in range(E)]
        w1_v = w1.rearrange("e (c p) f -> e p c f", p=P)
        w2_v = w2.rearrange("e (t p) d -> e p t d", p=P)
        x_v = x.rearrange("(t p) d -> p t d", p=P)
        out_v = out.rearrange("(t p) d -> p t d", p=P)


        def q_rows(b, lo, hi):
            return qx_dram[b * HQ + lo:b * HQ + hi].rearrange("h (d r a) t -> (h d) r (a t)", r=PARTS, a=PARTS)

        def k_rows(b):
            return kx_dram[b * HKV:(b + 1) * HKV].rearrange("h (d a r) t -> (h d) a r t", r=PARTS, a=PARTS)

        def copies(ap):
            return ap.unsqueeze(1).to_broadcast([ap.shape[0], PARTS, ap.shape[1]])

        def q_parts(b, lo, hi):
            row = Q_ROW + lo * HD
            tile, row = B_TILES * b + row // P, row % P
            return copies(tile_parts[tile].rearrange("p a t -> p (a t)")[row:row + (hi - lo) * HD])

        Q_ENDS = [((n + 1) * P - Q_ROW) // HD for n in range(B_TILES - 1)] + [HQ]

        c_in, wmod_in, wmod_rest_in, wkqv_in, bias_in, rope_in, wo_in = map(
            sem, ("c_in", "wmod_in", "wmod_rest_in", "wkqv_in", "bias_in", "rope_in", "wo_in"))
        x_in = [sem(f"x_in{b}") for b in range(B)]
        consts = sem("consts")
        ident_done, masks_done, rows_clear = sem("ident_done"), sem("masks_done"), sem("rows_clear")
        routed_zero, zeros_done, o_clear = map(
            sem, ("routed_zero", "zeros_done", "o_clear"))
        c_exp_done, silu_done, mod_done, mod_saved = map(
            sem, ("c_exp_done", "silu_done", "mod_done", "mod_saved"))
        stats_done = sem("stats_done")
        var_done, rstd_done, xn_done = map(sem, ("var_done", "rstd_done", "xn_done"))
        xT_done, hT_by_dve, hT_by_act = map(sem, ("xT_done", "hT_by_dve", "hT_by_act"))
        proj_done, v_proj_done, biased, rotated = map(
            sem, ("proj_done", "v_proj_done", "biased", "rotated"))
        rot_read, rot_copied, vx_done = map(sem, ("rot_read", "rot_copied", "vx_done"))
        split_by_dve, split_by_pool = sem("split_by_dve"), sem("split_by_pool")
        kx_written, qx_written = sem("kx_written"), sem("qx_written")
        kx_by_pool, qx_by_pool = sem("kx_by_pool"), sem("qx_by_pool")
        rows_in_dram, q0_written = sem("rows_in_dram"), sem("q0_written")
        q1_written = sem("q1_written")
        vo_bias_in = sem("vo_bias_in")
        rows_done, rows_copied = sem("rows_done"), sem("rows_copied")
        mod_written, rows_in = sem("mod_written"), sem("rows_in")
        xg_done = sem("xg_done")
        dve_step, pool_step = sem("dve_step"), sem("pool_step")
        qk_in = [sem(f"qk_in{u}") for u in range(SLOTS)]
        shift_in = [sem(f"shift_in{u}") for u in range(SLOTS)]
        a_done, max_done, b_done, exp_done, pv_done = map(
            sem, ("a_done", "max_done", "b_done", "exp_done", "pv_done"))
        neg_hi, neg_done, negT_done, shift_saved = map(
            sem, ("neg_hi", "neg_done", "negT_done", "shift_saved"))
        vs_done, o_saved, oT_done, rden_done, norm_done = map(
            sem, ("vs_done", "o_saved", "oT_done", "rden_done", "norm_done"))
        h2_norm, rT_saved, gate_tagged = map(
            sem, ("h2_norm", "rT_saved", "gate_tagged"))
        w_in = [sem(f"w_in{k}") for k in range(2)]
        aT_done, aT_by_dve, aT_by_act, wo_done = map(
            sem, ("aT_done", "aT_by_dve", "aT_by_act", "wo_done"))
        var2_done, rstd2_done, h2_done, h2T_done, h2T_by_dve, h2T_by_act = map(
            sem, ("var2_done", "rstd2_done", "h2_done", "h2T_done", "h2T_by_dve", "h2T_by_act"))
        logits_done, gate_sub, gate_exp, onehot_done, count_done = map(
            sem, ("logits_done", "gate_sub", "gate_exp", "onehot_done", "count_done"))
        slots_done, scattered, rT_done = map(sem, ("slots_done", "scattered", "rT_done"))
        routed_in = [sem(f"routed_in{k}") for k in range(E)]
        w7_in, tags_done = sem("w7_in"), sem("tags_done")
        h_done, gelu_done, y_done, y_saved = map(sem, ("h_done", "gelu_done", "y_done", "y_saved"))
        x1_done, x1_written, x1_out = map(sem, ("x1_done", "x1_written", "x1_out"))
        wo_scaled, cols_in, cols_done, cols_saved = map(
            sem, ("wo_scaled", "cols_in", "cols_done", "cols_saved"))
        slot_kept, picks_by_pool, picks_by_dve, first_by_dve, first_by_act = map(
            sem, ("slot_kept", "picks_by_pool", "picks_by_dve", "first_by_dve", "first_by_act"))
        first_done = sem("first_done")
        exps_taken, place_taken = sem("exps_taken"), sem("place_taken")
        token_done, slots_clear, gain_done, y_scaled = map(
            sem, ("token_done", "slots_clear", "gain_done", "y_scaled"))
        x1_in = [sem(f"x1_in{k}") for k in range(2)]
        y_out = [sem(f"y_out{k}") for k in range(2)]

        block = ctx.enter_context(nc.Block())

        TURNS = (NG - 4) // SLOTS


        @block.sync
        def _(sp):
            sp.dma_start(cT[:], c_t.rearrange("(c p) b -> p c b", p=P)).then_inc(c_in, 16)
            sp.dma_start(xres[:, 0:TB, :], x_v[:, 0:TB, :]).then_inc(x_in[0], 16)
            wmod_v = wmod.rearrange("(c p) n -> p c n", p=P)
            sp.dma_start(wmod_sb[:, :, 0:2 * D], wmod_v[:, :, 0:2 * D]).then_inc(wmod_in, 16)
            sp.dma_start(wkqv_sb, wkqv_t.rearrange("(c p) n -> p c n", p=P)).then_inc(wkqv_in, 16)
            for n in range(B_TILES):
                sp.dma_start(bkq_sb[0:TILE_ROWS[n], n:n + 1],
                             bkq[n * P:n * P + TILE_ROWS[n]].rearrange("(p a) -> p a", a=1)).then_inc(bias_in, 16)
            sp.dma_start(rot_sb, rope_rot).then_inc(rope_in, 16)
            sp.dma_start(cos_sb, rope_cos).then_inc(rope_in, 16)
            sp.dma_start(sin_sb, rope_sin).then_inc(rope_in, 16)
            sp.dma_start(xres[:, TB:, :], x_v[:, TB:, :]).then_inc(x_in[1], 16)
            sp.dma_start(wmod_sb[:, :, 2 * D:], wmod_v[:, :, 2 * D:]).then_inc(wmod_rest_in, 16)
            sp.dma_start(bv_sb[:], bv.rearrange("(a n) -> a n", a=1).to_broadcast([P, HKV * HD])).then_inc(vo_bias_in, 16)
            sp.dma_start(bo_sb[:], bo.rearrange("(a n) -> a n", a=1).to_broadcast([P, D])).then_inc(vo_bias_in, 16)
            sp.dma_start(wo_sb[:], wo_t.rearrange("(c p) n -> p c n", p=P)).then_inc(wo_in, 16)
            sp.dma_start(wg_sb[:], w_gate.rearrange("(c p) n -> p c n", p=P)).then_inc(wo_in, 16)

            sp.wait_ge(consts, 2)
            sp.wait_ge(rows_clear, 1)
            for a in range(PARTS):
                sp.wait_ge(split_by_dve, a + 1)
                if a == PARTS - 1:
                    sp.dma_start(q_rows(0, 0, G), q_parts(0, 0, G)).then_inc(q0_written, 16)
                sp.dma_start(k_rows(0)[:, a], copies(tile_parts[0][0:Q_ROW, a, :])).then_inc(kx_written, 16)
            sp.wait_ge(q0_written, 16)
            sp.dma_start(qx[0:ROWS, 0, :, :], qx_dram[0:G].rearrange("i r t -> r i t")).then_inc(qk_in[0], 16)
            sp.wait_ge(kx_written, 16 * PARTS)
            sp.dma_start(kx[0:ROWS, 0, :], kx_dram[0]).then_inc(qk_in[0], 16)
            sp.dma_start(q_rows(0, G, Q_ENDS[0]), q_parts(0, G, Q_ENDS[0])).then_inc(q1_written, 16)
            sp.wait_ge(split_by_dve, 2 * PARTS)
            sp.dma_start(q_rows(0, Q_ENDS[0], Q_ENDS[1]), q_parts(0, Q_ENDS[0], Q_ENDS[1])).then_inc(qx_written, 16)

            def load_group(g, u):
                sp.dma_start(kx[0:ROWS, u, :], kx_dram[g]).then_inc(qk_in[u], 16)
                sp.dma_start(qx[0:ROWS, u, :, :],
                             qx_dram[bass.ds(g * G, G)].rearrange("i r t -> r i t")).then_inc(qk_in[u], 16)

            def load_shift(buf, u):
                sp.dma_start(qx[SHIFT_ROW:BROWS, u, :, :].rearrange("a i (q t) -> a (i q) t", q=TB),
                             shift_rows[:, buf, :]).then_inc(shift_in[u], 16)

            sp.wait_ge(q1_written, 16)
            load_group(1, 1)
            sp.wait_ge(qx_written, 16)
            load_group(2, 2)
            sp.wait_ge(shift_saved, 1)
            load_shift(0, 0)

            def period(it, v, load=True, shift=True, expert=True):
                g = 4 * it + 1 + v
                if load:
                    if not isinstance(it, int):
                        sp.wait_ge(b_done, 16 * g)
                    load_group(g + 3, v)
                if shift:
                    sp.wait_ge(shift_saved, g + 2)
                    load_shift((v + 2) % 2, (v + 2) % SLOTS)
                if not expert:
                    return
                if v % 2:
                    sp.dma_start(wbuf[:, bass.ds(g * CHUNK, CHUNK)].rearrange("p (c f) -> p c f", c=DC),
                                 w1_v[2 * it + (1 + v) // 2]).then_inc(w_in[0], 16)
                else:
                    sp.dma_start(wbuf[:, bass.ds(g * CHUNK, CHUNK)].rearrange("p (t d) -> p t d", t=FT),
                                 w2_v[2 * it + v // 2]).then_inc(w_in[1], 16)

            period(-1, 3)
            sp.wait_ge(rows_copied, 3)
            sp.dma_start(mod_dram.rearrange("m b d -> b m d"),
                         mod_pair.rearrange("b (m d) -> b m d", m=4)).then_inc(mod_written, 16)
            sp.wait_ge(mod_written, 16)
            sp.dma_start(rows[:].rearrange("p m b d -> p (m b d)"),
                         mod_dram.rearrange("(a m) b d -> a (m b d)", a=1).to_broadcast([P, 4 * B * D])
                         ).then_inc(rows_in, 16)
            sp.dma_start(cols_rows, mod_dram.rearrange("m b (c p) -> (m b c) p", p=P)[B * DC:3 * B * DC, :]
                         ).then_inc(cols_in, 16)
            with sp.Fori(0, TURNS) as it:
                for v in range(SLOTS):
                    period(it, v)
            period(TURNS, 0, load=False)
            period(TURNS, 1, load=False, expert=False)

            x1_v = x1_dram.rearrange("(t p) d -> p t d", p=P)
            for b in range(B):
                ts = slice(b * TB, (b + 1) * TB)
                sp.wait_ge(x1_done, TB // 2 * (b + 1))
                sp.dma_start(x1_v[:, ts, :], xres[:, ts, :]).then_inc(x1_written, 16)
                sp.dma_start(out_v[:, ts, :], xres[:, ts, :]).then_inc(x1_out, 16)

            sp.wait_ge(scattered, 16 * NT)
            for e in range(E):
                sp.dma_start(routed[:, e, :], routed_dram[e * CAP:(e + 1) * CAP, :]).then_inc(routed_in[e], 16)
            sp.wait_ge(first_done, 1)
            sp.dma_start(w1_sb[E - 1], w1_v[E - 1]).then_inc(w7_in, 16)
            sp.dma_start(w2_sb[E - 1], w2_v[E - 1]).then_inc(w7_in, 16)
            sp.wait_ge(x1_out, 16 * B)

        @block.gpsimd
        def _(pool):
            step = [0]

            def link(ins):
                step[0] += 1
                ins.then_inc(pool_step, 1)
                pool.wait_ge(pool_step, step[0])

            link(nc.gpsimd.memset(ident[:], 0.0))
            nc.gpsimd.affine_select(out=ident[:], in_=ident[:], compare_op=ALU.not_equal, fill=1.0,
                                    base=0, pattern=[[-1, P]], channel_multiplier=1).then_inc(ident_done, 1)
            link(nc.gpsimd.memset(minus_half[:], -0.5))
            nc.gpsimd.memset(qx[64:SHIFT_ROW].rearrange("p a b c -> p (a b c)").bitcast(F32),
                             0.0).then_inc(rows_clear, 1)
            pool.wait_ge(rows_clear, 1)
            for b in range(B):
                ts = slice(b * TB, (b + 1) * TB)
                pool.wait_ge(var_done, b + 1)
                nc.gpsimd.tensor_tensor(rstd[:, ts], rstd[:, ts], minus_half[:, ts],
                                        ALU.pow).then_inc(rstd_done, 1)
                pool.wait_ge(rstd_done, b + 1)
            pool.wait_ge(ident_done, 1)
            link(nc.gpsimd.tensor_copy(ident_h[:], ident[:]))
            link(nc.gpsimd.memset(ones_h[:], 1.0))
            nc.gpsimd.affine_select(out=before[:], in_=ones_h[:], compare_op=ALU.is_gt, fill=0.0,
                                    base=0, pattern=[[1, P]], channel_multiplier=-1).then_inc(masks_done, 1)
            pool.wait_ge(masks_done, 1)
            nc.gpsimd.iota(expert_no[:], pattern=[[0, NT], [-1, E]], base=E, channel_multiplier=0,
                           allow_small_or_imprecise_dtypes=True).then_inc(masks_done, 1)
            pool.wait_ge(masks_done, 2)
            nc.gpsimd.iota(slot_no[:], pattern=[[1, CAP]], base=0, channel_multiplier=0,
                           allow_small_or_imprecise_dtypes=True).then_inc(masks_done, 1)
            pool.wait_ge(masks_done, 3)

            pool.wait_ge(rope_in, 48)
            for n in range(2, 6):
                r = TILE_ROWS[n]
                biased_w, turned_w, sum_w = (w[0:r, :] for w in tile_words[n])
                part = tile_parts[n]
                pool.wait_ge(rot_copied, n - 1)
                link(nc.gpsimd.tensor_tensor(turned_w, turned_w, sin_sb[0:r, :], ALU.mult))
                link(nc.gpsimd.tensor_tensor(sum_w, biased_w, cos_sb[0:r, :], ALU.mult))
                link(nc.gpsimd.tensor_tensor(sum_w, sum_w, turned_w, ALU.add))
                link(nc.gpsimd.tensor_copy(part[0:r, 0, :], sum_w))
                link(nc.gpsimd.tensor_tensor(sum_w, sum_w, part[0:r, 0, :], ALU.subtract))
                link(nc.gpsimd.tensor_copy(part[0:r, 1, :], sum_w))
                link(nc.gpsimd.tensor_tensor(part[0:r, 2, :], sum_w, part[0:r, 1, :], ALU.subtract))
                if n == 3:
                    for a in range(PARTS):
                        pool.dma_start(k_rows(1)[:, a], copies(part[0:Q_ROW, a, :])).then_inc(kx_by_pool, 16)
                b, lo, hi = n // B_TILES, (0 if n == 3 else Q_ENDS[n % B_TILES - 1]), Q_ENDS[n % B_TILES]
                pool.dma_start(q_rows(b, lo, hi), q_parts(b, lo, hi)).then_inc(qx_by_pool, 16)
                if n != 3:
                    if n > 3:
                        pool.wait_ge(kx_by_pool, 16 * PARTS)
                    pool.wait_ge(qx_by_pool, 16 * (n - 1))
                    pool.sem_inc(rows_in_dram, 1)
            pool.sem_inc(rows_in_dram, 1)

            pool.wait_ge(rows_in, 16)
            pool.wait_ge(vo_bias_in, 32)
            sign = ga_bo[:].rearrange("p b d -> p (b d)")
            for m in (0, 3):
                gate = rows[:, m].rearrange("p b d -> p (b d)")
                link(nc.gpsimd.tensor_scalar(sign, gate, 0.0, 2.0, ALU.is_ge, ALU.mult))
                link(nc.gpsimd.tensor_scalar(sign, sign, -1.0, None, ALU.add))
                link(nc.gpsimd.tensor_tensor(gate, gate, sign, ALU.mult))
                link(nc.gpsimd.tensor_scalar(gate, gate, GATE_MIN, None, ALU.max))
                link(nc.gpsimd.tensor_tensor(gate, gate, sign, ALU.mult))
            pool.wait_ge(wo_in, 32)
            for b in range(B):
                nc.gpsimd.tensor_tensor(wo_ga[:, b], wo_sb[:], rows[:, 0, b].unsqueeze(1).to_broadcast([P, DC, D]),
                                        ALU.mult).then_inc(wo_scaled, 1)
                pool.wait_ge(wo_scaled, b + 1)
            for b in range(B):
                link(nc.gpsimd.tensor_tensor(ga_bo[:, b], rows[:, 0, b], bo_sb[:], ALU.mult))
                for t in range(b * TB, (b + 1) * TB):
                    nc.gpsimd.tensor_tensor(xres[:, t], xres[:, t], ga_bo[:, b], ALU.add).then_inc(xg_done, 1)
                    pool.wait_ge(xg_done, t + 1)
            nc.gpsimd.memset(zeros_row[:], 0.0).then_inc(zeros_done, 1)
            pool.wait_ge(zeros_done, 1)
            link(nc.gpsimd.memset(h2x[:, :, D:], 0.0))
            nc.gpsimd.iota(h2x[:, :, D:D + 1], pattern=[[-P, NT], [0, 1]], base=FAR, channel_multiplier=-1,
                           allow_small_or_imprecise_dtypes=True).then_inc(tags_done, 1)
            pool.wait_ge(tags_done, 1)
            pool.dma_start(routed_dram.rearrange("(p e) d -> p e d", p=P),
                           zeros_row[:].unsqueeze(1).to_broadcast([P, E, D + TAGS])).then_inc(routed_zero, 16)

            for b in range(B):
                ts = slice(b * TB, (b + 1) * TB)
                pool.wait_ge(var2_done, b + 1)
                nc.gpsimd.tensor_tensor(rstd[:, ts], rstd[:, ts], minus_half[:, ts],
                                        ALU.pow).then_inc(rstd2_done, 1)
                pool.wait_ge(rstd2_done, b + 1)
            pool.wait_ge(routed_zero, 16)
            for b in range(B):
                pool.wait_ge(h2_done, b + 1)
                pool.wait_ge(slots_done, b + 1)
                for t in range(b * TB, (b + 1) * TB):
                    pool.indirect_dma_start(
                        routed_dram[:, :], bass.IndirectOffsetOnAxis(ap=slot_i[:, t:t + 1], axis=0),
                        h2x[:, t, :], None, bounds_check=E * CAP - 1, oob_is_err=False).then_inc(scattered, 16)
                if b == 0:
                    pool.wait_ge(slot_kept, 1)
                    for t in range(TB):
                        nc.gpsimd.tensor_scalar(picks[:, t], slot_no[:], g_one[:, 7, t:t + 1], None,
                                                ALU.is_equal).then_inc(picks_by_pool, 1)
                        pool.wait_ge(picks_by_pool, t + 1)

            pool.wait_ge(vs_done, NG)
            nc.gpsimd.memset(x1_slots, 0.0).then_inc(slots_clear, 1)
            pool.wait_ge(slots_clear, 1)
            pool.wait_ge(x1_written, 16 * B)

            def gather(e):
                pool.wait_ge(token_done, e + 1)
                if e >= 2:
                    pool.wait_ge(y_scaled, e - 1)
                pool.indirect_dma_start(
                    x1_slots[:, e % 2, :], None, x1_dram[:, :],
                    bass.IndirectOffsetOnAxis(ap=token_of[:, e:e + 1], axis=0),
                    bounds_check=S - 1, oob_is_err=False).then_inc(x1_in[e % 2], 16)

            gather(0)
            gather(1)
            pool.wait_ge(x1_out, 16 * B)
            for e in range(E):
                pool.wait_ge(y_scaled, e + 1)
                pool.indirect_dma_start(
                    out[:, :], bass.IndirectOffsetOnAxis(ap=token_of[:, e:e + 1], axis=0),
                    y_slots[:, e % 2, :], None, bounds_check=S - 1, oob_is_err=False).then_inc(y_out[e % 2], 16)
                if e + 2 < E:
                    gather(e + 2)
            for k in range(2):
                pool.wait_ge(y_out[k], 16 * (E // 2))

        @block.scalar
        def _(act):
            act.wait_ge(c_in, 16)
            nc.scalar.activation(c_exp[:], cT[:], ACT.Exp, scale=-1.0).then_inc(c_exp_done, 1)

            def modulate(b, c):
                act.wait_ge(mod_saved, 2)
                act.wait_ge(xT_done, 2 * b + c + 1)
                nc.scalar.activation(hT[:, c, b * T:(b + 1) * T], bank[X_BANK[2 * b + c]][:], ACT.Identity,
                                     bias=mod_shift[:, c, b:b + 1],
                                     scale=mod_scale[:, c, b:b + 1]).then_inc(hT_by_act, 1)

            def add_bias(n):
                r = TILE_ROWS[n]
                act.wait_ge(proj_done, n + 1)
                if n == 0:
                    act.wait_ge(bias_in, 16 * B_TILES)
                nc.scalar.activation(tile_words[n][0][0:r, :], bank[PROJ_BANK[n]][0:r, :], ACT.Identity,
                                     bias=bkq_sb[0:r, n % B_TILES:n % B_TILES + 1]).then_inc(biased, 1)

            def copy_rotated(n):
                r = TILE_ROWS[n]
                act.wait_ge(rotated, n + 1)
                nc.scalar.copy(tile_words[n][1][0:r, :], bank[ROT_BANK[n]][0:r, :]).then_inc(rot_copied, 1)

            def copy_rows(half):
                act.wait_ge(rows_done, half + 1)
                src = bank[ROWS_BANK[half]][0:B, :]
                dst = mod_pair[:, half * 2 * D:(half + 1) * 2 * D]
                if half == 0:
                    nc.scalar.copy(dst, src).then_inc(rows_copied, 1)
                else:
                    nc.scalar.activation(dst[:, 0:D], src[:, 0:D], ACT.Identity,
                                         bias=one[0:B]).then_inc(rows_copied, 1)
                    nc.scalar.copy(dst[:, D:], src[:, D:]).then_inc(rows_copied, 1)

            modulate(0, 1)
            for n in range(3):
                add_bias(n)
            copy_rows(0)
            copy_rows(1)
            copy_rotated(2)
            modulate(1, 0)
            modulate(1, 1)
            add_bias(3)
            add_bias(4)
            copy_rotated(3)
            add_bias(5)
            copy_rotated(4)
            copy_rotated(5)

            def period(it, v):
                g = 4 * it + 1 + v
                for j in range(TB):
                    for i in range(G):
                        act.wait_ge(b_done, 16 * g + 4 * j + i + 1)
                        if i == 0 and not (v == 3 and isinstance(it, int) and j < 2):
                            act.wait_ge(pv_done, 4 * g + j - 1)
                        nc.scalar.activation(probs[:, j % 2, i, :], exp_bank[i % 2][:], ACT.Exp,
                                             scale=SCALE).then_inc(exp_done, 1)
                        if (j, i) == (0, 1) and not (v == 3 and isinstance(it, int)):
                            save_o(4 * g)

            def save_o(steps):
                act.wait_ge(pv_done, steps)
                nc.scalar.copy(osb[:], o_bank[:]).then_inc(o_saved, 1)

            period(-1, 3)
            with act.Fori(0, TURNS) as it:
                for v in range(SLOTS):
                    period(it, v)
            for v in range(3):
                period(TURNS, v)
            save_o(4 * NG)

            def gate_exps(b):
                act.wait_ge(gate_sub, b + 1)
                e_b = gate_e[:, b * TB:(b + 1) * TB]
                nc.scalar.activation(e_b, e_b, ACT.Exp).then_inc(gate_exp, 1)

            gate_exps(0)
            act.wait_ge(aT_done, 4)
            nc.scalar.copy(attnT[3], bank[0][:]).then_inc(aT_by_act, 1)
            act.wait_ge(cols_saved, 1)
            act.wait_ge(h2T_done, DC + 1)
            nc.scalar.activation(h2T[:, 1, 0, :], bank[0][:], ACT.Identity, bias=h2_cols[:, 0, 1, 0:1],
                                 scale=h2_cols[:, 1, 1, 0:1]).then_inc(h2T_by_act, 1)
            gate_exps(1)
            act.wait_ge(first_done, 1)
            nc.scalar.copy(routedT[:, 1, 0:CAP], bank[5][:, 0:CAP]).then_inc(first_by_act, 1)
            for e in range(E):
                for k in range(2):
                    act.wait_ge(h_done, 2 * e + k + 1)
                    if e >= 2 and k == 0:
                        act.wait_ge(y_done, e - 1)
                    nc.scalar.activation(
                        gelu[:, e % 2, k * FT // 2:(k + 1) * FT // 2, :].rearrange("p f s -> p (f s)"),
                        bank[2 * (e % 2) + k][:], ACT.Gelu_apprx_tanh).then_inc(gelu_done, 1)

        @block.vector
        def _(dve):
            step = [0]

            def link(ins):
                step[0] += 1
                ins.then_inc(dve_step, 1)
                dve.wait_ge(dve_step, step[0])

            nc.vector.memset(one[:], 1.0).then_inc(consts, 1)
            link(nc.vector.memset(kx[64:SHIFT_ROW].rearrange("p a b -> p (a b)").bitcast(F32), 0.0))
            nc.vector.memset(kx[SHIFT_ROW:P].rearrange("p a b -> p (a b)"), 1.0).then_inc(consts, 1)
            nc.vector.memset(vx[:], 1.0).then_inc(consts, 1)
            dve.wait_ge(consts, 3)
            dve.wait_ge(c_exp_done, 1)
            link(nc.vector.tensor_scalar_add(c_exp[:], c_exp[:], 1.0))
            link(nc.vector.reciprocal(c_exp[:], c_exp[:]))
            nc.vector.tensor_tensor(silu[:], cT[:], c_exp[:], ALU.mult).then_inc(silu_done, 1)

            def row_stats(tiles):
                for t in tiles:
                    nc.vector.bn_stats(stats[:, t, :], xres[:, t, :]).then_inc(stats_done, 1)

            def norm_stats(b, done, round, taken=0):
                row_stats(range(b * TB + taken, (b + 1) * TB))
                dve.wait_ge(stats_done, TB * (B * round + b + 1))
                for t in range(b * TB, (b + 1) * TB):
                    ins = nc.vector.bn_aggr(meanvar[:, t, :], stats[:, t, :])
                link(ins)
                ts = slice(b * TB, (b + 1) * TB)
                nc.vector.tensor_scalar(rstd[:, ts], meanvar[:, ts, 1], EPS, None, ALU.add).then_inc(done, 1)

            def normalise(b, dst, ready, done):
                dve.wait_ge(ready, b + 1)
                for t in range(b * TB, (b + 1) * TB):
                    nc.vector.tensor_scalar(dst[:, t, :], xres[:, t, :], meanvar[:, t, 0:1], rstd[:, t:t + 1],
                                            ALU.subtract, ALU.mult).then_inc(done, 1)

            dve.wait_ge(x_in[0], 16)
            norm_stats(0, var_done, 0)
            normalise(0, xn, rstd_done, xn_done)
            dve.wait_ge(mod_done, 1)
            mod_ps = bank[7][:, 0:2 * DC * B].rearrange("p (m c b) -> p m c b", m=2, c=DC)
            nc.vector.tensor_copy(mod_shift[:], mod_ps[:, 0]).then_inc(mod_saved, 1)
            nc.vector.tensor_scalar_add(mod_scale[:], mod_ps[:, 1], 1.0).then_inc(mod_saved, 1)
            dve.wait_ge(mod_saved, 2)
            dve.wait_ge(xT_done, 1)
            nc.vector.tensor_scalar(hT[:, 0, 0:T], bank[X_BANK[0]][:], mod_scale[:, 0, 0:1], mod_shift[:, 0, 0:1],
                                    ALU.mult, ALU.add).then_inc(hT_by_dve, 1)
            dve.wait_ge(x_in[1], 16)
            norm_stats(1, var_done, 0)

            def rope_split(n):
                r = TILE_ROWS[n]
                biased_w, turned_w, sum_w = (w[0:r, :] for w in tile_words[n])
                part = tile_parts[n]
                dve.wait_ge(biased, n + 1)
                link(nc.vector.tensor_tensor(sum_w, biased_w, cos_sb[0:r, :], ALU.mult))
                dve.wait_ge(rotated, n + 1)
                rotated_ps = nc.vector.tensor_tensor(turned_w, bank[ROT_BANK[n]][0:r, :], sin_sb[0:r, :], ALU.mult)
                rotated_ps.then_inc(rot_read, 1)
                dve.wait_ge(rot_read, n + 1)
                link(nc.vector.tensor_tensor(sum_w, sum_w, turned_w, ALU.add))
                nc.vector.tensor_copy(part[0:r, 0, :], sum_w).then_inc(split_by_dve, 1)
                dve.wait_ge(split_by_dve, PARTS * n + 1)
                link(nc.vector.tensor_tensor(sum_w, sum_w, part[0:r, 0, :], ALU.subtract))
                nc.vector.tensor_copy(part[0:r, 1, :], sum_w).then_inc(split_by_dve, 1)
                dve.wait_ge(split_by_dve, PARTS * n + 2)
                nc.vector.tensor_tensor(part[0:r, 2, :], sum_w, part[0:r, 1, :],
                                        ALU.subtract).then_inc(split_by_dve, 1)

            def save_v(b):
                dve.wait_ge(v_proj_done, b + 1)
                dve.wait_ge(vo_bias_in, 32)
                dst = vx[:, b * HKV:(b + 1) * HKV, :].rearrange("p h (k c) -> p h k c", c=HD + 1)[:, :, :, 0:HD]
                for k in range(TB):
                    nc.vector.tensor_tensor(
                        dst[:, :, k, :],
                        bank[V_BANK[b]][:, k * HKV * HD:(k + 1) * HKV * HD].rearrange("p (h d) -> p h d", h=HKV),
                        bv_sb[:].rearrange("p (h d) -> p h d", h=HKV), ALU.add).then_inc(vx_done, 1)

            dve.wait_ge(rope_in, 48)
            rope_split(0)
            rope_split(1)
            normalise(1, xn, rstd_done, xn_done)
            save_v(0)

            def take_max(count, buf, col, i):
                dve.wait_ge(a_done, count)
                nc.vector.tensor_reduce(negmax[:, buf, col:col + 1], max_bank[i][:], AX_X, ALU.max,
                                        negate=True).then_inc(max_done, 1)

            def split_max(g, buf):
                dve.wait_ge(max_done, 16 * (g + 1))
                if not (isinstance(g, int) and g == 0):
                    dve.wait_ge(negT_done, g)
                nc.vector.tensor_copy(negparts[:, 0, :], negmax[:, buf, :]).then_inc(neg_hi, 1)
                dve.wait_ge(neg_hi, g + 1)
                nc.vector.tensor_tensor(negparts[:, 1, :], negmax[:, buf, :], negparts[:, 0, :],
                                        ALU.subtract).then_inc(neg_done, 1)

            def save_shift(g, buf, slot, turn):
                dve.wait_ge(negT_done, g + 1)
                if slot is not None:
                    dve.wait_ge(shift_in[slot], 16 * turn)
                nc.vector.tensor_copy(shift_rows[:, buf, :],
                                      tr_bank[0:2 * G * TB, 0:P // 2].bitcast(BF16)).then_inc(shift_saved, 1)

            def copy_v(g, u):
                nc.vector.tensor_copy(vs[:, u].rearrange("p k c -> p (k c)"), vx[:, g, :]).then_inc(vs_done, 1)

            def norm(g, it, u):
                dve.wait_ge(oT_done, g + 1)
                o = tr_bank[:].rearrange("p (q i c) -> p q i c", q=TB, i=G)
                nc.vector.reciprocal(rden[:], o[:, :, :, HD]).then_inc(rden_done, 1)
                dve.wait_ge(rden_done, g + 1)
                nc.vector.tensor_tensor(
                    attn[:, it, :, u * G * HD:(u + 1) * G * HD].rearrange("p q (i d) -> p q i d", i=G),
                    o[:, :, :, 0:HD], rden[:].unsqueeze(3).to_broadcast([P, TB, G, HD]),
                    ALU.mult).then_inc(norm_done, 1)

            def period(it, v, second=True, third=True):
                g = 4 * it + 1 + v
                first = isinstance(it, int) and it == -1
                for j in range(TB):
                    ahead, jj, take = 1 + j // 2, (j + 2) % TB, (second, third)[j // 2]
                    if j == 2 and take:
                        dve.wait_ge(neg_done, g + 1)
                    for i in range(G):
                        if take:
                            take_max(16 * (g + ahead) + 4 * jj + i + 1, (v + 1 + ahead) % 2, 4 * i + jj, i)
                        if (j, i) == (1, 2) and not first:
                            norm(g - 1, it, v)
                        if (j, i) == (1, 3) and second:
                            split_max(g + 1, (v + 2) % 2)
                        if (j, i) == (2, 0) and second:
                            save_shift(g + 1, (v + 2) % 2, None if first else v, it + 1)
                        if (j, i) == (3, 2) and second:
                            copy_v(g + 1, (v + 2) % SLOTS)

            for j in range(TB):
                for i in range(G):
                    take_max(4 * j + i + 1, 0, 4 * i + j, i)
            split_max(0, 0)
            copy_v(0, 0)
            save_shift(0, 0, None, 0)
            for j in range(TB // 2):
                for i in range(G):
                    take_max(16 + 4 * j + i + 1, 1, 4 * i + j, i)
                    if (j, i) == (0, 3):
                        save_v(1)
            dve.wait_ge(rot_copied, 3)
            nc.vector.memset(o_bank[:], 0.0).then_inc(o_clear, 1)
            period(-1, 3)
            with dve.Fori(0, TURNS) as it:
                for v in range(SLOTS):
                    period(it, v)
            period(TURNS, 0)
            period(TURNS, 1, third=False)

            def residual(k, from_banks):
                dve.wait_ge(wo_done, k + 1)
                if k == 0:
                    dve.wait_ge(xg_done, NT)
                n = 2 // len(from_banks)
                for i, from_bank in enumerate(from_banks):
                    ts = slice(2 * k + i, 2 * k + i + n)
                    y = bank[from_bank][:, 0:n * D].rearrange("p (t d) -> p t d", t=n)
                    last = nc.vector.tensor_tensor(xres[:, ts, :], xres[:, ts, :], y, ALU.add)
                last.then_inc(x1_done, 1)
                dve.wait_ge(x1_done, k + 1)

            def modulate_rows(b):
                ts = slice(b * TB, (b + 1) * TB)
                dve.wait_ge(h2T_done, DC * (b + 1))
                link(nc.vector.tensor_tensor(h2[:, ts], h2[:, ts],
                                             rows[:, 2, b].unsqueeze(1).to_broadcast([P, TB, D]), ALU.mult))
                nc.vector.tensor_tensor(h2[:, ts], h2[:, ts],
                                        rows[:, 1, b].unsqueeze(1).to_broadcast([P, TB, D]),
                                        ALU.add).then_inc(h2_done, 1)

            def over_e(ap):
                return ap.unsqueeze(2).to_broadcast([P, TB, E])

            def of_batch(b):
                ts = slice(b * TB, (b + 1) * TB)
                return [gate_e[:, ts], is_top[:, ts]] + [g_one[:, k, ts] for k in range(7)]

            def start_gates(b):
                gates, tops, top = of_batch(b)[0:3]
                logits = bank[2][:, 0:TB * E].rearrange("p (t e) -> p t e", e=E)
                dve.wait_ge(logits_done, b + 1)
                link(nc.vector.tensor_reduce(top, logits, AX_X, ALU.max))
                nc.vector.tensor_tensor(gates, logits, over_e(top), ALU.subtract).then_inc(gate_sub, 1)

            def choose(b):
                gates, tops, top, total, best, place, number, over, gate = of_batch(b)
                dve.wait_ge(gate_exp, b + 1)
                nc.vector.tensor_reduce(total, gates, AX_X, ALU.add).then_inc(exps_taken, 1)
                nc.vector.tensor_reduce(top, gates, AX_X, ALU.max).then_inc(exps_taken, 1)
                dve.wait_ge(exps_taken, 2 * b + 2)
                link(nc.vector.reciprocal(total, total))
                link(nc.vector.tensor_tensor(gate, top, total, ALU.mult))
                link(nc.vector.tensor_tensor(gates, gates, over_e(total), ALU.mult))
                link(nc.vector.tensor_tensor(tops, gates, over_e(gate), ALU.is_equal))
                link(nc.vector.tensor_tensor(tops, tops, expert_no[:, b * TB:(b + 1) * TB], ALU.mult))
                link(nc.vector.tensor_reduce(best, tops, AX_X, ALU.max))
                nc.vector.tensor_tensor(onehot[:, b * TB:(b + 1) * TB], tops, over_e(best),
                                        ALU.is_equal).then_inc(onehot_done, 1)
                link(nc.vector.tensor_scalar(number, best, -float(CAP), float(E * CAP), ALU.mult, ALU.add))
                dve.wait_ge(tags_done, 1)
                nc.vector.tensor_copy(h2x[:, b * TB:(b + 1) * TB, D + 1 + b], gate).then_inc(gate_tagged, 1)

            def place_tokens(b):
                gates, tops, top, total, best, place, number, over, gate = of_batch(b)
                ts = slice(b * TB, (b + 1) * TB)
                dve.wait_ge(count_done, b + 1)
                counts = bank[3][:, 0:TB * E].rearrange("p (t e) -> p t e", e=E)
                dve.wait_ge(onehot_done, b + 1)
                link(nc.vector.tensor_tensor(tops, counts, onehot[:, ts], ALU.mult))
                link(nc.vector.tensor_reduce(place, tops, AX_X, ALU.add))
                nc.vector.tensor_scalar(over, place, float(CAP), float(FAR), ALU.is_ge,
                                        ALU.mult).then_inc(place_taken, 1)
                nc.vector.tensor_tensor(number, place, number, ALU.add).then_inc(place_taken, 1)
                dve.wait_ge(place_taken, 2 * b + 2)
                dve.wait_ge(gate_tagged, b + 1)
                nc.vector.tensor_tensor(slot_i[:, ts], number, over, ALU.add).then_inc(slots_done, 1)
                nc.vector.tensor_tensor(g_one[:, 7, ts], number, over, ALU.add).then_inc(slot_kept, 1)

            for c in range(DC):
                dve.wait_ge(aT_done, c + 1)
                nc.vector.tensor_copy(attnT[c], bank[c][:]).then_inc(aT_by_dve, 1)
            dve.wait_ge(cols_done, 1)
            nc.vector.tensor_copy(h2_cols[:].rearrange("p a b c -> p (a b c)"),
                                  bank[2][:, 0:2 * B * DC]).then_inc(cols_saved, 1)
            residual(0, [3])
            row_stats(range(2))
            residual(1, [2])
            norm_stats(0, var2_done, 1, taken=2)
            dve.wait_ge(aT_done, 3)
            nc.vector.tensor_copy(attnT[2], bank[1][:]).then_inc(aT_by_dve, 1)
            period(TURNS, 2, second=False, third=False)
            normalise(0, h2, rstd2_done, h2_norm)
            dve.wait_ge(cols_saved, 1)

            def modulate_columns(b, c):
                dve.wait_ge(h2T_done, DC * b + c + 1)
                nc.vector.tensor_scalar(h2T[:, b, c, :], bank[c][:], h2_cols[:, 1, b, c:c + 1],
                                        h2_cols[:, 0, b, c:c + 1], ALU.mult, ALU.add).then_inc(h2T_by_dve, 1)

            for c in range(DC):
                modulate_columns(0, c)
            modulate_rows(0)
            start_gates(0)
            norm(NG - 1, TURNS, 3)
            choose(0)
            residual(2, X1_BANKS[0])
            row_stats(range(TB, TB + 2))
            residual(3, X1_BANKS[1])
            norm_stats(1, var2_done, 1, taken=2)
            place_tokens(0)
            normalise(1, h2, rstd2_done, h2_norm)
            modulate_columns(1, 1)
            modulate_rows(1)
            start_gates(1)
            choose(1)
            place_tokens(1)
            dve.wait_ge(slot_kept, 2)
            nc.vector.tensor_tensor(picks[:, TB:], g_one[:, 7, TB:].unsqueeze(2).to_broadcast([P, TB, CAP]),
                                    slot_no[:].unsqueeze(1).to_broadcast([P, TB, CAP]),
                                    ALU.is_equal).then_inc(picks_by_dve, 1)
            dve.wait_ge(first_done, 1)
            nc.vector.tensor_copy(routedT[:, 0, 0:CAP], bank[4][:, 0:CAP]).then_inc(first_by_dve, 1)

            def take_routed(e):
                dve.wait_ge(routed_in[e], 16)
                nc.vector.tensor_scalar(token_of[:, e:e + 1], routed[:, e, D:D + 1], -1.0, float(FAR),
                                        ALU.mult, ALU.add).then_inc(token_done, 1)
                if e == 0:
                    return
                dve.wait_ge(rT_done, e)
                nc.vector.tensor_copy(routedT[:, :, e * CAP:(e + 1) * CAP],
                                      bank[6 + e % 2][:, 0:DC * CAP].rearrange("p (c s) -> p c s", c=DC)
                                      ).then_inc(rT_saved, 1)

            take_routed(0)
            take_routed(1)
            take_routed(2)
            for e in range(E):
                g0, g1 = routed[:, e, D + 1:D + 2], routed[:, e, D + 2:D + 3]
                if e > 0:
                    dve.wait_ge(y_scaled, e)
                nc.vector.tensor_scalar(share, rows[:, 3, 0], g0, None, ALU.mult).then_inc(gain_done, 1)
                dve.wait_ge(gain_done, 2 * e + 1)
                nc.vector.scalar_tensor_tensor(out=gain, in0=rows[:, 3, 1], scalar=g1, in1=share,
                                               op0=ALU.mult, op1=ALU.add).then_inc(gain_done, 1)
                dve.wait_ge(gain_done, 2 * e + 2)
                dve.wait_ge(y_done, e + 1)
                if e >= 2:
                    dve.wait_ge(y_out[e % 2], 16 * (e // 2))
                nc.vector.tensor_tensor(y_slots[:, e % 2, :], bank[4 + e % 2][:, 0:D], gain,
                                        ALU.mult).then_inc(y_saved, 1)
                dve.wait_ge(y_saved, e + 1)
                dve.wait_ge(x1_in[e % 2], 16 * (e // 2 + 1))
                nc.vector.tensor_tensor(y_slots[:, e % 2, :], y_slots[:, e % 2, :], x1_slots[:, e % 2, :],
                                        ALU.add).then_inc(y_scaled, 1)
                if e + 3 < E:
                    take_routed(e + 3)

        @block.tensor
        def _(pe):
            def keep_clock(times, to=3, blocks=4):
                for _ in range(times):
                    nc.tensor.matmul(bank[to][:, 0:blocks * P].rearrange("p (t q) -> p t q", t=blocks), ident[:],
                                     ident[:].unsqueeze(1).to_broadcast([P, blocks, P]), start=True, stop=True)

            pe.wait_ge(ident_done, 1)
            keep_clock(3)
            pe.wait_ge(silu_done, 1)
            pe.wait_ge(wmod_in, 16)
            for m in range(2):
                for c in range(DC):
                    col = (m * DC + c) * B
                    for k in range(DC):
                        last = nc.tensor.matmul(bank[7][:, col:col + B],
                                                wmod_sb[:, k, m * D + c * P:m * D + (c + 1) * P],
                                                silu[:, k, :], start=(k == 0), stop=(k == DC - 1))
            last.then_inc(mod_done, 1)

            def transpose_x(b):
                for c in range(DC):
                    for t in range(TB):
                        if c == 0:
                            pe.wait_ge(xn_done, TB * b + t + 1)
                        last = nc.tensor.transpose(bank[X_BANK[DC * b + c]][:, t * P:(t + 1) * P],
                                                   xn[:, TB * b + t, c * P:(c + 1) * P], ident[:])
                    last.then_inc(xT_done, 1)

            def project(n):
                b, r, lo = n // B_TILES, TILE_ROWS[n], n % B_TILES * P
                for c in range(DC):
                    last = nc.tensor.matmul(bank[PROJ_BANK[n]][0:r, :], wkqv_sb[:, c, lo:lo + r],
                                            hT[:, c, b * T:(b + 1) * T], start=(c == 0), stop=(c == DC - 1))
                last.then_inc(proj_done, 1)

            def project_v(b):
                for t in range(TB):
                    for c in range(DC):
                        s0 = b * T + t * P
                        last = nc.tensor.matmul(bank[V_BANK[b]][:, t * HKV * HD:(t + 1) * HKV * HD],
                                                hT[:, c, s0:s0 + P], wkqv_sb[:, c, (HQ + HKV) * HD:],
                                                start=(c == 0), stop=(c == DC - 1))
                last.then_inc(v_proj_done, 1)

            def rotate(n):
                r = TILE_ROWS[n]
                pe.wait_ge(biased, n + 1)
                nc.tensor.matmul(bank[ROT_BANK[n]][0:r, :], rot_sb[0:r, 0:r], tile_words[n][0][0:r, :],
                                 start=True, stop=True).then_inc(rotated, 1)

            def mod_rows(half):
                for c in range(DC):
                    last = nc.tensor.matmul(bank[ROWS_BANK[half]][0:B, :], silu[:, c, :],
                                            wmod_sb[:, c, (2 + 2 * half) * D:(4 + 2 * half) * D],
                                            start=(c == 0), stop=(c == DC - 1))
                last.then_inc(rows_done, 1)

            keep_clock(1)
            transpose_x(0)
            keep_clock(2)
            pe.wait_ge(wkqv_in, 16)
            pe.wait_ge(rope_in, 48)
            pe.wait_ge(hT_by_dve, 1)
            pe.wait_ge(hT_by_act, 1)
            project(0)
            pe.wait_ge(mod_saved, 2)
            rotate(0)
            project(1)
            project_v(0)
            rotate(1)
            project(2)
            pe.wait_ge(wmod_rest_in, 16)
            mod_rows(0)
            pe.wait_ge(rot_read, 1)
            mod_rows(1)
            rotate(2)
            transpose_x(1)

            def second_batch(piece):
                if piece == 0:
                    pe.wait_ge(hT_by_act, 3)
                    pe.wait_ge(vx_done, TB)
                    project(3)
                elif piece == 1:
                    project(4)
                elif piece == 2:
                    pe.wait_ge(rows_copied, 3)
                    rotate(3)
                elif piece == 3:
                    project(5)
                elif piece == 4:
                    pe.wait_ge(biased, 5)
                    rotate(4)
                elif piece == 5:
                    pe.wait_ge(biased, 6)
                    project_v(1)
                elif piece == 6:
                    rotate(5)

            def max_scores(slot, j, i, free):
                if free is not None:
                    pe.wait_ge(max_done, free)
                nc.tensor.matmul(max_bank[i][:], qx[0:SHIFT_ROW, slot, i, j * P:(j + 1) * P],
                                 kx[0:SHIFT_ROW, slot, :], start=True, stop=True).then_inc(a_done, 1)

            def exp_scores(slot, j, i, free):
                if free is not None:
                    pe.wait_ge(exp_done, free)
                nc.tensor.matmul(exp_bank[i % 2][:], kx[0:BROWS, slot, j * P:(j + 1) * P],
                                 qx[0:BROWS, slot, i, :], start=True, stop=True).then_inc(b_done, 1)

            def values(steps, slot, j):
                pe.wait_ge(exp_done, 4 * steps)
                for i in range(G):
                    last = nc.tensor.matmul(o_bank[32 * i:32 * i + HD + 1, :], vs[:, slot, j, :],
                                            probs[:, j % 2, i, :], start=(j == 0), stop=(j == TB - 1))
                last.then_inc(pv_done, 1)

            def transpose_max():
                nc.tensor.transpose(tr_bank[0:2 * G * TB, 0:P // 2].bitcast(BF16),
                                    negparts[:].rearrange("p a n -> p (a n)"), ident_h[:]).then_inc(negT_done, 1)

            def transpose_o():
                for q in range(TB):
                    last = nc.tensor.transpose(tr_bank[:, q * P:(q + 1) * P], osb[:, q * P:(q + 1) * P], ident[:])
                last.then_inc(oT_done, 1)

            def transpose_attn(k, to):
                for q in range(TB):
                    last = nc.tensor.transpose(bank[to][:, q * P:(q + 1) * P], attn[:, k, q, :], ident[:])
                last.then_inc(aT_done, 1)

            def wo_product(k, to):
                b = 2 * k // TB
                for t in range(2 * k, 2 * k + 2):
                    q = t % TB
                    for c in range(DC):
                        last = nc.tensor.matmul(bank[to][:, (t % 2) * D:(t % 2 + 1) * D],
                                                attnT[DC * b + c][:, q * P:(q + 1) * P], wo_ga[:, b, c, :],
                                                start=(c == 0), stop=(c == DC - 1))
                last.then_inc(wo_done, 1)

            def wo_half(k, banks, c):
                b = 2 * k // TB
                for t in range(2):
                    q = (2 * k + t) % TB
                    last = nc.tensor.matmul(bank[banks[t]][:, 0:D], attnT[DC * b + c][:, q * P:(q + 1) * P],
                                            wo_ga[:, b, c, :], start=(c == 0), stop=(c == DC - 1))
                return last

            def transpose_h2(b):
                for t in range(TB):
                    pe.wait_ge(h2_norm, TB * b + t + 1)
                    for c in range(DC):
                        last = nc.tensor.transpose(bank[c][:, t * P:(t + 1) * P],
                                                   h2[:, TB * b + t, c * P:(c + 1) * P], ident[:])
                        if t == TB - 1:
                            last.then_inc(h2T_done, 1)

            def logits(b):
                for t in range(TB):
                    for c in range(DC):
                        last = nc.tensor.matmul(bank[2][:, t * E:(t + 1) * E], h2T[:, b, c, t * P:(t + 1) * P],
                                                wg_sb[:, c, :], start=(c == 0), stop=(c == DC - 1))
                last.then_inc(logits_done, 1)

            def count(b):
                pe.wait_ge(onehot_done, b + 1)
                nc.tensor.matmul(bank[3][:, 0:TB * E], before[:],
                                 onehot[:, b * TB:(b + 1) * TB, :].rearrange("p t e -> p (t e)"),
                                 start=True, stop=False)
                for t in range(b * TB + TB - 1):
                    first = max(t + 1 - b * TB, 0)
                    last = nc.tensor.matmul(
                        bank[3][:, first * E:TB * E].rearrange("p (t e) -> p t e", e=E), ones_h[:],
                        onehot[:, t:t + 1, :].to_broadcast([P, TB - first, E]), start=False,
                        stop=(t == b * TB + TB - 2))
                last.then_inc(count_done, 1)

            def first_batch(piece):
                if piece == 0:
                    pe.wait_ge(max_done, 4 * TB * NG)
                    pe.wait_ge(norm_done, NG // B)
                    pe.wait_ge(cols_in, 16)
                    nc.tensor.transpose(bank[2][:, 0:2 * B * DC], cols_rows,
                                        ident[0:2 * B * DC, 0:2 * B * DC]).then_inc(cols_done, 1)
                    for c in range(DC):
                        transpose_attn(c, c)
                elif piece == 1:
                    pe.wait_ge(wo_scaled, B)
                    pe.wait_ge(aT_by_dve, DC)
                    wo_product(0, 3)
                elif piece == 2:
                    pe.wait_ge(cols_saved, 1)
                    wo_product(1, 2)
                    pe.wait_ge(norm_done, NG // B + TB)
                    transpose_attn(2, 1)
                elif piece == 4:
                    pe.wait_ge(aT_by_dve, DC + 1)
                    transpose_h2(0)
                elif piece == 5:
                    pe.wait_ge(x1_done, 2)
                    pe.wait_ge(h2T_by_dve, DC)
                    logits(0)
                    keep_clock(1, to=0)

            def period(it, v, second=True, third=True, piece=None):
                g = 4 * it + 1 + v
                first = isinstance(it, int) and it == -1
                slot = (v + 1) % SLOTS
                if v == 3:
                    pe.wait_ge(rows_in_dram, it + 2)
                for j in range(TB):
                    ahead, jj = 1 + j // 2, (j + 2) % TB
                    mslot = (slot + ahead) % SLOTS
                    take = (second, third)[j // 2]
                    if j == 2 and take:
                        pe.wait_ge(qk_in[mslot], 32 * (it + (3 + v) // 4 + 1))

                    def for_max(i):
                        if take:
                            max_scores(mslot, jj, i, 16 * (g + ahead) + 4 * jj + i - 3)

                    def for_exp(i):
                        exp_scores(slot, j, i, None if first and j == 0 and i < 2 else 16 * g + 4 * j + i - 1)

                    for_max(0)
                    for_max(1)
                    if j == 0:
                        pe.wait_ge(shift_in[slot], 16 * (it + (1 + v) // 4 + 1))
                    for_exp(0)
                    for_max(2)
                    for_exp(1)
                    if j == 1:
                        pe.wait_ge(vs_done, g + 1)
                        if first:
                            pe.wait_ge(o_clear, 1)
                        else:
                            pe.wait_ge(o_saved, g)
                            if isinstance(it, int) and not second:
                                pe.wait_ge(norm_done, g - 1)
                            else:
                                pe.wait_ge(shift_saved, g + 1)
                            transpose_o()
                    if j == 2 and second:
                        pe.wait_ge(neg_done, g + 2)
                        if not first:
                            pe.wait_ge(norm_done, g)
                        transpose_max()
                    if j > 0:
                        values(4 * g + j, slot, j - 1)
                    elif not first:
                        values(4 * g, v % SLOTS, TB - 1)
                    for_exp(2)
                    for_max(3)
                    for_exp(3)
                    if piece is not None and piece + j >= 0:
                        first_batch(piece + j)

            pe.wait_ge(consts, 3)
            pe.wait_ge(masks_done, 2)
            pe.wait_ge(qk_in[0], 32)
            pe.wait_ge(biased, 3)
            pe.wait_ge(rot_read, 2)
            pe.wait_ge(rot_copied, 1)
            pe.wait_ge(rows_copied, 1)
            for n in range(4 * TB):
                max_scores(0, n // G, n % G, n - 3 if n > 3 else None)
                if n % 4 == 3:
                    second_batch(n // 4)
            pe.wait_ge(rot_copied, 2)
            pe.wait_ge(qk_in[1], 32)
            for n in range(4 * TB, 6 * TB):
                max_scores(1, n // G - TB, n % G, n - 3)
                if n == 4 * TB + 1:
                    pe.wait_ge(neg_done, 1)
                    transpose_max()
                if n % 2:
                    second_batch(n // 2 - 4)
            pe.wait_ge(shift_saved, 1)
            pe.wait_ge(rot_copied, 4)
            pe.wait_ge(vx_done, 2 * TB)
            period(-1, 3)
            with pe.Fori(0, TURNS) as it:
                for v in range(SLOTS):
                    period(it, v)
            period(TURNS, 0)
            period(TURNS, 1, third=False, piece=-2)
            period(TURNS, 2, second=False, third=False, piece=2)
            values(4 * NG, 3, TB - 1)

            pe.wait_ge(exp_done, 4 * TB * NG)
            wo_half(2, X1_BANKS[0], 0)
            pe.wait_ge(o_saved, NG)
            pe.wait_ge(norm_done, NG - 1)
            transpose_o()
            wo_half(3, X1_BANKS[1], 0)
            pe.wait_ge(norm_done, NG)
            transpose_attn(3, 0)
            pe.wait_ge(aT_by_act, 1)
            for k in range(2):
                wo_half(2 + k, X1_BANKS[k], 1).then_inc(wo_done, 1)
            count(0)
            keep_clock(1, to=0)
            pe.wait_ge(var2_done, 2)
            keep_clock(1, to=0)
            transpose_h2(1)
            keep_clock(1, to=6)
            pe.wait_ge(h2T_by_act, 1)
            pe.wait_ge(h2T_by_dve, DC + 1)
            pe.wait_ge(gate_sub, 1)
            logits(1)
            keep_clock(2, to=6)
            pe.wait_ge(gate_sub, 2)
            pe.wait_ge(slots_done, 1)

            def pick_first(b):
                pe.wait_ge(h2_done, b + 1)
                for c in range(DC):
                    for t in range(b * TB, (b + 1) * TB):
                        last = nc.tensor.matmul(bank[4 + c][:, 0:CAP], h2[:, t, c * P:(c + 1) * P],
                                                picks[:, t, :], start=(t == 0), stop=(t == NT - 1))
                return last

            count(1)
            pe.wait_ge(x1_done, NT // 2)
            pe.wait_ge(picks_by_pool, TB)
            pick_first(0)
            pe.wait_ge(picks_by_dve, 1)
            pick_first(1).then_inc(first_done, 1)

            def transpose_routed(e):
                pe.wait_ge(routed_in[e], 16)
                if e >= 3:
                    pe.wait_ge(rT_saved, e - 2)
                for c in range(DC):
                    last = nc.tensor.transpose(bank[6 + e % 2][:, c * P:(c + 1) * P],
                                               routed[:, e, c * P:(c + 1) * P], ident[:])
                last.then_inc(rT_done, 1)

            for k in range(2):
                pe.wait_ge(w_in[k], 16 * (E - 1))

            def hidden(e):
                if e == 0:
                    pe.wait_ge(first_by_dve, 1)
                    pe.wait_ge(first_by_act, 1)
                else:
                    pe.wait_ge(rT_saved, e)
                if e >= 2:
                    pe.wait_ge(gelu_done, 2 * e - 2)
                if e == E - 1:
                    pe.wait_ge(w7_in, 32)
                for k in range(2):
                    for f in range(FT // 2):
                        f0 = (k * FT // 2 + f) * P
                        for c in range(DC):
                            last = nc.tensor.matmul(bank[2 * (e % 2) + k][:, f * P:(f + 1) * P],
                                                    w1_sb[e][:, c, f0:f0 + P],
                                                    routedT[:, c, e * CAP:(e + 1) * CAP],
                                                    start=(c == 0), stop=(c == DC - 1))
                    last.then_inc(h_done, 1)

            def expert_out(e):
                if e >= 2:
                    pe.wait_ge(y_saved, e - 1)
                for f in range(FT):
                    if f % (FT // 2) == 0:
                        pe.wait_ge(gelu_done, 2 * e + 1 + 2 * f // FT)
                    if e == 0 and f == FT - 2:
                        transpose_routed(1)
                    last = nc.tensor.matmul(bank[4 + e % 2][:, 0:D], gelu[:, e % 2, f, :], w2_sb[e][:, f, :],
                                            start=(f == 0), stop=(f == FT - 1))
                last.then_inc(y_done, 1)

            hidden(0)
            expert_out(0)
            transpose_routed(2)
            hidden(1)
            for e in range(1, E):
                if e + 1 < E:
                    hidden(e + 1)
                if e + 2 < E:
                    transpose_routed(e + 2)
                expert_out(e)


def kernel(L0_attn_x, L0_attn_Wq, L0_attn_bq, L0_attn_Wk, L0_attn_bk, L0_attn_Wv, L0_attn_bv, L0_attn_Wo,
           L0_attn_bo, L0_ffn_w_gate, L0_ffn_w1, L0_ffn_w2, L0_c, L0_wmod):
    import numpy as np
    import concourse.bacc as bacc
    from concourse.bass_utils import run_bass_kernel_spmd

    a = {k: np.asarray(v) for k, v in dict(
        x=L0_attn_x, wq=L0_attn_Wq, bq=L0_attn_bq, wk=L0_attn_Wk, bk=L0_attn_bk, wv=L0_attn_Wv,
        bv=L0_attn_bv, wo=L0_attn_Wo, bo=L0_attn_bo, w_gate=L0_ffn_w_gate, w1=L0_ffn_w1, w2=L0_ffn_w2,
        c=L0_c, wmod=L0_wmod).items()}
    B, T, D = a["x"].shape
    HD = 8
    inv = (1.0 / np.float32(10000.0) ** (np.arange(0, HD, 2, dtype=np.float32) / np.float32(HD))).astype(np.float32)
    angle = np.tile((inv[:, None] * np.arange(T, dtype=np.float32)[None, :]).astype(np.float32), (2 * P // HD, 1))
    turn = np.zeros((P, P), np.float32)
    for row in range(P):
        if row % HD < HD // 2:
            turn[row + HD // 2, row] = -1.0
        else:
            turn[row - HD // 2, row] = 1.0
    arrays = {
        "x": a["x"].reshape(B * T, D),
        "c_t": np.ascontiguousarray(a["c"].T),
        "wmod": a["wmod"],
        "wkqv_t": np.ascontiguousarray(np.concatenate([a["wk"], a["wq"], a["wv"]], 0).T),
        "bkq": np.concatenate([a["bk"], a["bq"]], 0), "bv": a["bv"],
        "wo_t": np.ascontiguousarray(a["wo"].T),
        "bo": a["bo"], "w_gate": a["w_gate"], "w1": a["w1"], "w2": a["w2"],
        "rope_cos": np.cos(angle), "rope_sin": np.sin(angle), "rope_rot": turn,
    }
    nc = bacc.Bacc("TRN2", target_bir_lowering=False, num_devices=1)
    args = {n: nc.dram_tensor(n + "_in", v.shape, mybir.dt.from_np(v.dtype), kind="ExternalInput").ap()
            for n, v in arrays.items()}
    out = nc.dram_tensor("out_0", (B * T, D), F32, kind="ExternalOutput").ap()
    adaln_attention_moe_kernel(nc, out=out, **args)
    r = run_bass_kernel_spmd(nc, [{n + "_in": v for n, v in arrays.items()}], core_ids=[0])
    return r.results[0]["out_0"].reshape(B, T, D)
```
